# Optimizing a Trainium2 kernel written in Bass

```python
import numpy as np
import jax
import jax.numpy as jnp

def _softmax(x, axis=-1):
    return jax.nn.softmax(x, axis=axis)

def _gelu(x):
    return jax.nn.gelu(x, approximate=True)

def _silu(x):
    return jax.nn.silu(x)

def _sigmoid(x):
    return jax.nn.sigmoid(x)

def _layernorm(x, axis=-1, eps=1e-05):
    m = jnp.mean(x, axis=axis, keepdims=True)
    v = jnp.var(x, axis=axis, keepdims=True)
    return (x - m) / jnp.sqrt(v + eps)

def _scatter_add(tgt, idx, src, axis=0):
    return tgt.at[idx].add(src)

def _segment_sum(src, seg, n):
    return jax.ops.segment_sum(src, seg, n)
kernel_name = 'mk_seq_postln_d2_jaxref_r8_f57a28'

def setup_inputs(seed: int=0):
    np.random.seed(seed)
    _w = jnp.asarray

    def _L0_attn_setup():
        import jax, jax.numpy as jnp
        import numpy as np
        from jax import lax
        D_MODEL = 256
        D_INNER = 512
        D_CONV = 4
        B, T = (4, 256)

        def _rmsnorm(h):
            n = jnp.sqrt(jnp.sum(h * h, axis=-1, keepdims=True))
            return h / jnp.maximum(n, 1e-12) * h.shape[-1] ** 0.5

        def _mamba_fallback(h, W_in, conv_w, conv_b, W_out):
            xz = jnp.einsum('btd,ed->bte', h, W_in)
            xp, z = jnp.split(xz, 2, axis=-1)
            xc = lax.conv_general_dilated(xp.transpose(0, 2, 1), conv_w, window_strides=(1,), padding=[(D_CONV - 1, 0)], dimension_numbers=('NCH', 'OIH', 'NCH'), feature_group_count=D_INNER) + conv_b[None, :, None]
            xc = xc.transpose(0, 2, 1)
            y = jax.nn.silu(xc) * jax.nn.silu(z)
            return jnp.einsum('bte,de->btd', y, W_out)
        key = jax.random.key(seed)
        ks = jax.random.split(key, 7)
        std = 0.02
        return {'x': jax.random.normal(ks[0], (B, T, D_MODEL), jnp.float32), 'W_in': jax.random.normal(ks[1], (2 * D_INNER, D_MODEL), jnp.float32) * std, 'conv_w': jax.random.normal(ks[2], (D_INNER, 1, D_CONV), jnp.float32) * std, 'conv_b': jnp.zeros((D_INNER,), jnp.float32), 'W_out': jax.random.normal(ks[3], (D_MODEL, D_INNER), jnp.float32) * std, 'W_mlp1': jax.random.normal(ks[4], (4 * D_MODEL, D_MODEL), jnp.float32) * std, 'W_mlp2': jax.random.normal(ks[5], (D_MODEL, 4 * D_MODEL), jnp.float32) * std}
    _L0_attn_in = _L0_attn_setup()

    def _L0_ffn_setup():
        import jax, jax.numpy as jnp
        import numpy as np
        B, S, H = (1, 128, 256)
        I = 176
        E = 32
        K = 6
        G = 8
        TG = 3
        NSH = 2
        SCALE = 16.0
        C = 48

        def _moe_forward(x3, gate_w, w_gate_up, w_down, ws_gate_up, ws_down):
            b, s, h = x3.shape
            x = x3.reshape(-1, h)
            T = x.shape[0]
            logits = x @ gate_w.T
            grouped = logits.reshape(T, G, E // G)
            group_scores = jnp.max(grouped, axis=-1)
            _, group_idx = jax.lax.top_k(group_scores, TG)
            group_keep = jnp.zeros((T, G), bool).at[jnp.arange(T)[:, None], group_idx].set(True)
            masked = jnp.where(group_keep[..., None], grouped, 0.0)
            scores = masked.reshape(T, E)
            probs = jax.nn.softmax(scores.astype(jnp.float32), axis=-1)
            topk_w, topk_idx = jax.lax.top_k(probs, K)
            topk_w = topk_w * SCALE
            flat_e = topk_idx.reshape(-1)
            tok_idx = jnp.repeat(jnp.arange(T), K)
            oh = jax.nn.one_hot(flat_e, E, dtype=jnp.int32)
            pos = jnp.take_along_axis(jnp.cumsum(oh, axis=0) - 1, flat_e[:, None], axis=1)[:, 0]
            valid = pos < C
            slot = jnp.where(valid, flat_e * C + pos, E * C)
            buf = jnp.zeros((E * C + 1, h), x.dtype).at[slot].set(x[tok_idx])
            xb = buf[:E * C].reshape(E, C, h)
            gu = jnp.einsum('ech,ehf->ecf', xb, w_gate_up)
            g, u = jnp.split(gu, 2, axis=-1)
            act = jax.nn.silu(g) * u
            yb = jnp.einsum('eci,eih->ech', act, w_down)
            yflat = jnp.concatenate([yb.reshape(E * C, h), jnp.zeros((1, h), yb.dtype)], axis=0)
            y_pairs = yflat[slot].reshape(T, K, h)
            out = jnp.einsum('tk,tkh->th', topk_w.astype(x.dtype), y_pairs)
            gu_s = x @ ws_gate_up
            gs, us = jnp.split(gu_s, 2, axis=-1)
            out = out + jax.nn.silu(gs) * us @ ws_down
            return out.reshape(b, s, h)
        key = jax.random.key(seed)
        ks = jax.random.split(key, 6)
        s = 0.02
        return {'hidden_states': jax.random.normal(ks[0], (B, S, H), jnp.float32), 'gate_w': jax.random.normal(ks[1], (E, H), jnp.float32) * s, 'w_gate_up': jax.random.normal(ks[2], (E, H, 2 * I), jnp.float32) * s, 'w_down': jax.random.normal(ks[3], (E, I, H), jnp.float32) * s, 'ws_gate_up': jax.random.normal(ks[4], (H, 2 * I * NSH), jnp.float32) * s, 'ws_down': jax.random.normal(ks[5], (I * NSH, H), jnp.float32) * s}
    _L0_ffn_in = _L0_ffn_setup()

    def _L1_attn_setup():
        import jax, jax.numpy as jnp
        import numpy as np
        B, T, C = (1, 512, 256)
        H = 16
        D = C // H
        BLOCK = 64
        WINDOW = 128
        DILATION = 32
        GLOBAL_TOKENS = 128
        ROPE_BASE = 10000.0
        SCALE = 1.0 / np.sqrt(D)

        def _rope(x):
            t = jnp.arange(x.shape[2], dtype=jnp.float32)
            inv_freq = 1.0 / ROPE_BASE ** (jnp.arange(0, D, 2, dtype=jnp.float32) / D)
            freqs = jnp.outer(t, inv_freq)
            emb = jnp.concatenate([freqs, freqs], axis=-1)
            cos = jnp.cos(emb)[None, None].astype(x.dtype)
            sin = jnp.sin(emb)[None, None].astype(x.dtype)
            x1, x2 = jnp.split(x, 2, axis=-1)
            rot = jnp.concatenate([-x2, x1], axis=-1)
            return x * cos + rot * sin

        def _token_mask(seq_len):
            nb = (seq_len + BLOCK - 1) // BLOCK
            bp = jnp.arange(nb)
            qb, kb = (bp[:, None], bp[None, :])
            dist = qb - kb
            window_blocks = WINDOW // BLOCK
            window_mask = (dist >= 0) & (dist <= window_blocks)
            global_blocks = max(1, GLOBAL_TOKENS // BLOCK)
            global_mask = kb < global_blocks
            dilation_blocks = max(1, DILATION // BLOCK)
            dilated_mask = kb % dilation_blocks == 0
            causal_mask = kb <= qb
            block_mask = (window_mask | global_mask | dilated_mask) & causal_mask
            tok = jnp.repeat(jnp.repeat(block_mask, BLOCK, axis=0), BLOCK, axis=1)
            return tok[:seq_len, :seq_len]
        key = jax.random.key(seed)
        ks = jax.random.split(key, 5)
        x = jax.random.normal(ks[0], (B, T, C), dtype=jnp.float32)
        w_q = jax.random.normal(ks[1], (C, C), dtype=jnp.float32) * 0.02
        w_k = jax.random.normal(ks[2], (C, C), dtype=jnp.float32) * 0.02
        w_v = jax.random.normal(ks[3], (C, C), dtype=jnp.float32) * 0.02
        w_o = jax.random.normal(ks[4], (C, C), dtype=jnp.float32) * 0.02
        return {'x': x, 'w_q': w_q, 'w_k': w_k, 'w_v': w_v, 'w_o': w_o}
    _L1_attn_in = _L1_attn_setup()

    def _L1_ffn_setup():
        import jax, jax.numpy as jnp
        import numpy as np

        def _sparsify_2to4(h):
            B, S, I = h.shape
            g = h.reshape(B, S, I // 4, 4)
            a = jnp.abs(g)
            _, idx = jax.lax.top_k(a, 2)
            pos = jnp.arange(4)
            mask = (pos == idx[..., 0:1]) | (pos == idx[..., 1:2])
            return (g * mask.astype(g.dtype)).reshape(B, S, I)
        key = jax.random.key(seed)
        k1, k2, k3, k4 = jax.random.split(key, 4)
        B, S, H, I = (4, 256, 256, 1024)
        x = jax.random.normal(k1, (B, S, H), dtype=jnp.float32)
        w_gate = jax.random.normal(k2, (H, I), dtype=jnp.float32) / np.sqrt(H)
        w_up = jax.random.normal(k3, (H, I), dtype=jnp.float32) / np.sqrt(H)
        w_down = jax.random.normal(k4, (I, H), dtype=jnp.float32) / np.sqrt(I)
        return {'x': x, 'w_gate': w_gate, 'w_up': w_up, 'w_down': w_down}
    _L1_ffn_in = _L1_ffn_setup()
    _d = {'L0_attn_x': _L0_attn_in['x'], 'L0_attn_W_in': _L0_attn_in['W_in'], 'L0_attn_conv_w': _L0_attn_in['conv_w'], 'L0_attn_conv_b': _L0_attn_in['conv_b'], 'L0_attn_W_out': _L0_attn_in['W_out'], 'L0_attn_W_mlp1': _L0_attn_in['W_mlp1'], 'L0_attn_W_mlp2': _L0_attn_in['W_mlp2'], 'L0_ffn_gate_w': _L0_ffn_in['gate_w'], 'L0_ffn_w_gate_up': _L0_ffn_in['w_gate_up'], 'L0_ffn_w_down': _L0_ffn_in['w_down'], 'L0_ffn_ws_gate_up': _L0_ffn_in['ws_gate_up'], 'L0_ffn_ws_down': _L0_ffn_in['ws_down'], 'L1_attn_w_q': _L1_attn_in['w_q'], 'L1_attn_w_k': _L1_attn_in['w_k'], 'L1_attn_w_v': _L1_attn_in['w_v'], 'L1_attn_w_o': _L1_attn_in['w_o'], 'L1_ffn_w_gate': _L1_ffn_in['w_gate'], 'L1_ffn_w_up': _L1_ffn_in['w_up'], 'L1_ffn_w_down': _L1_ffn_in['w_down']}
    _x0 = _d['L0_attn_x']
    _d['L0_attn_x'] = jax.random.normal(jax.random.fold_in(jax.random.key(seed), 1), (4, 1024, 256), dtype=_x0.dtype)
    del _x0
    return _d

def reference(L0_attn_x, L0_attn_W_in, L0_attn_conv_w, L0_attn_conv_b, L0_attn_W_out, L0_attn_W_mlp1, L0_attn_W_mlp2, L0_ffn_gate_w, L0_ffn_w_gate_up, L0_ffn_w_down, L0_ffn_ws_gate_up, L0_ffn_ws_down, L1_attn_w_q, L1_attn_w_k, L1_attn_w_v, L1_attn_w_o, L1_ffn_w_gate, L1_ffn_w_up, L1_ffn_w_down):

    def _L0_attn_ref(x, W_in, conv_w, conv_b, W_out, W_mlp1, W_mlp2):
        import jax, jax.numpy as jnp
        import numpy as np
        from jax import lax
        D_MODEL = 256
        D_INNER = 512
        D_CONV = 4
        B, T = (4, 256)

        def _rmsnorm(h):
            n = jnp.sqrt(jnp.sum(h * h, axis=-1, keepdims=True))
            return h / jnp.maximum(n, 1e-12) * h.shape[-1] ** 0.5

        def _mamba_fallback(h, W_in, conv_w, conv_b, W_out):
            xz = jnp.einsum('btd,ed->bte', h, W_in)
            xp, z = jnp.split(xz, 2, axis=-1)
            xc = lax.conv_general_dilated(xp.transpose(0, 2, 1), conv_w, window_strides=(1,), padding=[(D_CONV - 1, 0)], dimension_numbers=('NCH', 'OIH', 'NCH'), feature_group_count=D_INNER) + conv_b[None, :, None]
            xc = xc.transpose(0, 2, 1)
            y = jax.nn.silu(xc) * jax.nn.silu(z)
            return jnp.einsum('bte,de->btd', y, W_out)
        h = _rmsnorm(x)
        x = x + _mamba_fallback(h, W_in, conv_w, conv_b, W_out)
        h = _rmsnorm(x)
        m = jnp.einsum('bte,de->btd', jax.nn.relu(jnp.einsum('btd,ed->bte', h, W_mlp1)), W_mlp2)
        return x + m

    def _L0_ffn_ref(hidden_states, gate_w, w_gate_up, w_down, ws_gate_up, ws_down):
        import jax, jax.numpy as jnp
        import numpy as np
        B, S, H = (1, 128, 256)
        I = 176
        E = 32
        K = 6
        G = 8
        TG = 3
        NSH = 2
        SCALE = 16.0
        C = 48

        def _moe_forward(x3, gate_w, w_gate_up, w_down, ws_gate_up, ws_down):
            b, s, h = x3.shape
            x = x3.reshape(-1, h)
            T = x.shape[0]
            logits = x @ gate_w.T
            grouped = logits.reshape(T, G, E // G)
            group_scores = jnp.max(grouped, axis=-1)
            _, group_idx = jax.lax.top_k(group_scores, TG)
            group_keep = jnp.zeros((T, G), bool).at[jnp.arange(T)[:, None], group_idx].set(True)
            masked = jnp.where(group_keep[..., None], grouped, 0.0)
            scores = masked.reshape(T, E)
            probs = jax.nn.softmax(scores.astype(jnp.float32), axis=-1)
            topk_w, topk_idx = jax.lax.top_k(probs, K)
            topk_w = topk_w * SCALE
            flat_e = topk_idx.reshape(-1)
            tok_idx = jnp.repeat(jnp.arange(T), K)
            oh = jax.nn.one_hot(flat_e, E, dtype=jnp.int32)
            pos = jnp.take_along_axis(jnp.cumsum(oh, axis=0) - 1, flat_e[:, None], axis=1)[:, 0]
            valid = pos < C
            slot = jnp.where(valid, flat_e * C + pos, E * C)
            buf = jnp.zeros((E * C + 1, h), x.dtype).at[slot].set(x[tok_idx])
            xb = buf[:E * C].reshape(E, C, h)
            gu = jnp.einsum('ech,ehf->ecf', xb, w_gate_up)
            g, u = jnp.split(gu, 2, axis=-1)
            act = jax.nn.silu(g) * u
            yb = jnp.einsum('eci,eih->ech', act, w_down)
            yflat = jnp.concatenate([yb.reshape(E * C, h), jnp.zeros((1, h), yb.dtype)], axis=0)
            y_pairs = yflat[slot].reshape(T, K, h)
            out = jnp.einsum('tk,tkh->th', topk_w.astype(x.dtype), y_pairs)
            gu_s = x @ ws_gate_up
            gs, us = jnp.split(gu_s, 2, axis=-1)
            out = out + jax.nn.silu(gs) * us @ ws_down
            return out.reshape(b, s, h)
        return _moe_forward(hidden_states, gate_w, w_gate_up, w_down, ws_gate_up, ws_down)

    def _L1_attn_ref(x, w_q, w_k, w_v, w_o):
        import jax, jax.numpy as jnp
        import numpy as np
        B, T, C = (1, 512, 256)
        H = 16
        D = C // H
        BLOCK = 64
        WINDOW = 128
        DILATION = 32
        GLOBAL_TOKENS = 128
        ROPE_BASE = 10000.0
        SCALE = 1.0 / np.sqrt(D)

        def _rope(x):
            t = jnp.arange(x.shape[2], dtype=jnp.float32)
            inv_freq = 1.0 / ROPE_BASE ** (jnp.arange(0, D, 2, dtype=jnp.float32) / D)
            freqs = jnp.outer(t, inv_freq)
            emb = jnp.concatenate([freqs, freqs], axis=-1)
            cos = jnp.cos(emb)[None, None].astype(x.dtype)
            sin = jnp.sin(emb)[None, None].astype(x.dtype)
            x1, x2 = jnp.split(x, 2, axis=-1)
            rot = jnp.concatenate([-x2, x1], axis=-1)
            return x * cos + rot * sin

        def _token_mask(seq_len):
            nb = (seq_len + BLOCK - 1) // BLOCK
            bp = jnp.arange(nb)
            qb, kb = (bp[:, None], bp[None, :])
            dist = qb - kb
            window_blocks = WINDOW // BLOCK
            window_mask = (dist >= 0) & (dist <= window_blocks)
            global_blocks = max(1, GLOBAL_TOKENS // BLOCK)
            global_mask = kb < global_blocks
            dilation_blocks = max(1, DILATION // BLOCK)
            dilated_mask = kb % dilation_blocks == 0
            causal_mask = kb <= qb
            block_mask = (window_mask | global_mask | dilated_mask) & causal_mask
            tok = jnp.repeat(jnp.repeat(block_mask, BLOCK, axis=0), BLOCK, axis=1)
            return tok[:seq_len, :seq_len]
        Bc, Tc, Cc = x.shape
        q = (x @ w_q.T).reshape(Bc, Tc, H, D).transpose(0, 2, 1, 3)
        k = (x @ w_k.T).reshape(Bc, Tc, H, D).transpose(0, 2, 1, 3)
        v = (x @ w_v.T).reshape(Bc, Tc, H, D).transpose(0, 2, 1, 3)
        q = _rope(q)
        k = _rope(k)
        scores = jnp.einsum('bhqd,bhkd->bhqk', q, k) * SCALE
        tok_mask = _token_mask(Tc)
        scores = jnp.where(tok_mask[None, None], scores, -jnp.inf)
        attn = jax.nn.softmax(scores, axis=-1)
        ctx = jnp.einsum('bhqk,bhkd->bhqd', attn, v)
        ctx = ctx.transpose(0, 2, 1, 3).reshape(Bc, Tc, Cc)
        return ctx @ w_o.T

    def _L1_ffn_ref(x, w_gate, w_up, w_down):
        import jax, jax.numpy as jnp
        import numpy as np

        def _sparsify_2to4(h):
            B, S, I = h.shape
            g = h.reshape(B, S, I // 4, 4)
            a = jnp.abs(g)
            _, idx = jax.lax.top_k(a, 2)
            pos = jnp.arange(4)
            mask = (pos == idx[..., 0:1]) | (pos == idx[..., 1:2])
            return (g * mask.astype(g.dtype)).reshape(B, S, I)
        h = jax.nn.silu(jnp.einsum('bsh,hi->bsi', x, w_gate)) * jnp.einsum('bsh,hi->bsi', x, w_up)
        h_sparse = _sparsify_2to4(h)
        return jnp.einsum('bsi,ih->bsh', h_sparse, w_down)
    x = L0_attn_x
    x = _layernorm(x + _L0_attn_ref(x, L0_attn_W_in, L0_attn_conv_w, L0_attn_conv_b, L0_attn_W_out, L0_attn_W_mlp1, L0_attn_W_mlp2), axis=-1)
    x = _layernorm(x + _L0_ffn_ref(x, L0_ffn_gate_w, L0_ffn_w_gate_up, L0_ffn_w_down, L0_ffn_ws_gate_up, L0_ffn_ws_down), axis=-1)
    x = _layernorm(x + _L1_attn_ref(x, L1_attn_w_q, L1_attn_w_k, L1_attn_w_v, L1_attn_w_o), axis=-1)
    x = _layernorm(x + _L1_ffn_ref(x, L1_ffn_w_gate, L1_ffn_w_up, L1_ffn_w_down), axis=-1)
    return x

_drawn_inputs = setup_inputs


def setup_inputs(seed=0):
    import zlib

    import numpy as np

    out = dict(_drawn_inputs(seed))
    spreads = {'L0_attn_conv_b': (0.0, 0.8)}
    factors = {'L0_attn_W_in': 8.0,
     'L0_attn_conv_w': 8.0,
     'L0_attn_W_out': 8.0,
     'L0_ffn_gate_w': 3.628,
     'L0_ffn_w_gate_up': 2.795,
     'L0_ffn_w_down': 2.79,
     'L1_attn_w_q': 8.0,
     'L1_attn_w_k': 8.0,
     'L1_attn_w_v': 3.915,
     'L1_attn_w_o': 3.942}
    for name, (base, spread) in spreads.items():
        noise = np.random.default_rng([zlib.crc32(name.encode()), seed]).standard_normal(out[name].shape)
        drawn = base * np.exp(spread * noise) if base else spread * noise
        out[name] = jnp.asarray(drawn.astype(out[name].dtype))
    for name, factor in factors.items():
        out[name] = (out[name] * factor).astype(out[name].dtype)
    return out
```

```python
from contextlib import ExitStack

import numpy as np

import concourse.bass as bass
from concourse import mybir

F32 = mybir.dt.float32
BF16 = mybir.dt.bfloat16
I32 = mybir.dt.int32
U32 = mybir.dt.uint32
ALU = mybir.AluOpType
ACT = mybir.ActivationFunctionType
AX = mybir.AxisListType

P = 128
D = 256
KD = D // P
NT = 32
TOK = NT * P
GT = 4
GTOK = GT * P
NG = NT // GT
DI = 512
NC_ = DI // P
TAPS = 4
N_CONST = 8
DF = 1024
NF = DF // P
E = 32
ROW = D + E


class Step:

    def __init__(self, reg, mul, off):
        self.reg, self.mul, self.off = reg, mul, off

    def __call__(self, per, plus=0):
        fixed = self.off * per + plus
        return fixed if self.reg is None else self.reg * (self.mul * per) + fixed

    def before(self, k):
        return Step(self.reg, self.mul, self.off - k)

    def among(self, low, high):
        return self.reg is not None or low <= self.off < high


def wait(eng, sem, value):
    if not isinstance(value, int) or value > 0:
        eng.wait_ge(sem, value)


def steps(eng, first, last):
    pairs = (NG - first) // 2
    for n in range(first):
        yield Step(None, 0, n), n % 2
    with eng.Fori(0, pairs) as m:
        for k in range(2):
            yield Step(m, 2, first + k), (first + k) % 2
    for n in range(first + 2 * pairs, last):
        yield Step(None, 0, n), n % 2


def tiles(n, count=GT):
    return bass.ds(n(GT), count)


class Kit:

    def __init__(self, nc, ctx):
        self.nc, self.ctx = nc, ctx

    def sb(self, name, shape, dt=F32):
        return self.ctx.enter_context(self.nc.sbuf_tensor(name + "_sb", list(shape), dt))

    def ps(self, name, shape, dt=F32):
        return self.ctx.enter_context(self.nc.psum_tensor(name + "_ps", list(shape), dt))

    def sems(self, names):
        return [self.ctx.enter_context(self.nc.semaphore(n)) for n in names.split()]


def conv_mlp_phase(nc, io, keep):
    with ExitStack() as ctx:
        kit = Kit(nc, ctx)
        sb, ps = kit.sb, kit.ps
        x_sb, xT, ident, logits = keep["x_sb"], keep["xT"], keep["ident"], keep["logits"]

        w_in = sb("w_in", [P, KD, 2 * DI])
        w_out = sb("w_out", [P, NC_, D])
        w_up = sb("w_up", [P, KD, DF])
        w_dn = sb("w_dn", [P, NF, D])
        w_gate = sb("w_gate", [P, KD, E])
        conv_w = sb("conv_w", [P, NC_, TAPS])
        conv_b = sb("conv_b", [P, NC_])
        power = sb("power", [P, GT])
        eps = sb("eps", [P, GT])
        h = sb("h", [P, GT, D])
        hT = sb("hT", [P, KD, GTOK])
        xp = [sb(f"xp{i}", [P, NC_, TAPS - 1 + GTOK]) for i in range(2)]
        xc = sb("xc", [P, NC_, GTOK])
        sz = sb("sz", [P, NC_, GTOK])
        yT = sb("yT", [P, NC_, GTOK])
        x1 = sb("x1", [P, GT, D])
        h1 = sb("h1", [P, GT, D])
        h1T = sb("h1T", [P, KD, GTOK])
        m1T = sb("m1T", [P, NF, GTOK])
        sq = sb("sq", [P, GT, D], BF16)
        ss1 = sb("ss1", [P, GT])
        ss2 = sb("ss2", [P, GT])
        g1 = sb("g1", [P, GT])
        g2 = sb("g2", [P, GT])
        rn1 = sb("rn1", [P, GT])
        rn2 = sb("rn2", [P, GT])
        bn = sb("bn", [P, GT, 6])
        mv = sb("mv", [P, GT, 2])
        x_in = [sb(f"x_in{i}", [P, GT, D]) for i in range(2)]
        xx = sb("xx", [P, GT, D])
        x2 = sb("x2", [P, GT, D])
        xa = sb("xa", [P, GT, D])
        xaT = sb("xaT", [P, KD, GTOK])
        ve = sb("ve", [P, GT])
        rs = sb("rs", [P, GT])

        tp = ps("tp", [P, KD, GTOK])
        mm = [ps(f"mm{i}", [P, GTOK]) for i in range(4)]
        ro = [ps(f"ro{i}", [P, 2, D]) for i in range(2)]

        (consts, xl0, xl1, ss1_ok, g1_ok, rn1_ok, h_ok, tr1, hT_ok, in_mm, xp_ok, sz_ok, tap, conv_ok,
         xc_ok, y_ok, out_mm, x1_ok, ss2_ok, g2_ok, rn2_ok, h1_ok, xx_ok, tr2, h1T_ok, up_mm, m1a_ok,
         m1v_ok, dn_mm, x2_ok, bn_ok, mv_ok, ve_ok, rs_ok, xa_ok, tr3, xaT_ok, xT_ok, xs_ok, lg_mm, lg_ok, row_st,
         setup, passed_pool, passed_dve) = kit.sems(
            "consts x_loaded_even x_loaded_odd ss1_ready g1_ready rn1_ready h_ready tr1_done hT_ready in_done "
            "xp_ready sz_ready tap_done conv_ready xc_ready y_ready out_done x1_ready ss2_ready g2_ready "
            "rn2_ready h1_ready xx_ready tr2_done h1T_ready up_done m1_even_ready m1_odd_ready down_done "
            "x2_ready bn_ready mv_ready ve_ready rs_ready xa_ready tr3_done xaT_ready xT_kept x_kept logit_done logit_ready "
            "row_stored setup_done "
            "passed_pool passed_dve")
        x_loaded = [xl0, xl1]
        ALL = NG + 2
        block = ctx.enter_context(nc.Block())

        @block.sync
        def _(sp):
            def load(n, par):
                sp.dma_start(x_in[par][:, :, :], io["x"][:, tiles(n), :]).then_inc(x_loaded[par], 16)

            load(Step(None, 0, 0), 0)
            sp.dma_start(keep["ident"][:], io["ident"]).then_inc(consts, 16)
            for src, dst in (("w_in", w_in), ("conv_w", conv_w), ("conv_b", conv_b), ("w_out", w_out),
                             ("w_up", w_up), ("w_dn", w_dn), ("gate_w", w_gate)):
                sp.dma_start(dst[:], io[src]).then_inc(consts, 16)
            for n, par in steps(sp, 2, ALL):
                if n.among(0, NG):
                    wait(sp, xx_ok, n(1))
                    load(n.before(-1), 1 - par)
                if n.among(1, NG + 1):
                    b = n.before(1)
                    wait(sp, xa_ok, b(1, 1))
                    sp.dma_start(io["rows_t"][:, tiles(b), 0:D], xa[:, :, :]).then_inc(row_st, 16)
            sp.wait_ge(row_st, 16 * NG)

        @block.gpsimd
        def _(pool):
            pool.memset(power[:], -0.5).then_inc(setup, 1)
            pool.memset(eps[:], 1e-5).then_inc(setup, 1)
            pool.memset(xp[0][:, :, 0:TAPS - 1], 0.0).then_inc(setup, 1)
            pool.wait_ge(setup, 3)

            def rms(n, ss_ok, ss, g, g_ok, rn, rn_ok, used):
                wait(pool, ss_ok, n(GT, GT))
                wait(pool, rn_ok, n(1))
                pool.sem_inc(passed_pool, 1)
                pool.tensor_scalar(g[:], ss[:], 1e-24, None, ALU.max).then_inc(g_ok, 1)
                wait(pool, g_ok, n(1, 1))
                wait(pool, used, n(1))
                pool.tensor_tensor(rn[:], g[:], power[:], ALU.pow).then_inc(rn_ok, 1)

            rms(Step(None, 0, 0), ss1_ok, ss1, g1, g1_ok, rn1, rn1_ok, h_ok)
            for n, par in steps(pool, 2, ALL):
                if n.among(0, NG):
                    rms(n.before(-1), ss1_ok, ss1, g1, g1_ok, rn1, rn1_ok, h_ok)
                if n.among(0, NG):
                    for c in range(NC_):
                        if c == 0:
                            wait(pool, out_mm, n(2))
                        wait(pool, sz_ok, n(NC_, c + 1))
                        wait(pool, xc_ok, n(NC_, c + 1))
                        pool.tensor_tensor(yT[:, c, :], xc[:, c, :], sz[:, c, :], ALU.mult).then_inc(y_ok, 1)
                if n.among(2, ALL):
                    c = n.before(2)
                    wait(pool, xaT_ok, c(1, 1))
                    pool.tensor_copy(xT[:, :, bass.ds(c(GTOK), GTOK)], xaT[:, :, :]).then_inc(xT_ok, 1)
                if n.among(0, NG):
                    rms(n, ss2_ok, ss2, g2, g2_ok, rn2, rn2_ok, h1_ok)
                if n.among(1, NG + 1):
                    b = n.before(1)
                    wait(pool, mv_ok, b(GT, GT))
                    wait(pool, rs_ok, b(1))
                    pool.tensor_tensor(ve[:], mv[:, :, 1], eps[:], ALU.add).then_inc(ve_ok, 1)
                    wait(pool, ve_ok, b(1, 1))
                    wait(pool, xa_ok, b(1))
                    pool.tensor_tensor(rs[:], ve[:], power[:], ALU.pow).then_inc(rs_ok, 1)
                if n.among(0, NG):
                    wait(pool, x1_ok, n(2, 2))
                    wait(pool, x2_ok, n(2))
                    pool.tensor_tensor(xx[:, :, :], x_in[par][:, :, :], x1[:, :, :], ALU.add).then_inc(xx_ok, 1)
                if n.among(1, NG + 1):
                    b = n.before(1)
                    wait(pool, xa_ok, b(1, 1))
                    pool.tensor_copy(x_sb[:, tiles(b), :], xa[:, :, :]).then_inc(xs_ok, 1)
            pool.wait_ge(xs_ok, NG)
            pool.wait_ge(xT_ok, NG)

        @block.scalar
        def _(act):
            def squares(src, ss, ss_ok):
                for t in range(GT):
                    act.activation(sq[:, t, :], src[:, t, :], ACT.Square, accum_out=ss[:, t:t + 1]).then_inc(ss_ok, 1)

            act.wait_ge(x_loaded[0], 16)
            squares(x_in[0], ss1, ss1_ok)
            for n, par in steps(act, 2, ALL):
                if n.among(0, NG):
                    loads = n.before(-1)
                    if n.reg is None:
                        act.wait_ge(x_loaded[1 - par], 16 * (loads.off // 2 + 1))
                    else:
                        act.wait_ge(x_loaded[1 - par], n.reg * 16 + 16 * (loads.off // 2 + 1))
                    wait(act, g1_ok, n(1, 1))
                    squares(x_in[1 - par], ss1, ss1_ok)
                if n.among(0, NG):
                    for c in range(NC_):
                        wait(act, in_mm, n(2 * NC_, c + 1))
                        wait(act, conv_ok, n(NC_, c - NC_ + 1))
                        last = act.activation(xp[par][:, c, TAPS - 1:], mm[c][:], ACT.Copy)
                        if par == 0:
                            last = act.activation(xp[1][:, c, 0:TAPS - 1], mm[c][:, GTOK - TAPS + 1:], ACT.Copy)
                        last.then_inc(xp_ok, 1)
                    for c in range(NC_):
                        wait(act, in_mm, n(2 * NC_, NC_ + c + 1))
                        wait(act, y_ok, n(NC_, c - NC_ + 1))
                        act.activation(sz[:, c, :], mm[c][:], ACT.Silu).then_inc(sz_ok, 1)
                if n.among(2, ALL):
                    c = n.before(2)
                    wait(act, tr3, c(1, 1))
                    wait(act, xT_ok, c(1))
                    wait(act, lg_mm, c(1))
                    act.activation(xaT[:, :, :], tp[:, :, :], ACT.Copy).then_inc(xaT_ok, 1)
                if n.among(0, NG):
                    for c in range(NC_):
                        wait(act, conv_ok, n(NC_, c + 1))
                        act.activation(xc[:, c, :], xc[:, c, :], ACT.Silu).then_inc(xc_ok, 1)
                if n.among(1, NG + 1):
                    b = n.before(1)
                    for f in range(0, NF, 2):
                        wait(act, up_mm, b(NF, f + 1))
                        if f == 0:
                            wait(act, dn_mm, b(2))
                        act.activation(m1T[:, f, :], mm[f % 4][:], ACT.Relu).then_inc(m1a_ok, 1)
                if n.among(0, NG):
                    wait(act, x1_ok, n(2, 2))
                    wait(act, g2_ok, n(1))
                    squares(x1, ss2, ss2_ok)

        @block.vector
        def _(dve):
            def scaled(n, src, rn, rn_ok, dst, used, ok):
                wait(dve, rn_ok, n(1, 1))
                wait(dve, used, n(1))
                for t in range(GT):
                    last = dve.tensor_scalar(dst[:, t, :], src[:, t, :], rn[:, t:t + 1], D ** 0.5, ALU.mult, ALU.mult)
                last.then_inc(ok, 1)

            dve.wait_ge(x_loaded[0], 16)
            scaled(Step(None, 0, 0), x_in[0], rn1, rn1_ok, h, tr1, h_ok)
            dve.wait_ge(consts, N_CONST * 16)
            dve.wait_ge(setup, 3)
            for n, par in steps(dve, 2, ALL):
                if n.among(0, NG):
                    wait(dve, tr1, n(1, 1))
                    wait(dve, in_mm, n(2 * NC_))
                    dve.tensor_copy(hT[:, :, :], tp[:, :, :]).then_inc(hT_ok, 1)
                    for c in range(NC_):
                        wait(dve, xp_ok, n(NC_, c + 1))
                        wait(dve, y_ok, n(NC_, c - NC_ + 1))
                        dve.tensor_scalar(xc[:, c, :], xp[par][:, c, TAPS - 1:], conv_w[:, c, TAPS - 1:],
                                          conv_b[:, c:c + 1], ALU.mult, ALU.add).then_inc(tap, 1)
                        for k in range(TAPS - 1):
                            wait(dve, tap, n(NC_ * (TAPS - 1), c * (TAPS - 1) + k + 1))
                            dve.scalar_tensor_tensor(xc[:, c, :], xp[par][:, c, k:k + GTOK], conv_w[:, c, k:k + 1],
                                                     xc[:, c, :], ALU.mult, ALU.add)\
                               .then_inc(conv_ok if k == TAPS - 2 else tap, 1)
                if n.among(0, NG):
                    if n.reg is None:
                        dve.wait_ge(x_loaded[1 - par], 16 * ((n.off + 1) // 2 + 1))
                    else:
                        dve.wait_ge(x_loaded[1 - par], n.reg * 16 + 16 * ((n.off + 1) // 2 + 1))
                    scaled(n.before(-1), x_in[1 - par], rn1, rn1_ok, h, tr1, h_ok)
                if n.among(1, NG + 1):
                    b = n.before(1)
                    wait(dve, tr2, b(1, 1))
                    wait(dve, up_mm, b(NF))
                    dve.tensor_copy(h1T[:, :, :], tp[:, :, :]).then_inc(h1T_ok, 1)
                if n.among(2, ALL):
                    c = n.before(2)
                    wait(dve, lg_mm, c(1, 1))
                    dve.tensor_copy(logits[:, tiles(c), :],
                                    ro[0][:, 0, 0:GT * E].rearrange("p (t e) -> p t e", t=GT)).then_inc(lg_ok, 1)
                if n.among(1, NG + 1):
                    b = n.before(1)
                    for f in range(1, NF, 2):
                        wait(dve, up_mm, b(NF, f + 1))
                        if f == 1:
                            wait(dve, dn_mm, b(2))
                        dve.tensor_scalar(m1T[:, f, :], mm[f % 4][:], 0.0, None, ALU.max).then_inc(m1v_ok, 1)
                if n.among(0, NG):
                    wait(dve, xx_ok, n(1))
                    for j in range(2):
                        wait(dve, out_mm, n(2, j + 1))
                        dve.tensor_tensor(x1[:, 2 * j:2 * j + 2, :], ro[j][:, :, :],
                                          x_in[par][:, 2 * j:2 * j + 2, :], ALU.add).then_inc(x1_ok, 1)
                    wait(dve, x1_ok, n(2, 2))
                    scaled(n, x1, rn2, rn2_ok, h1, tr2, h1_ok)
                if n.among(1, NG + 1):
                    b = n.before(1)
                    wait(dve, xx_ok, b(1, 1))
                    wait(dve, xa_ok, b(1))
                    for j in range(2):
                        wait(dve, dn_mm, b(2, j + 1))
                        dve.tensor_tensor(x2[:, 2 * j:2 * j + 2, :], ro[j][:, :, :], xx[:, 2 * j:2 * j + 2, :],
                                          ALU.add).then_inc(x2_ok, 1)
                    for t in range(GT):
                        wait(dve, x2_ok, b(2, t // 2 + 1))
                        dve.bn_stats(bn[:, t, :], x2[:, t, :]).then_inc(bn_ok, 1)
                    wait(dve, bn_ok, b(GT, GT))
                    dve.sem_inc(passed_dve, 1)
                    for t in range(GT):
                        dve.bn_aggr(mv[:, t, :], bn[:, t, :]).then_inc(mv_ok, 1)
                    wait(dve, mv_ok, b(GT, GT))
                    wait(dve, rs_ok, b(1, 1))
                    wait(dve, row_st, b(16))
                    wait(dve, xs_ok, b(1))
                    wait(dve, tr3, b(1))
                    for t in range(GT):
                        last = dve.tensor_scalar(xa[:, t, :], x2[:, t, :], mv[:, t, 0:1], rs[:, t:t + 1],
                                                 ALU.subtract, ALU.mult)
                    last.then_inc(xa_ok, 1)

        @block.tensor
        def _(pe):
            def transposes(src, done):
                for f in range(KD):
                    for t in range(GT):
                        last = pe.transpose(tp[:, f, t * P:(t + 1) * P], src[:, t, f * P:(f + 1) * P], ident[:])
                last.then_inc(done, 1)

            def chunk(c, w, rhsT, done):
                for k in range(KD):
                    last = pe.matmul(mm[c % 4][:], w[:, k, c * P:(c + 1) * P], rhsT[:, k, :],
                                     start=(k == 0), stop=(k == KD - 1))
                last.then_inc(done, 1)

            def rows(lhsT, w, chunks, done):
                for t in range(GT):
                    for k in range(chunks):
                        last = pe.matmul(ro[t // 2][:, t % 2, :], lhsT[:, k, t * P:(t + 1) * P], w[:, k, :],
                                         start=(k == 0), stop=(k == chunks - 1))
                    if t % 2:
                        last.then_inc(done, 1)

            pe.wait_ge(consts, N_CONST * 16)
            for n, par in steps(pe, 2, ALL):
                a, b, c3 = n, n.before(1), n.before(2)
                has_a, has_b, has_c = n.among(0, NG), n.among(1, NG + 1), n.among(2, ALL)
                if has_a:
                    wait(pe, h_ok, a(1, 1))
                    wait(pe, h1T_ok, a(1, -1))
                    transposes(h, tr1)
                    wait(pe, hT_ok, a(1, 1))
                    for c in range(2 * NC_):
                        if c < 4:
                            wait(pe, sz_ok, a(NC_, c - NC_ + 1))
                            if c == 0:
                                wait(pe, m1a_ok, a(NF // 2, -NF // 2))
                                wait(pe, m1v_ok, a(NF // 2, -NF // 2))
                        else:
                            wait(pe, xp_ok, a(NC_, c - 4 + 1))
                        chunk(c, w_in, hT, in_mm)
                if has_c:
                    wait(pe, xa_ok, c3(1, 1))
                    wait(pe, hT_ok, a(1, 1)) if has_a else wait(pe, h1T_ok, c3(1, 1))
                    transposes(xa, tr3)
                if has_b:
                    wait(pe, h1_ok, b(1, 1))
                    if has_a:
                        wait(pe, hT_ok, a(1, 1))
                    if has_c:
                        wait(pe, xaT_ok, c3(1, 1))
                    transposes(h1, tr2)
                if has_c:
                    wait(pe, xaT_ok, c3(1, 1))
                    wait(pe, x2_ok, c3(2, 2))
                    for t in range(GT):
                        for k in range(KD):
                            last = pe.matmul(ro[0][:, 0, t * E:(t + 1) * E], xaT[:, k, t * P:(t + 1) * P],
                                             w_gate[:, k, :], start=(k == 0), stop=(k == KD - 1))
                    last.then_inc(lg_mm, 1)
                if has_b:
                    wait(pe, h1T_ok, b(1, 1))
                    for c in range(NF):
                        if c < 4:
                            if has_a:
                                wait(pe, sz_ok, a(NC_, c + 1))
                            elif c == 0:
                                wait(pe, m1a_ok, b(NF // 2))
                                wait(pe, m1v_ok, b(NF // 2))
                        else:
                            wait(pe, (m1a_ok, m1v_ok)[c % 2], b(NF // 2, (c - 4) // 2 + 1))
                        chunk(c, w_up, h1T, up_mm)
                if has_a:
                    wait(pe, y_ok, a(NC_, NC_))
                    wait(pe, x2_ok, a(2, -2))
                    if has_c:
                        wait(pe, lg_ok, c3(1, 1))
                    rows(yT, w_out, NC_, out_mm)
                if has_b:
                    wait(pe, m1a_ok, b(NF // 2, NF // 2))
                    wait(pe, m1v_ok, b(NF // 2, NF // 2))
                    if has_a:
                        wait(pe, x1_ok, a(2, 2))
                    if has_c:
                        wait(pe, lg_ok, c3(1, 1))
                    rows(m1T, w_dn, NF, dn_mm)



CAP = 48
TOPK = 6
TOPG = 3
EG = 8
IX = 88
NIX = 2
NSX = 4
CG = 4
CJ = CAP // CG
RING = 8
SCALE_MOE = 16.0
LOW = -3.0e38
TAKEN = 3.0e38


def experts_phase(nc, io, keep):
    with ExitStack() as ctx:
        kit = Kit(nc, ctx)
        sb, ps = kit.sb, kit.ps
        x_sb, ident, logits = keep["x_sb"], keep["ident"], keep["logits"]
        inner = ctx.enter_context(ExitStack())

        ws_gu = sb("ws_gu", [P, KD, 2 * NSX * IX])
        ws_dn = sb("ws_dn", [IX, NSX, D])
        we_gu = sb("we_gu", [P, RING, KD, 2 * NIX * IX])
        we_dn = sb("we_dn", [IX, RING, NIX, D])
        upper = sb("upper", [P, P], BF16)
        ones = sb("ones", [P, P], BF16)
        ones_f = sb("ones_f", [P, 1])
        place = sb("place", [P, CJ])
        mine = sb("mine", [P, E])
        lane = sb("lane", [P, P])
        sg = sb("sg", [IX, NSX, GTOK])
        su = sb("su", [IX, NSX, GTOK])
        so = sb("so", [P, GT, D])
        sel = sb("sel", [P, NT, E])
        selr = sb("selr", [P, NT, CG, E], BF16)
        pre = [sb(f"pre{i}", [P, NT // 2 + NT, E], BF16) for i in range(2)]
        prer = sb("prer", [P, NT, CG, E], BF16)
        cum = sb("cum", [P, TOK], BF16)
        eg = sb("eg", [IX, 2, NIX, CAP])
        ea = sb("ea", [IX, 2, NIX, CAP])
        cnt = sb("cnt", [P, CJ])
        idx = sb("idx", [P, CJ], U32)
        w_slot = sb("w_slot", [P, CJ])
        wtmp = sb("wtmp", [P, CJ, E])
        rel = sb("rel", [P, NT, CJ])
        base = sb("base", [P, NT])
        busy_f = sb("busy_f", [P, NT])
        busy = sb("busy", [1, NT], I32)
        rden = sb("rden", [P, NT])
        rsum = sb("rsum", [P, NT])
        arena = sb("arena", [P, 7168])
        at = [0]

        def view(*shape):
            n = int(np.prod(shape))
            v = arena[:, at[0]:at[0] + n]
            at[0] += n
            names = "abc"[:len(shape)]
            return v.rearrange(f"p ({' '.join(names)}) -> p {' '.join(names)}", **dict(zip(names, shape)))

        gm, gr = view(NT, 2 * EG), view(NT, 2 * EG)
        kept = view(NT, EG)
        sc, sr = view(NT, E + 8), view(NT, E + 8)
        ex, wt = view(NT, E), view(NT, E)
        t8, t8b = sb("t8", [P, NT, 8]), sb("t8b", [P, NT, 8])
        at[0] = 0
        xg = view(CJ, ROW)
        y = view(CJ, D)
        dump = arena[:, 0:TOK // 2].bitcast(BF16)
        xgT = keep["xT"][:, 0, 0:KD * E * CAP].rearrange("p (k e c) -> p k e c", k=KD, e=E)
        yT = keep["xT"][:, 1, 0:KD * E * CAP].rearrange("p (k c e) -> p k c e", k=KD, e=E)
        xT = keep["xT"]

        mm = [ps(f"em{i}", [P, GTOK]) for i in range(4)]
        ro = [ps(f"er{i}", [P, 2, D]) for i in range(2)]
        tp = [ps(f"et{i}", [P, GTOK]) for i in range(2)]

        (consts, gu_mm, sg_ok, su_ok, sa_ok, dn_mm, so_ok, r_ok, rt, mset, sub_ok, exp_ok, pre_ok, cum_mm,
         cum_ok, cnt_ok, idx_ok, w_st, gath, busy_mm, busy_ok, tr_ok, xg_ok, egu_mm, eg_ok, ea_ok, edn_mm, ey_ok,
         ty_ok, y_ok, ws_ok, oh_ok, cb_mm, cb_ok, rel_ok) = kit.sems(
            "consts2 shared_gu_done shared_gate_ready shared_up_ready shared_act_ready shared_down_done "
            "shared_out_ready shared_added route_step softmax_step centered exp_ready prefix_ready cum_done cum_ready "
            "count_done slot_token_ready weights_stored gathered busy_done busy_ready slots_transposed "
            "slot_features_ready expert_gu_done expert_gate_ready expert_act_ready expert_down_done "
            "expert_out_ready out_transposed slot_out_ready slot_weight_ready onehot_ready combine_done "
            "combined relative_ready")
        ring = kit.sems(" ".join(f"expert_weights_{i}" for i in range(RING)))
        N2 = 10
        HALF = 5

        def shared(eng, lo, hi):
            with eng.Fori(0, hi - lo) as r:
                yield Step(r, 1, lo)

        block = inner.enter_context(nc.Block())

        @block.sync
        def _(sp):
            for src, dst in (("ws_gu", ws_gu), ("ws_dn", ws_dn), ("upper", upper), ("ones", ones), ("ones_f", ones_f),
                             ("place", place), ("mine", mine), ("lane", lane), ("base", base)):
                sp.dma_start(dst[:], io[src]).then_inc(consts, 16)
            sp.dma_start(io["rows"][TOK:TOK + P, :], io["zeros"]).then_inc(consts, 16)

            def weights(i, e):
                sp.dma_start(we_gu[:, i, :, :], io["we_gu"][:, bass.ds(e, 1), :, :].rearrange("p e k n -> p (e k) n")).then_inc(ring[i], 16)
                sp.dma_start(we_dn[:, i, :, :], io["we_dn"][:, bass.ds(e, 1), :, :].rearrange("p e k n -> p (e k) n")).then_inc(ring[i], 16)

            for i in range(RING):
                weights(i, i)
            sp.wait_ge(rt, 12)
            sp.dma_start(io["rows_t"][:, :, D:ROW], wt).then_inc(w_st, 16)
            with sp.Fori(0, E // RING - 1) as r:
                for i in range(RING):
                    sp.wait_ge(edn_mm, r * RING + (i + 1))
                    weights(i, r * RING + (RING + i))

        @block.gpsimd
        def _(pool):
            def act(n):
                for i in range(NSX):
                    wait(pool, sg_ok, n(NSX, i + 1))
                    wait(pool, su_ok, n(NSX, i + 1))
                    pool.tensor_tensor(su[:, i, :], sg[:, i, :], su[:, i, :], ALU.mult).then_inc(sa_ok, 1)

            def add(b):
                wait(pool, so_ok, b(2, 2))
                pool.tensor_tensor(x_sb[:, tiles(b), :], x_sb[:, tiles(b), :], so[:, :, :], ALU.add).then_inc(r_ok, 1)

            act(Step(None, 0, 0))
            for n in shared(pool, 1, NG):
                act(n)
                add(n.before(1))
            pool.wait_ge(idx_ok, 1)
            pool.wait_ge(w_st, 16)
            pool.wait_ge(consts, 16 * N2)
            for j in range(CJ):
                pool.indirect_dma_start(out=xg[:, j, :], out_offset=None, in_=io["rows"][:, :],
                                        in_offset=bass.IndirectOffsetOnAxis(ap=idx[:, j:j + 1], axis=0)).then_inc(gath, 16)
            add(Step(None, 0, NG - 1))

        @block.scalar
        def _(act):
            def gate_up(n):
                for i in range(NSX):
                    wait(act, gu_mm, n(2 * NSX, 2 * i + 1))
                    if i == 0:
                        wait(act, sa_ok, n(NSX))
                        wait(act, dn_mm, n(2))
                    act.activation(sg[:, i, :], mm[(2 * i) % 4][0:IX, :], ACT.Silu).then_inc(sg_ok, 1)
                    wait(act, gu_mm, n(2 * NSX, 2 * i + 2))
                    act.activation(su[:, i, :], mm[(2 * i + 1) % 4][0:IX, :], ACT.Copy).then_inc(su_ok, 1)

            def down(b):
                wait(act, r_ok, b(1))
                for j in range(2):
                    wait(act, dn_mm, b(2, j + 1))
                    act.activation(so[:, 2 * j:2 * j + 2, :], ro[j][:, :, :], ACT.Copy).then_inc(so_ok, 1)

            gate_up(Step(None, 0, 0))
            for lo, hi in ((1, HALF), (HALF, NG)):
                for n in shared(act, lo, hi):
                    down(n.before(1))
                    gate_up(n)
                if lo == 1:
                    act.wait_ge(sub_ok, 1)
                    act.activation(ex, ex, ACT.Exp).then_inc(exp_ok, 1)
            down(Step(None, 0, NG - 1))
            with act.Fori(0, E // RING) as r:
                for i in range(RING):
                    act.wait_ge(egu_mm, r * RING + (i + 1))
                    if i >= 2:
                        act.wait_ge(ea_ok, r * RING + (i - 1))
                    else:
                        act.wait_ge(ea_ok, r * RING)
                    act.activation(eg[:, i % 2, :, :],
                                   mm[i % 4][0:IX, 0:NIX * CAP].rearrange("p (a c) -> p a c", a=NIX), ACT.Silu).then_inc(eg_ok, 1)
                    act.wait_ge(edn_mm, r * RING + (i + 1))
                    act.activation(yT[:, :, :, bass.ds(r * RING + i, 1)].rearrange("p k c e -> p k (c e)"),
                                   ro[i % 2][:, 0, 0:KD * CAP].rearrange("p (k c) -> p k c", k=KD), ACT.Copy).then_inc(ey_ok, 1)

        @block.vector
        def _(dve):
            step = [0]

            def then(ins):
                step[0] += 1
                ins.then_inc(rt, 1)
                dve.wait_ge(rt, step[0])

            dve.memset(gm[:, :, EG:], LOW)
            dve.memset(sc[:, :, E:], LOW)
            dve.memset(pre[0][:, 0:NT // 2, :], 0.0)
            dve.memset(pre[1][:, 0:NT // 2, :], 0.0)
            then(dve.tensor_reduce(gm[:, :, 0:EG], logits[:, :, :].rearrange("p t (g m) -> p t g m", g=EG), AX.X, ALU.max))
            for t in range(NT):
                last = dve.max(t8[:, t, :], gm[:, t, 0:EG])
            then(last)
            then(dve.memset(t8[:, :, TOPG:], LOW))
            for t in range(NT):
                last = dve.match_replace(gr[:, t, :], t8[:, t, :], gm[:, t, :], TAKEN)
            then(last)
            then(dve.tensor_scalar(kept, gr[:, :, 0:EG], TAKEN, None, ALU.is_equal))
            then(dve.tensor_tensor(wt.rearrange("p t (g m) -> p (t g) m", g=EG),
                                   logits[:, :, :].rearrange("p t (g m) -> p (t g) m", g=EG),
                                   kept.rearrange("p t g -> p (t g)").unsqueeze(2).to_broadcast([P, NT * EG, E // EG]), ALU.mult))
            then(dve.tensor_scalar(sc[:, :, 0:E], wt, 0.0, None, ALU.add))
            for t in range(NT):
                last = dve.max(t8b[:, t, :], sc[:, t, 0:E])
            then(last)
            dve.tensor_tensor(ex, sc[:, :, 0:E], t8b[:, :, 0:1].to_broadcast([P, NT, E]), ALU.subtract).then_inc(sub_ok, 1)
            then(dve.memset(t8b[:, :, TOPK:], LOW))
            for t in range(NT):
                last = dve.match_replace(sr[:, t, :], t8b[:, t, :], sc[:, t, :], TAKEN)
            then(last)
            then(dve.tensor_scalar(sel[:, :, :], sr[:, :, 0:E], TAKEN, None, ALU.is_equal))
            dve.tensor_copy(selr[:, :, :, :], sel[:, :, :].unsqueeze(2).to_broadcast([P, NT, CG, E])).then_inc(pre_ok, 1)
            dve.tensor_copy(pre[0][:, NT // 2:, :], sel[:, :, :]).then_inc(pre_ok, 1)
            for d in range(5):
                dve.wait_ge(pre_ok, 2 + d)
                a, b = pre[d % 2], pre[(d + 1) % 2]
                dve.tensor_tensor(b[:, NT // 2:, :], a[:, NT // 2:, :],
                                  a[:, NT // 2 - (1 << d):NT // 2 + NT - (1 << d), :], ALU.add).then_inc(pre_ok, 1)
            dve.wait_ge(pre_ok, 7)
            dve.tensor_copy(prer[:, :, :, :],
                            pre[1][:, NT // 2 - 1:NT // 2 - 1 + NT, :].unsqueeze(2).to_broadcast([P, NT, CG, E])).then_inc(pre_ok, 1)
            dve.wait_ge(exp_ok, 1)
            dve.tensor_reduce(rsum[:], ex, AX.X, ALU.add).then_inc(mset, 1)
            dve.wait_ge(mset, 1)
            dve.reciprocal(rden[:], rsum[:]).then_inc(mset, 1)
            dve.wait_ge(mset, 2)
            dve.tensor_tensor(wt, ex, rden[:, :].unsqueeze(2).to_broadcast([P, NT, E]), ALU.mult).then_inc(mset, 1)
            dve.wait_ge(mset, 3)
            then(dve.scalar_tensor_tensor(wt, wt, SCALE_MOE, sel[:, :, :], ALU.mult, ALU.mult))
            assert step[0] == 12
            for g in range(NG):
                dve.wait_ge(cum_mm, g + 1)
                dve.tensor_copy(cum[:, g * GTOK:(g + 1) * GTOK], tp[g % 2][:, :]).then_inc(cum_ok, 1)
            dve.wait_ge(cum_ok, NG)
            dve.wait_ge(consts, 16 * N2)
            dve.memset(busy_f[:, 0:1], 1.0)
            dve.tensor_scalar(busy_f[:, 1:], cum[:, 0:TOK].rearrange("p (t c) -> p t c", c=P)[:, 0:NT - 1, P - 1],
                              float(CAP), None, ALU.is_lt).then_inc(cnt_ok, 1)
            for j in range(CJ):
                dve.wait_ge(cnt_ok, j + 1)
                dve.tensor_scalar(dump, cum[:, :], place[:, j:j + 1], 0.0, ALU.is_le, ALU.add,
                                  accum_out=cnt[:, j:j + 1]).then_inc(cnt_ok, 1)
            dve.wait_ge(cnt_ok, CJ + 1)
            dve.tensor_copy(idx[:, :], cnt[:, :]).then_inc(idx_ok, 1)
            dve.wait_ge(busy_mm, 1)
            dve.tensor_copy(busy[:, :], tp[0][0:1, 0:NT]).then_inc(busy_ok, 1)
            dve.wait_ge(gath, 16 * CJ)
            dve.tensor_tensor(wtmp[:, :, :], xg[:, :, D:ROW], mine[:, :].unsqueeze(1).to_broadcast([P, CJ, E]), ALU.mult).then_inc(ws_ok, 1)
            dve.wait_ge(ws_ok, 1)
            dve.tensor_reduce(w_slot[:, :], wtmp[:, :, :], AX.X, ALU.add).then_inc(ws_ok, 1)
            for j in range(CJ):
                for k in range(KD):
                    m = j * KD + k
                    dve.wait_ge(tr_ok, m + 1)
                    dve.tensor_copy(xgT[:, k, :, j * CG:(j + 1) * CG].rearrange("p e c -> p c e"),
                                    tp[m % 2][:, 0:P].rearrange("p (c e) -> p c e", c=CG)).then_inc(xg_ok, 1)
            with dve.Fori(0, E // RING) as r:
                for i in range(RING):
                    dve.wait_ge(eg_ok, r * RING + (i + 1))
                    dve.wait_ge(edn_mm, r * RING + max(i - 1, 0))
                    dve.tensor_tensor(ea[:, i % 2, :, :], eg[:, i % 2, :, :],
                                      mm[i % 4][0:IX, NIX * CAP:2 * NIX * CAP].rearrange("p (a c) -> p a c", a=NIX),
                                      ALU.mult).then_inc(ea_ok, 1)
            dve.wait_ge(ws_ok, 2)
            for j in range(CJ):
                dve.wait_ge(ty_ok, j + 1)
                dve.tensor_scalar(y[:, j, :], tp[j % 2][:, 0:D], w_slot[:, j:j + 1], None, ALU.mult).then_inc(y_ok, 1)

        @block.tensor
        def _(pe):
            def gate_up(n):
                for c in range(2 * NSX):
                    if c == 0:
                        wait(pe, su_ok, n(NSX))
                    if c >= 4:
                        wait(pe, sg_ok if c % 2 == 0 else su_ok, n(NSX, (c - 4) // 2 + 1))
                    col = (c // 2 + (c % 2) * NSX) * IX
                    for k in range(KD):
                        last = pe.matmul(mm[c % 4][0:IX, :], ws_gu[:, k, col:col + IX],
                                         xT[:, k, bass.ds(n(GTOK), GTOK)], start=(k == 0), stop=(k == KD - 1))
                    last.then_inc(gu_mm, 1)

            def down(b):
                wait(pe, sa_ok, b(NSX, NSX))
                wait(pe, so_ok, b(2))
                for t in range(GT):
                    for k in range(NSX):
                        last = pe.matmul(ro[t // 2][:, t % 2, :], su[:, k, t * P:(t + 1) * P], ws_dn[:, k, :],
                                         start=(k == 0), stop=(k == NSX - 1))
                    if t % 2:
                        last.then_inc(dn_mm, 1)

            pe.wait_ge(consts, 16 * N2)
            gate_up(Step(None, 0, 0))
            for lo, hi in ((1, HALF), (HALF, NG)):
                for n in shared(pe, lo, hi):
                    down(n.before(1))
                    gate_up(n)
                if lo == 1:
                    pe.wait_ge(pre_ok, 8)
                    for t in range(NT):
                        g = t // GT
                        if t % GT == 0 and g >= 2:
                            pe.wait_ge(cum_ok, g - 1)
                        o = tp[g % 2][:, (t % GT) * P:(t % GT + 1) * P]
                        pe.matmul(o, selr[:, t, :, :].rearrange("p c e -> p (c e)"), upper[:], start=True, stop=False)
                        last = pe.matmul(o, prer[:, t, :, :].rearrange("p c e -> p (c e)"), ones[:], start=False, stop=True)
                        if t % GT == GT - 1:
                            last.then_inc(cum_mm, 1)
            down(Step(None, 0, NG - 1))
            pe.wait_ge(cnt_ok, 1)
            pe.wait_ge(cum_ok, NG)
            pe.matmul(tp[0][0:1, 0:NT], ones_f[:, 0:1], busy_f[:, :], start=True, stop=True).then_inc(busy_mm, 1)
            pe.wait_ge(busy_ok, 1)
            pe.wait_ge(gath, 16 * CJ)
            for j in range(CJ):
                for k in range(KD):
                    m = j * KD + k
                    if m >= 2:
                        pe.wait_ge(xg_ok, m - 1)
                    pe.transpose(tp[m % 2][:, 0:P], xg[:, j, k * P:(k + 1) * P], ident[:]).then_inc(tr_ok, 1)
            pe.wait_ge(xg_ok, CJ * KD)
            pe.wait_ge(so_ok, 2 * NG)

            def expert_gu(e, i):
                pe.wait_ge(ring[i], e[1])
                pe.wait_ge(ea_ok, e[2])
                for c in range(2 * NIX):
                    for k in range(KD):
                        last = pe.matmul(mm[i % 4][0:IX, c * CAP:(c + 1) * CAP], we_gu[:, i, k, c * IX:(c + 1) * IX],
                                         xgT[:, k, bass.ds(e[0], 1), :].rearrange("p e c -> p (e c)"),
                                         start=(k == 0), stop=(k == KD - 1))
                last.then_inc(egu_mm, 1)

            def expert_down(count, i):
                pe.wait_ge(ea_ok, count(1))
                pe.wait_ge(ey_ok, count(-1))
                for f in range(KD):
                    for k in range(NIX):
                        last = pe.matmul(ro[i % 2][:, 0, f * CAP:(f + 1) * CAP], we_dn[:, i, k, f * P:(f + 1) * P],
                                         ea[:, i % 2, k, :], start=(k == 0), stop=(k == NIX - 1))
                last.then_inc(edn_mm, 1)

            with pe.Fori(0, E // RING) as r:
                for i in range(RING):
                    expert_gu((r * RING + i, r * 32 + 32, r * RING + max(i - 3, 0)), i)
                    if i >= 1:
                        expert_down(lambda d: r * RING + (i - 1 + d) if i - 1 + d > 0 else r * RING, i - 1)
                expert_down(lambda d: r * RING + (RING - 1 + d), RING - 1)
            pe.wait_ge(ey_ok, E)
            for j in range(CJ):
                if j >= 2:
                    pe.wait_ge(y_ok, j - 1)
                for k in range(KD):
                    last = pe.transpose(tp[j % 2][:, k * P:(k + 1) * P],
                                        yT[:, k, j * CG:(j + 1) * CG, :].rearrange("p c e -> p (c e)"), ident[:])
                last.then_inc(ty_ok, 1)

        inner.close()

        hot = [xT[:, 0, i * CJ * P:(i + 1) * CJ * P].rearrange("p (j c) -> p j c", j=CJ) for i in range(2)]
        block = ctx.enter_context(nc.Block())

        @block.vector
        def _(dve):
            dve.tensor_tensor(rel[:, :, :], cnt[:, :].unsqueeze(1).to_broadcast([P, NT, CJ]),
                              base[:, :].unsqueeze(2).to_broadcast([P, NT, CJ]), ALU.subtract).then_inc(rel_ok, 1)
            dve.wait_ge(rel_ok, 1)
            with dve.Fori(0, NT // 2) as r:
                for i in range(2):
                    t = Step(r, 2, i)
                    some = dve.value_load(busy[0:1, bass.ds(t(1), 1)], min_val=0, max_val=P)
                    with dve.If(some > 0):
                        dve.wait_ge(cb_mm, r * 2)
                        dve.tensor_tensor(hot[i], rel[:, bass.ds(t(1), 1), :].rearrange("p a j -> p (a j)")
                                          .unsqueeze(2).to_broadcast([P, CJ, P]),
                                          lane[:, :].unsqueeze(1).to_broadcast([P, CJ, P]), ALU.is_equal).then_inc(oh_ok, 1)
                        dve.wait_ge(cb_mm, t(1, 1))
                        xt = x_sb[:, bass.ds(t(1), 1), :].rearrange("p a b -> p (a b)")
                        dve.tensor_tensor(xt, ro[i][:, 0, :], xt, ALU.add).then_inc(cb_ok, 1)

        @block.tensor
        def _(pe):
            with pe.Fori(0, NT // 2) as r:
                for i in range(2):
                    t = Step(r, 2, i)
                    some = pe.value_load(busy[0:1, bass.ds(t(1), 1)], min_val=0, max_val=P)
                    with pe.If(some > 0):
                        pe.wait_ge(oh_ok, t(1, 1))
                        pe.wait_ge(cb_ok, r * 2)
                        for j in range(CJ):
                            last = pe.matmul(ro[i][:, 0, :], hot[i][:, j, :], y[:, j, :],
                                             start=(j == 0), stop=(j == CJ - 1))
                        last.then_inc(cb_mm, 1)


NB = 4
ST = NT // NB
SEQ = ST * P
HEADS = 16
HD = D // HEADS
HG = 4
NHG = HEADS // HG
HP = 32
HALF_D = HD // 2
BLK = 64
MASKED = -1.0e30
NLN = 6
N3 = 12

MAX_UNITS = [(i, p, c, min(512, (i + 1) * P - 512 * c))
             for i in range(ST) for c in range(i // 4 + 1) for p in range(2)]
SUM_UNITS = [(c, j, p, max(512 * c, P * j), 512 * (c + 1) - max(512 * c, P * j))
             for c in range(2) for j in range(4 * (c + 1)) for p in range(2)]
NU = len(MAX_UNITS)
FIRST_Q = sum(u[0] == 0 for u in SUM_UNITS)


class Chain:

    def __init__(self, eng, sem, n, per):
        self.eng, self.sem, self.n, self.per, self.k = eng, sem, n, per, 0

    def then(self, ins):
        self.k += 1
        ins.then_inc(self.sem, 1)
        wait(self.eng, self.sem, self.n(self.per, self.k))

    def end(self):
        assert self.k == self.per, (self.k, self.per)


def attention_ffn_phase(nc, io, keep):
    with ExitStack() as ctx:
        kit = Kit(nc, ctx)
        sb, ps = kit.sb, kit.ps
        x_sb, ident = keep["x_sb"], keep["ident"]

        w_qkv = sb("w_qkv", [P, KD, NHG, 3 * HG * HD])
        w_o = sb("w_o", [P, KD, D])
        w_fg = sb("w_fg", [P, KD, DF])
        w_fu = sb("w_fu", [P, KD, DF])
        w_fd = sb("w_fd", [P, NF, D])
        cos = sb("cos", [P, ST, HALF_D])
        sin = sb("sin", [P, ST, HALF_D])
        first_half = sb("first_half", [P, P])
        last_half = sb("last_half", [P, P])
        masked = sb("masked", [P, BLK])
        power = sb("power3", [P, GT])
        eps = sb("eps3", [P, GT])
        xb = sb("xb", [P, ST, D])
        xr = sb("xr", [P, ST, D])
        xbT = sb("xbT", [P, KD, SEQ])
        qk = sb("qk", [P, ST, 2 * HG, HD])
        v = sb("v", [P, ST, HG, HP])
        qkp = sb("qkp", [P, ST, 2 * HG, HP])
        r1 = [sb(f"rope{i}", [P, ST, 2 * HG, HALF_D]) for i in range(4)]
        mtmp = sb("mtmp", [P, ST // 2, 2, HG])
        qT = sb("qT", [P, SEQ])
        kT = sb("kT", [P, SEQ])
        pb = [sb(f"pb{i}", [P, 2, 512]) for i in range(3)]
        cs = sb("cs", [P, 2, 512])
        rc = sb("rc", [P, GT, HG])
        ctok = sb("ctok", [P, ST, D])
        cT = sb("cT", [P, KD, SEQ])
        sgl = sb("sgl", [P, 2, 512])
        hj = sb("hj", [P, 4, 512])
        aj = sb("aj", [P, 4, 512])
        ge = sb("ge", [P, 6, 512], BF16)
        nb = sb("nb", [P, 4, 512], BF16)
        hs = sb("hs", [P, NF, 512])
        ot = sb("ot", [P, GT, D])
        bn = sb("bn3", [P, GT, 6])
        mv = sb("mv3", [P, GT, 2])
        ve = sb("ve3", [P, GT])
        rs = sb("rs3", [P, GT])

        S = [ps(f"s{i}", [P, 2, 512]) for i in range(3)]
        C = ps("c", [P, 512])
        M = ps("m", [P, 512])

        (consts, setup, passed, bn_ok, mv_ok, ve_ok, rs_ok, ln_ok, tx, xTv_ok, xTa_ok, qkv_mm, qkv_ok, rope_v, rope_p,
         rv_ok, rp_ok, tq, q0_ok, k_ok, p1_mm, mx_ok, nm_ok, q1_ok, p2_mm, exp_ok, pv_mm, cs_ok, tm, rc_ok, cn_ok,
         tc, cTv_ok, cTa_ok, wo_mm, xr_ok, ff_mm, sl_ok, hm_ok, ab_ok, sp, hs_ok, fd_mm, f2_ok, out_st) = kit.sems(
            "consts3 setup3 passed3 bn3_ready mv3_ready ve3_ready rs3_ready layernorm_done x_transposed xT_low_ready "
            "xT_high_ready qkv_done qkv_ready rope_step_v rope_step_p rope_low_ready rope_high_ready qk_transposed "
            "qT_ready kT_ready max_scores_done maxima_ready negmax_ready qT_max_ready scores_done weights_ready "
            "weighted_done context_copied context_transposed rowsum_inverted context_ready ctx_transposed "
            "cT_low_ready cT_high_ready wo_done attn_residual_ready ffn_in_done silu_ready hidden_ready abs_ready "
            "sparse_step sparse_ready ffn_down_done ffn_residual_ready out_stored")

        block = ctx.enter_context(nc.Block())

        def x_tile(n, t):
            return x_sb[:, bass.ds(n(ST, t), 1), :].rearrange("p a b -> p (a b)")

        @block.sync
        def _(sync):
            for src, dst in (("w_qkv", w_qkv), ("cos", cos), ("sin", sin), ("first_half", first_half),
                             ("last_half", last_half), ("masked", masked), ("w_o", w_o), ("w_fg", w_fg), ("w_fu", w_fu),
                             ("w_fd", w_fd)):
                sync.dma_start(dst[:], io[src]).then_inc(consts, 16)
            with sync.Fori(0, NB) as b:
                n = Step(b, 1, 0)
                for g in range(2):
                    wait(sync, ln_ok, n(NLN, 5 + g))
                    sync.dma_start(io["out"][:, bass.ds(n(ST, g * GT), GT), :], ot[:, :, :]).then_inc(out_st, 16)
            sync.wait_ge(out_st, 16 * 2 * NB)

        @block.gpsimd
        def _(pool):
            pool.memset(power[:], -0.5)
            pool.memset(eps[:], 1e-5)
            pool.memset(v[:, :, :, :], 0.0).then_inc(setup, 1)
            pool.memset(qkp[:, :, :, :], 0.0).then_inc(setup, 1)
            pool.wait_ge(setup, 2)
            pool.memset(v[:, :, :, HD:HD + 1], 1.0).then_inc(setup, 1)
            pool.memset(qkp[:, :, HG:, HD:HD + 1], 1.0).then_inc(setup, 1)
            pool.wait_ge(setup, 4)
            pool.wait_ge(consts, 16 * 10)

            def inverse_deviation(n, k):
                wait(pool, mv_ok, n(NLN, k + 1))
                wait(pool, rs_ok, n(NLN, k))
                pool.tensor_tensor(ve[:], mv[:, :, 1], eps[:], ALU.add).then_inc(ve_ok, 1)
                wait(pool, ve_ok, n(NLN, k + 1))
                wait(pool, ln_ok, n(NLN, k))
                pool.tensor_tensor(rs[:], ve[:], power[:], ALU.pow).then_inc(rs_ok, 1)

            with pool.Fori(0, NB) as b:
                n = Step(b, 1, 0)
                inverse_deviation(n, 0)
                inverse_deviation(n, 1)
                with pool.Fori(0, NHG) as h:
                    q = Step(b * NHG + h, 1, 0)
                    chain = Chain(pool, rope_p, q, 2)
                    x1, x2 = qk[:, :, :, 0:HALF_D], qk[:, :, :, HALF_D:]
                    wait(pool, qkv_ok, q(2, 2))
                    wait(pool, rp_ok, q(1))
                    pool.tensor_tensor(r1[2][:, :, :, :], x2, cos[:, :, :].unsqueeze(2).to_broadcast([P, ST, 2 * HG, HALF_D]),
                                       ALU.mult).then_inc(rope_p, 1)
                    pool.tensor_tensor(r1[3][:, :, :, :], x1, sin[:, :, :].unsqueeze(2).to_broadcast([P, ST, 2 * HG, HALF_D]),
                                       ALU.mult).then_inc(rope_p, 1)
                    wait(pool, rope_p, q(2, 2))
                    wait(pool, tq, q(3))
                    pool.tensor_tensor(qkp[:, :, :, HALF_D:HD], r1[2][:, :, :, :], r1[3][:, :, :, :], ALU.add).then_inc(rp_ok, 1)
                for k in range(2, NLN):
                    inverse_deviation(n, k)

        @block.scalar
        def _(act):
            act.wait_ge(setup, 4)
            with act.Fori(0, NB) as b:
                n = Step(b, 1, 0)
                wait(act, tx, n(4, 2))
                act.activation(xbT[:, 1, :].rearrange("p (a c) -> p a c", a=2), S[1][:, :, :], ACT.Copy).then_inc(xTa_ok, 1)
                with act.Fori(0, NHG) as h:
                    q = Step(b * NHG + h, 1, 0)
                    for s in range(2):
                        wait(act, qkv_mm, q(2, s + 1))
                        wait(act, rv_ok, q(1))
                        wait(act, rp_ok, q(1))
                        wait(act, pv_mm, q(NU))
                        src = S[s][:, :, :].rearrange("p a (t c) -> p (a t) c", t=2)
                        act.activation(qk[:, s * GT:(s + 1) * GT, :, :].rearrange("p t h d -> p t (h d)"),
                                       src[:, :, 0:2 * HG * HD], ACT.Copy)
                        act.activation(v[:, s * GT:(s + 1) * GT, :, 0:HD],
                                       src[:, :, 2 * HG * HD:3 * HG * HD].rearrange("p t (h d) -> p t h d", h=HG),
                                       ACT.Copy).then_inc(qkv_ok, 1)
                    wait(act, tq, q(3, 1))
                    wait(act, p2_mm, q(NU))
                    act.activation(qT[:, :].rearrange("p (a c) -> p a c", a=2), S[0][:, :, :], ACT.Copy).then_inc(q0_ok, 1)
                    wait(act, tq, q(3, 3))
                    act.activation(qT[:, :].rearrange("p (a c) -> p a c", a=2), S[0][:, :, :], ACT.Copy).then_inc(q1_ok, 1)
                    for u, (c, j, p, first, width) in enumerate(SUM_UNITS):
                        wait(act, p2_mm, q(NU, u + 1))
                        wait(act, pv_mm, q(NU, u - 2 if u >= 3 else 0))
                        act.activation(pb[u % 3][:, :, 0:width], S[u % 3][:, :, 0:width], ACT.Exp,
                                       scale=HD ** -0.5).then_inc(exp_ok, 1)
                wait(act, tc, n(2, 2))
                wait(act, wo_mm, n(2))
                act.activation(cT[:, 1, :].rearrange("p (a c) -> p a c", a=2), S[1][:, :, :], ACT.Copy).then_inc(cTa_ok, 1)
                wait(act, tx, n(4, 4))
                act.activation(xbT[:, 1, :].rearrange("p (a c) -> p a c", a=2), S[1][:, :, :], ACT.Copy).then_inc(xTa_ok, 1)
                for w in range(17):
                    if w < 16:
                        wait(act, ff_mm, n(16, w + 1))
                        wait(act, hm_ok, n(16, max(w - 1, 0)))
                        act.activation(sgl[:, w % 2, :], S[w % 3][:, 0, :], ACT.Silu).then_inc(sl_ok, 1)
                    if w >= 1:
                        wait(act, hm_ok, n(16, w))
                        wait(act, hs_ok, n(4, (w - 1) // 4))
                        act.activation(aj[:, (w - 1) % 4, :], hj[:, (w - 1) % 4, :], ACT.Abs).then_inc(ab_ok, 1)

        @block.vector
        def _(dve):
            dve.wait_ge(consts, 16 * 10)
            dve.wait_ge(setup, 4)

            def layernorm(n, k, src, dst):
                wait(dve, mv_ok, n(NLN, k))
                for t in range(GT):
                    last = dve.bn_stats(bn[:, t, :], src(t))
                last.then_inc(bn_ok, 1)
                wait(dve, bn_ok, n(NLN, k + 1))
                wait(dve, ln_ok, n(NLN, k))
                dve.sem_inc(passed, 1)
                for t in range(GT):
                    last = dve.bn_aggr(mv[:, t, :], bn[:, t, :])
                last.then_inc(mv_ok, 1)
                wait(dve, mv_ok, n(NLN, k + 1))
                wait(dve, rs_ok, n(NLN, k + 1))
                for t in range(GT):
                    last = dve.tensor_scalar(dst(t), src(t), mv[:, t, 0:1], rs[:, t:t + 1], ALU.subtract, ALU.mult)
                last.then_inc(ln_ok, 1)

            with dve.Fori(0, NB) as b:
                n = Step(b, 1, 0)
                wait(dve, f2_ok, n(4))
                for g in range(2):
                    layernorm(n, g, lambda t: x_tile(n, g * GT + t), lambda t: xb[:, g * GT + t, :])
                wait(dve, tx, n(4, 1))
                dve.tensor_copy(xbT[:, 0, :].rearrange("p (a c) -> p a c", a=2), S[0][:, :, :]).then_inc(xTv_ok, 1)
                with dve.Fori(0, NHG) as h:
                    q = Step(b * NHG + h, 1, 0)
                    x1, x2 = qk[:, :, :, 0:HALF_D], qk[:, :, :, HALF_D:]
                    wait(dve, qkv_ok, q(2, 2))
                    wait(dve, rv_ok, q(1))
                    dve.tensor_tensor(r1[0][:, :, :, :], x1, cos[:, :, :].unsqueeze(2).to_broadcast([P, ST, 2 * HG, HALF_D]),
                                      ALU.mult).then_inc(rope_v, 1)
                    dve.tensor_tensor(r1[1][:, :, :, :], x2, sin[:, :, :].unsqueeze(2).to_broadcast([P, ST, 2 * HG, HALF_D]),
                                      ALU.mult).then_inc(rope_v, 1)
                    wait(dve, rope_v, q(2, 2))
                    wait(dve, tq, q(3))
                    dve.tensor_tensor(qkp[:, :, :, 0:HALF_D], r1[0][:, :, :, :], r1[1][:, :, :, :], ALU.subtract).then_inc(rv_ok, 1)
                    wait(dve, tq, q(3, 2))
                    wait(dve, p2_mm, q(NU))
                    dve.tensor_copy(kT[:, :].rearrange("p (a c) -> p a c", a=2), S[1][:, :, :]).then_inc(k_ok, 1)
                    for u, (i, p, c, width) in enumerate(MAX_UNITS):
                        wait(dve, p1_mm, q(NU, u + 1))
                        if i < ST // 2:
                            dst = qkp[:, i, 2 * p:2 * p + 2, HD]
                        else:
                            dst = mtmp[:, i - ST // 2, c, 2 * p:2 * p + 2]
                            if i == ST // 2:
                                wait(dve, nm_ok, q(1))
                        dve.tensor_reduce(dst, S[u % 3][:, :, 0:width], AX.X, ALU.max, negate=True).then_inc(mx_ok, 1)
                    wait(dve, mx_ok, q(NU, NU))
                    dve.tensor_tensor(qkp[:, ST // 2:, 0:HG, HD], mtmp[:, :, 0, :], mtmp[:, :, 1, :], ALU.min).then_inc(nm_ok, 1)
                    for c in range(2):
                        wait(dve, pv_mm, q(NU, (FIRST_Q, NU)[c]))
                        wait(dve, tm, q(2, c))
                        dve.tensor_copy(cs[:, c, :], C[:, :]).then_inc(cs_ok, 1)
                        wait(dve, tm, q(2, c + 1))
                        wait(dve, cn_ok, q(2, c))
                        m = M[:, :].rearrange("p (t h d) -> p t h d", t=GT, h=HG)
                        dve.reciprocal(rc[:, :, :], m[:, :, :, HD]).then_inc(rc_ok, 1)
                        wait(dve, rc_ok, q(2, c + 1))
                        wait(dve, tc, n(2))
                        dve.tensor_tensor(ctok[:, c * GT:(c + 1) * GT, bass.ds(h * (HG * HD), HG * HD)]
                                          .rearrange("p t (h d) -> p t h d", h=HG),
                                          m[:, :, :, 0:HD], rc[:, :, :].unsqueeze(3).to_broadcast([P, GT, HG, HD]),
                                          ALU.mult).then_inc(cn_ok, 1)
                wait(dve, tc, n(2, 1))
                wait(dve, wo_mm, n(2))
                dve.tensor_copy(cT[:, 0, :].rearrange("p (a c) -> p a c", a=2), S[0][:, :, :]).then_inc(cTv_ok, 1)
                for s, bank in enumerate((S[2], S[0])):
                    wait(dve, wo_mm, n(2, s + 1))
                    rows = slice(s * GT, (s + 1) * GT)
                    dve.tensor_tensor(xr[:, rows, :], bank[:, :, :].rearrange("p a (t c) -> p (a t) c", t=2),
                                      xb[:, rows, :], ALU.add).then_inc(xr_ok, 1)
                wait(dve, xr_ok, n(2, 2))
                for g in range(2):
                    layernorm(n, 2 + g, lambda t: xr[:, g * GT + t, :], lambda t: xb[:, g * GT + t, :])
                wait(dve, tx, n(4, 3))
                dve.tensor_copy(xbT[:, 0, :].rearrange("p (a c) -> p a c", a=2), S[0][:, :, :]).then_inc(xTv_ok, 1)

                def hidden(w):
                    wait(dve, sl_ok, n(16, w + 1))
                    if w % 4 == 0:
                        wait(dve, hs_ok, n(4, w // 4))
                        wait(dve, ab_ok, n(16, w))
                    dve.tensor_tensor(hj[:, w % 4, :], S[w % 3][:, 1, :], sgl[:, w % 2, :], ALU.mult).then_inc(hm_ok, 1)

                def sparsify(k):
                    g, half = divmod(k, 2)
                    s = Step(n(4, k), 1, 0)
                    wait(dve, ab_ok, n(16, 4 * (k + 1)))
                    if k == 0:
                        wait(dve, fd_mm, n(4))
                    if k == 2:
                        wait(dve, fd_mm, n(4, 2))
                    wait(dve, hs_ok, s(1))
                    chain = Chain(dve, sp, s, 3)
                    def row(i, m):
                        return aj[:, i:i + 1, :].to_broadcast([P, m, 512])
                    dve.tensor_tensor(ge[:, 0:3, :], row(0, 3), aj[:, 1:4, :], ALU.is_ge)
                    dve.tensor_tensor(ge[:, 3:5, :], row(1, 2), aj[:, 2:4, :], ALU.is_ge)
                    chain.then(dve.tensor_tensor(ge[:, 5, :], aj[:, 2, :], aj[:, 3, :], ALU.is_ge))
                    dve.tensor_tensor(nb[:, 0, :], ge[:, 0, :], ge[:, 1, :], ALU.add)
                    dve.tensor_tensor(nb[:, 1, :], ge[:, 3, :], ge[:, 4, :], ALU.add)
                    dve.tensor_tensor(nb[:, 2, :], ge[:, 1, :], ge[:, 3, :], ALU.add)
                    chain.then(dve.tensor_tensor(nb[:, 3, :], ge[:, 2, :], ge[:, 4, :], ALU.add))
                    dve.tensor_tensor(nb[:, 0, :], nb[:, 0, :], ge[:, 2, :], ALU.add)
                    dve.tensor_tensor(nb[:, 1, :], nb[:, 1, :], ge[:, 0, :], ALU.subtract)
                    dve.tensor_tensor(nb[:, 2, :], nb[:, 2, :], ge[:, 5, :], ALU.subtract)
                    chain.then(dve.tensor_tensor(nb[:, 3, :], nb[:, 3, :], ge[:, 5, :], ALU.add))
                    for i, (op, bound) in enumerate(((ALU.is_ge, 2.0), (ALU.is_ge, 1.0), (ALU.is_le, 0.0), (ALU.is_le, 1.0))):
                        last = dve.scalar_tensor_tensor(hs[:, half * 4 + i, :], nb[:, i, :], bound, hj[:, i, :], op, ALU.mult)
                    last.then_inc(hs_ok, 1)
                    chain.end()

                def finish(g):
                    for s, bank in enumerate((C, M)):
                        wait(dve, fd_mm, n(4, 2 * g + s + 1))
                        rows = slice(g * GT + 2 * s, g * GT + 2 * s + 2)
                        dve.tensor_tensor(xr[:, rows, :], bank[:, :].rearrange("p (t c) -> p t c", t=2),
                                          xb[:, rows, :], ALU.add).then_inc(f2_ok, 1)
                    wait(dve, f2_ok, n(4, 2 * g + 2))
                    wait(dve, out_st, n(32, 16 * g))
                    layernorm(n, 4 + g, lambda t: xr[:, g * GT + t, :], lambda t: ot[:, t, :])

                for k in range(4):
                    for w in range(4 * k, 4 * k + 4):
                        hidden(w)
                    sparsify(k)
                    if k == 2:
                        finish(0)
                finish(1)

        @block.tensor
        def _(pe):
            pe.wait_ge(consts, 16 * 10)
            pe.wait_ge(setup, 4)

            def transposes(dst, src, done):
                for t in range(ST):
                    last = pe.transpose(dst[:, t // 4, (t % 4) * P:(t % 4 + 1) * P], src(t), ident[:])
                last.then_inc(done, 1)

            with pe.Fori(0, NB) as b:
                n = Step(b, 1, 0)
                wait(pe, ln_ok, n(NLN, 2))
                wait(pe, hm_ok, n(16))
                for f in range(KD):
                    transposes(S[f], lambda t: xb[:, t, f * P:(f + 1) * P], tx)
                with pe.Fori(0, NHG) as h:
                    q = Step(b * NHG + h, 1, 0)
                    wait(pe, xTv_ok, n(2, 1))
                    wait(pe, xTa_ok, n(2, 1))
                    wait(pe, exp_ok, q(NU))
                    for t in range(ST):
                        for k in range(KD):
                            last = pe.matmul(S[t // 4][:, t % 4 // 2, (t % 2) * 256:(t % 2) * 256 + 3 * HG * HD],
                                             xbT[:, k, t * P:(t + 1) * P],
                                             w_qkv[:, k, bass.ds(h, 1), :].rearrange("p a b -> p (a b)"),
                                             start=(k == 0), stop=(k == KD - 1))
                        if t % 4 == 3:
                            last.then_inc(qkv_mm, 1)
                    wait(pe, rv_ok, q(1, 1))
                    wait(pe, rp_ok, q(1, 1))
                    for s in range(2):
                        transposes(S[s], lambda t: qkp[:, t, s * HG:(s + 1) * HG, :].rearrange("p h d -> p (h d)"), tq)
                    wait(pe, q0_ok, q(1, 1))
                    wait(pe, k_ok, q(1, 1))
                    for u, (i, p, c, width) in enumerate(MAX_UNITS):
                        if u >= 3:
                            wait(pe, mx_ok, q(NU, u - 2))
                        diagonal = 512 * c + width == (i + 1) * P
                        for e in range(2):
                            o = HP * (2 * p + e)
                            last = pe.matmul(S[u % 3][:, e, 0:width], qT[o:o + HD, i * P:(i + 1) * P],
                                             kT[o:o + HD, 512 * c:512 * c + width], start=True, stop=not diagonal)
                            if diagonal:
                                last = pe.matmul(S[u % 3][:, e, width - BLK:width], first_half[o:o + 1, :],
                                                 masked[o:o + 1, :], start=False, stop=True)
                        last.then_inc(p1_mm, 1)
                    wait(pe, nm_ok, q(1, 1))
                    transposes(S[0], lambda t: qkp[:, t, 0:HG, :].rearrange("p h d -> p (h d)"), tq)
                    wait(pe, q1_ok, q(1, 1))

                    def scores(u):
                        c, j, p, first, width = SUM_UNITS[u]
                        if u >= 3:
                            wait(pe, exp_ok, q(NU, u - 2))
                        diagonal = first == j * P
                        for e in range(2):
                            o = HP * (2 * p + e)
                            last = pe.matmul(S[u % 3][:, e, 0:width], kT[o:o + HD + 1, j * P:(j + 1) * P],
                                             qT[o:o + HD + 1, first:first + width], start=True, stop=not diagonal)
                            if diagonal:
                                last = pe.matmul(S[u % 3][:, e, 0:BLK], last_half[o:o + 1, :],
                                                 masked[o:o + 1, :], start=False, stop=True)
                        last.then_inc(p2_mm, 1)

                    def weighted(u):
                        c, j, p, first, width = SUM_UNITS[u]
                        wait(pe, exp_ok, q(NU, u + 1))
                        if j == 0 and p == 0:
                            wait(pe, cs_ok, q(2, c))
                            wait(pe, f2_ok, n(4))
                        for e in range(2):
                            o = HP * (2 * p + e)
                            last = pe.matmul(C[o:o + HP, first - 512 * c:512], v[:, j, 2 * p + e, :],
                                             pb[u % 3][:, e, 0:width], start=(j == 0), stop=(j == 4 * c + 3))
                        last.then_inc(pv_mm, 1)

                    def back(c):
                        wait(pe, cs_ok, q(2, c + 1))
                        wait(pe, cn_ok, q(2, c))
                        for t in range(GT):
                            last = pe.transpose(M[:, t * P:(t + 1) * P], cs[:, c, t * P:(t + 1) * P], ident[:])
                        last.then_inc(tm, 1)

                    scores(0)
                    scores(1)
                    for u in range(NU):
                        if u + 2 < NU:
                            scores(u + 2)
                        weighted(u)
                        if u == FIRST_Q + 1:
                            back(0)
                    back(1)
                wait(pe, cn_ok, n(8, 8))
                for f in range(KD):
                    transposes(S[f], lambda t: ctok[:, t, f * P:(f + 1) * P], tc)
                wait(pe, cTv_ok, n(1, 1))
                wait(pe, cTa_ok, n(1, 1))
                for t in range(ST):
                    bank = (S[2], S[0])[t // 4]
                    for k in range(KD):
                        last = pe.matmul(bank[:, t % 4 // 2, (t % 2) * D:(t % 2 + 1) * D], cT[:, k, t * P:(t + 1) * P],
                                         w_o[:, k, :], start=(k == 0), stop=(k == KD - 1))
                    if t % 4 == 3:
                        last.then_inc(wo_mm, 1)
                wait(pe, ln_ok, n(NLN, 4))
                for f in range(KD):
                    transposes(S[f], lambda t: xb[:, t, f * P:(f + 1) * P], tx)
                wait(pe, xTv_ok, n(2, 2))
                wait(pe, xTa_ok, n(2, 2))

                def hidden(w):
                    g, c = divmod(w, NF)
                    if w >= 3:
                        wait(pe, hm_ok, n(16, w - 2))
                    for e, wt in enumerate((w_fg, w_fu)):
                        for k in range(KD):
                            last = pe.matmul(S[w % 3][:, e, :], wt[:, k, c * P:(c + 1) * P],
                                             xbT[:, k, g * 512:(g + 1) * 512], start=(k == 0), stop=(k == KD - 1))
                    last.then_inc(ff_mm, 1)

                def down(g):
                    wait(pe, hs_ok, n(4, 2 * g + 2))
                    wait(pe, f2_ok, n(4, 2 * g))
                    wait(pe, cn_ok, n(8, 8))
                    for t in range(GT):
                        for k in range(NF):
                            last = pe.matmul((C, M)[t // 2][:, (t % 2) * D:(t % 2 + 1) * D], hs[:, k, t * P:(t + 1) * P],
                                             w_fd[:, k, :], start=(k == 0), stop=(k == NF - 1))
                        if t % 2:
                            last.then_inc(fd_mm, 1)

                for w in range(16):
                    if w == 11:
                        down(0)
                    hidden(w)
                down(1)


def build(nc, io):
    io["rows"] = nc.dram_tensor("rows", (TOK + P, ROW), F32, kind="Internal").ap()
    io["rows_t"] = io["rows"][0:TOK, :].rearrange("(t p) c -> p t c", p=P)
    with ExitStack() as ctx:
        kit = Kit(nc, ctx)
        keep = {"x_sb": kit.sb("x_sb", [P, NT, D]), "ident": kit.sb("ident", [P, P])}
        with ExitStack() as first:
            kit = Kit(nc, first)
            keep["xT"] = kit.sb("xT", [P, KD, TOK])
            keep["logits"] = kit.sb("logits", [P, NT, E])
            conv_mlp_phase(nc, io, keep)
            experts_phase(nc, io, keep)
        attention_ffn_phase(nc, io, keep)


def kernel(**inputs):
    import ml_dtypes
    from concourse import bacc
    from concourse.bass_utils import run_bass_kernel_spmd

    BF = ml_dtypes.bfloat16

    def chunks(a):
        return np.ascontiguousarray(a.reshape(-1, P, a.shape[-1]).transpose(1, 0, 2))

    def quads(a):
        return np.ascontiguousarray(a.reshape(2, P, 4, -1).transpose(0, 2, 1, 3).reshape(DF, -1))

    def at_heads(row):
        a = np.zeros((P, len(row)), np.float32)
        a[::HP] = row
        return a

    frequency = np.float32(1.0) / np.float32(10000.0) ** (np.arange(0, HD, 2, dtype=np.float32) / np.float32(HD))
    position = (np.arange(P)[:, None] + P * np.arange(ST)[None, :]).astype(np.float32)
    angle = position[:, :, None] * frequency[None, None, :]

    g = {k: np.asarray(v) for k, v in inputs.items()}
    arrays = {
        "x": np.pad(chunks(g["L0_attn_x"].reshape(TOK, D)), ((0, 0), (0, GT), (0, 0))),
        "ident": np.eye(P, dtype=np.float32),
        "w_in": chunks(g["L0_attn_W_in"].T),
        "conv_w": chunks(g["L0_attn_conv_w"].reshape(DI, TAPS)),
        "conv_b": np.ascontiguousarray(g["L0_attn_conv_b"].reshape(NC_, P).T),
        "w_out": chunks(g["L0_attn_W_out"].T),
        "w_up": chunks(g["L0_attn_W_mlp1"].T),
        "w_dn": chunks(g["L0_attn_W_mlp2"].T),
        "gate_w": chunks(g["L0_ffn_gate_w"].T),
        "we_gu": np.ascontiguousarray(g["L0_ffn_w_gate_up"].reshape(E, KD, P, -1).transpose(2, 0, 1, 3)),
        "we_dn": np.ascontiguousarray(g["L0_ffn_w_down"].reshape(E, NIX, IX, D).transpose(2, 0, 1, 3)),
        "ws_gu": chunks(g["L0_ffn_ws_gate_up"]),
        "ws_dn": np.ascontiguousarray(g["L0_ffn_ws_down"].reshape(NSX, IX, D).transpose(1, 0, 2)),
        "upper": np.triu(np.ones((P, P))).astype(BF),
        "ones": np.ones((P, P), BF),
        "ones_f": np.ones((P, 1), np.float32),
        "place": (np.arange(P)[:, None] // E + CG * np.arange(CJ)[None, :]).astype(np.float32),
        "mine": (np.arange(P)[:, None] % E == np.arange(E)[None, :]).astype(np.float32),
        "lane": np.tile(np.arange(P, dtype=np.float32), (P, 1)),
        "base": np.tile(P * np.arange(NT, dtype=np.float32), (P, 1)),
        "zeros": np.zeros((P, ROW), np.float32),
        "w_qkv": chunks(np.concatenate([g[f"L1_attn_w_{c}"].T.reshape(D, NHG, HG * HD) for c in "qkv"],
                                       axis=2).reshape(D, -1)).reshape(P, KD, NHG, -1),
        "w_o": chunks(g["L1_attn_w_o"].T),
        "w_fg": chunks(quads(g["L1_ffn_w_gate"].T).T),
        "w_fu": chunks(quads(g["L1_ffn_w_up"].T).T),
        "w_fd": chunks(quads(g["L1_ffn_w_down"])),
        "cos": np.ascontiguousarray(np.cos(angle).astype(np.float32)),
        "sin": np.ascontiguousarray(np.sin(angle).astype(np.float32)),
        "first_half": at_heads(np.arange(P) < BLK),
        "last_half": at_heads(np.arange(P) >= BLK),
        "masked": at_heads(np.ones(BLK)) * np.float32(MASKED),
    }
    nc = bacc.Bacc("TRN2", target_bir_lowering=False, num_devices=1)
    io = {n: nc.dram_tensor(n, a.shape, mybir.dt.from_np(a.dtype), kind="ExternalInput").ap()
          for n, a in arrays.items()}
    io["out"] = nc.dram_tensor("out", (P, NT, D), F32, kind="ExternalOutput").ap()
    build(nc, io)
    r = run_bass_kernel_spmd(nc, [arrays], core_ids=[0])
    out = np.asarray(r.results[0]["out"])
    return out.transpose(1, 0, 2).reshape(4, 1024, D)
```

```python
from contextlib import ExitStack

import numpy as np

import concourse.bass as bass
from concourse import mybir

F32 = mybir.dt.float32
BF16 = mybir.dt.bfloat16
I32 = mybir.dt.int32
U32 = mybir.dt.uint32
ALU = mybir.AluOpType
ACT = mybir.ActivationFunctionType
AX = mybir.AxisListType

P = 128
D = 256
KD = D // P
NT = 32
TOK = NT * P
GT = 4
GTOK = GT * P
NG = NT // GT
DI = 512
NCI = DI // P
TAPS = 4
N_CONST = 8
DF = 1024
NF = DF // P
E = 32
ROW = D + E


class Step:

    def __init__(self, reg, mul, off):
        self.reg, self.mul, self.off = reg, mul, off

    def __call__(self, per, plus=0):
        fixed = self.off * per + plus
        return fixed if self.reg is None else self.reg * (self.mul * per) + fixed

    def before(self, k):
        return Step(self.reg, self.mul, self.off - k)

    def among(self, low, high):
        return self.reg is not None or low <= self.off < high


def wait(eng, sem, value):
    if not isinstance(value, int) or value > 0:
        eng.wait_ge(sem, value)


def steps(eng, first, last):
    pairs = (NG - first) // 2
    for n in range(first):
        yield Step(None, 0, n), n % 2
    with eng.Fori(0, pairs) as m:
        for k in range(2):
            yield Step(m, 2, first + k), (first + k) % 2
    for n in range(first + 2 * pairs, last):
        yield Step(None, 0, n), n % 2


def tiles(n, count=GT):
    return bass.ds(n(GT), count)


class Kit:

    def __init__(self, nc, ctx):
        self.nc, self.ctx = nc, ctx

    def sb(self, name, shape, dt=F32):
        return self.ctx.enter_context(self.nc.sbuf_tensor(name + "_sb", list(shape), dt))

    def ps(self, name, shape, dt=F32):
        return self.ctx.enter_context(self.nc.psum_tensor(name + "_ps", list(shape), dt))

    def sems(self, names):
        return [self.ctx.enter_context(self.nc.semaphore(n)) for n in names.split()]


def conv_mlp_phase(nc, io, keep):
    with ExitStack() as ctx:
        kit = Kit(nc, ctx)
        sb, ps = kit.sb, kit.ps
        x_sb, xT, ident, logits = keep["x_sb"], keep["xT"], keep["ident"], keep["logits"]

        w_in = sb("w_in", [P, KD, 2 * DI])
        w_out = sb("w_out", [P, NCI, D])
        w_up = sb("w_up", [P, KD, DF])
        w_dn = sb("w_dn", [P, NF, D])
        w_gate = sb("w_gate", [P, KD, E])
        conv_w = sb("conv_w", [P, NCI, TAPS])
        conv_b = sb("conv_b", [P, NCI])
        power = sb("power", [P, GT])
        eps = sb("eps", [P, GT])
        h = sb("h", [P, GT, D])
        hT = sb("hT", [P, KD, GTOK])
        xp = [sb(f"xp{i}", [P, NCI, TAPS - 1 + GTOK]) for i in range(2)]
        xc = sb("xc", [P, NCI, GTOK])
        sz = sb("sz", [P, NCI, GTOK])
        yT = sb("yT", [P, NCI, GTOK])
        x1 = sb("x1", [P, GT, D])
        h1 = sb("h1", [P, GT, D])
        h1T = sb("h1T", [P, KD, GTOK])
        m1T = sb("m1T", [P, NF, GTOK])
        sq = sb("sq", [P, GT, D], BF16)
        ss1 = sb("ss1", [P, GT])
        ss2 = sb("ss2", [P, GT])
        g1 = sb("g1", [P, GT])
        g2 = sb("g2", [P, GT])
        rn1 = sb("rn1", [P, GT])
        rn2 = sb("rn2", [P, GT])
        bn = sb("bn", [P, GT, 6])
        mv = sb("mv", [P, GT, 2])
        x_in = [sb(f"x_in{i}", [P, GT, D]) for i in range(2)]
        xx = sb("xx", [P, GT, D])
        x2 = sb("x2", [P, GT, D])
        xa = sb("xa", [P, GT, D])
        xaT = sb("xaT", [P, KD, GTOK])
        ve = sb("ve", [P, GT])
        rs = sb("rs", [P, GT])

        tp = ps("tp", [P, KD, GTOK])
        mm = [ps(f"mm{i}", [P, GTOK]) for i in range(4)]
        ro = [ps(f"ro{i}", [P, 2, D]) for i in range(2)]

        (consts, xl0, xl1, ss1_ok, g1_ok, rn1_ok, h_ok, tr1, hT_ok, in_mm, xp_ok, sz_ok, tap, conv_ok,
         xc_ok, y_ok, out_mm, x1_ok, ss2_ok, g2_ok, rn2_ok, h1_ok, xx_ok, tr2, h1T_ok, up_mm, m1a_ok,
         m1v_ok, dn_mm, x2_ok, bn_ok, mv_ok, ve_ok, rs_ok, xa_ok, tr3, xaT_ok, xT_ok, xs_ok, lg_mm, lg_ok, row_st,
         setup, passed_pool, passed_dve) = kit.sems(
            "consts x_loaded_even x_loaded_odd ss1_ready g1_ready rn1_ready h_ready tr1_done hT_ready in_done "
            "xp_ready sz_ready tap_done conv_ready xc_ready y_ready out_done x1_ready ss2_ready g2_ready "
            "rn2_ready h1_ready xx_ready tr2_done h1T_ready up_done m1_even_ready m1_odd_ready down_done "
            "x2_ready bn_ready mv_ready ve_ready rs_ready xa_ready tr3_done xaT_ready xT_kept x_kept logit_done logit_ready "
            "row_stored setup_done "
            "passed_pool passed_dve")
        x_loaded = [xl0, xl1]
        ALL = NG + 2
        block = ctx.enter_context(nc.Block())

        @block.sync
        def _(sp):
            def load(n, par):
                sp.dma_start(x_in[par][:, :, :], io["x"][:, tiles(n), :]).then_inc(x_loaded[par], 16)

            load(Step(None, 0, 0), 0)
            sp.dma_start(keep["ident"][:], io["ident"]).then_inc(consts, 16)
            for src, dst in (("w_in", w_in), ("conv_w", conv_w), ("conv_b", conv_b), ("w_out", w_out),
                             ("w_up", w_up), ("w_dn", w_dn), ("gate_w", w_gate)):
                sp.dma_start(dst[:], io[src]).then_inc(consts, 16)
            for n, par in steps(sp, 2, ALL):
                if n.among(0, NG):
                    wait(sp, xx_ok, n(1))
                    load(n.before(-1), 1 - par)
                if n.among(1, NG + 1):
                    b = n.before(1)
                    wait(sp, xa_ok, b(1, 1))
                    sp.dma_start(io["rows_t"][:, tiles(b), 0:D], xa[:, :, :]).then_inc(row_st, 16)
            sp.wait_ge(row_st, 16 * NG)

        @block.gpsimd
        def _(pool):
            pool.memset(power[:], -0.5).then_inc(setup, 1)
            pool.memset(eps[:], 1e-5).then_inc(setup, 1)
            pool.memset(xp[0][:, :, 0:TAPS - 1], 0.0).then_inc(setup, 1)
            pool.wait_ge(setup, 3)

            def rms(n, ss_ok, ss, g, g_ok, rn, rn_ok, used):
                wait(pool, ss_ok, n(GT, GT))
                wait(pool, rn_ok, n(1))
                pool.sem_inc(passed_pool, 1)
                pool.tensor_scalar(g[:], ss[:], 1e-24, None, ALU.max).then_inc(g_ok, 1)
                wait(pool, g_ok, n(1, 1))
                wait(pool, used, n(1))
                pool.tensor_tensor(rn[:], g[:], power[:], ALU.pow).then_inc(rn_ok, 1)

            rms(Step(None, 0, 0), ss1_ok, ss1, g1, g1_ok, rn1, rn1_ok, h_ok)
            for n, par in steps(pool, 2, ALL):
                if n.among(0, NG):
                    rms(n.before(-1), ss1_ok, ss1, g1, g1_ok, rn1, rn1_ok, h_ok)
                if n.among(0, NG):
                    for c in range(NCI):
                        if c == 0:
                            wait(pool, out_mm, n(2))
                        wait(pool, sz_ok, n(NCI, c + 1))
                        wait(pool, xc_ok, n(NCI, c + 1))
                        pool.tensor_tensor(yT[:, c, :], xc[:, c, :], sz[:, c, :], ALU.mult).then_inc(y_ok, 1)
                if n.among(2, ALL):
                    c = n.before(2)
                    wait(pool, xaT_ok, c(1, 1))
                    pool.tensor_copy(xT[:, :, bass.ds(c(GTOK), GTOK)], xaT[:, :, :]).then_inc(xT_ok, 1)
                if n.among(0, NG):
                    rms(n, ss2_ok, ss2, g2, g2_ok, rn2, rn2_ok, h1_ok)
                if n.among(1, NG + 1):
                    b = n.before(1)
                    wait(pool, mv_ok, b(GT, GT))
                    wait(pool, rs_ok, b(1))
                    pool.tensor_tensor(ve[:], mv[:, :, 1], eps[:], ALU.add).then_inc(ve_ok, 1)
                    wait(pool, ve_ok, b(1, 1))
                    wait(pool, xa_ok, b(1))
                    pool.tensor_tensor(rs[:], ve[:], power[:], ALU.pow).then_inc(rs_ok, 1)
                if n.among(0, NG):
                    wait(pool, x1_ok, n(2, 2))
                    wait(pool, x2_ok, n(2))
                    pool.tensor_tensor(xx[:, :, :], x_in[par][:, :, :], x1[:, :, :], ALU.add).then_inc(xx_ok, 1)
                if n.among(1, NG + 1):
                    b = n.before(1)
                    wait(pool, xa_ok, b(1, 1))
                    pool.tensor_copy(x_sb[:, tiles(b), :], xa[:, :, :]).then_inc(xs_ok, 1)
            pool.wait_ge(xs_ok, NG)
            pool.wait_ge(xT_ok, NG)

        @block.scalar
        def _(act):
            def squares(src, ss, ss_ok):
                for t in range(GT):
                    act.activation(sq[:, t, :], src[:, t, :], ACT.Square, accum_out=ss[:, t:t + 1]).then_inc(ss_ok, 1)

            act.wait_ge(x_loaded[0], 16)
            squares(x_in[0], ss1, ss1_ok)
            for n, par in steps(act, 2, ALL):
                if n.among(0, NG):
                    loads = n.before(-1)
                    if n.reg is None:
                        act.wait_ge(x_loaded[1 - par], 16 * (loads.off // 2 + 1))
                    else:
                        act.wait_ge(x_loaded[1 - par], n.reg * 16 + 16 * (loads.off // 2 + 1))
                    wait(act, g1_ok, n(1, 1))
                    squares(x_in[1 - par], ss1, ss1_ok)
                if n.among(0, NG):
                    for c in range(NCI):
                        wait(act, in_mm, n(2 * NCI, c + 1))
                        wait(act, conv_ok, n(NCI, c - NCI + 1))
                        last = act.activation(xp[par][:, c, TAPS - 1:], mm[c][:], ACT.Copy)
                        if par == 0:
                            last = act.activation(xp[1][:, c, 0:TAPS - 1], mm[c][:, GTOK - TAPS + 1:], ACT.Copy)
                        last.then_inc(xp_ok, 1)
                    for c in range(NCI):
                        wait(act, in_mm, n(2 * NCI, NCI + c + 1))
                        wait(act, y_ok, n(NCI, c - NCI + 1))
                        act.activation(sz[:, c, :], mm[c][:], ACT.Silu).then_inc(sz_ok, 1)
                if n.among(2, ALL):
                    c = n.before(2)
                    wait(act, tr3, c(1, 1))
                    wait(act, xT_ok, c(1))
                    wait(act, lg_mm, c(1))
                    act.activation(xaT[:, :, :], tp[:, :, :], ACT.Copy).then_inc(xaT_ok, 1)
                if n.among(0, NG):
                    for c in range(NCI):
                        wait(act, conv_ok, n(NCI, c + 1))
                        act.activation(xc[:, c, :], xc[:, c, :], ACT.Silu).then_inc(xc_ok, 1)
                if n.among(1, NG + 1):
                    b = n.before(1)
                    for f in range(0, NF, 2):
                        wait(act, up_mm, b(NF, f + 1))
                        if f == 0:
                            wait(act, dn_mm, b(2))
                        act.activation(m1T[:, f, :], mm[f % 4][:], ACT.Relu).then_inc(m1a_ok, 1)
                if n.among(0, NG):
                    wait(act, x1_ok, n(2, 2))
                    wait(act, g2_ok, n(1))
                    squares(x1, ss2, ss2_ok)

        @block.vector
        def _(dve):
            def scaled(n, src, rn, rn_ok, dst, used, ok):
                wait(dve, rn_ok, n(1, 1))
                wait(dve, used, n(1))
                for t in range(GT):
                    last = dve.tensor_scalar(dst[:, t, :], src[:, t, :], rn[:, t:t + 1], D ** 0.5, ALU.mult, ALU.mult)
                last.then_inc(ok, 1)

            dve.wait_ge(x_loaded[0], 16)
            scaled(Step(None, 0, 0), x_in[0], rn1, rn1_ok, h, tr1, h_ok)
            dve.wait_ge(consts, N_CONST * 16)
            dve.wait_ge(setup, 3)
            for n, par in steps(dve, 2, ALL):
                if n.among(0, NG):
                    wait(dve, tr1, n(1, 1))
                    wait(dve, in_mm, n(2 * NCI))
                    dve.tensor_copy(hT[:, :, :], tp[:, :, :]).then_inc(hT_ok, 1)
                    for c in range(NCI):
                        wait(dve, xp_ok, n(NCI, c + 1))
                        wait(dve, y_ok, n(NCI, c - NCI + 1))
                        dve.tensor_scalar(xc[:, c, :], xp[par][:, c, TAPS - 1:], conv_w[:, c, TAPS - 1:],
                                          conv_b[:, c:c + 1], ALU.mult, ALU.add).then_inc(tap, 1)
                        for k in range(TAPS - 1):
                            wait(dve, tap, n(NCI * (TAPS - 1), c * (TAPS - 1) + k + 1))
                            dve.scalar_tensor_tensor(xc[:, c, :], xp[par][:, c, k:k + GTOK], conv_w[:, c, k:k + 1],
                                                     xc[:, c, :], ALU.mult, ALU.add)\
                               .then_inc(conv_ok if k == TAPS - 2 else tap, 1)
                if n.among(0, NG):
                    if n.reg is None:
                        dve.wait_ge(x_loaded[1 - par], 16 * ((n.off + 1) // 2 + 1))
                    else:
                        dve.wait_ge(x_loaded[1 - par], n.reg * 16 + 16 * ((n.off + 1) // 2 + 1))
                    scaled(n.before(-1), x_in[1 - par], rn1, rn1_ok, h, tr1, h_ok)
                if n.among(1, NG + 1):
                    b = n.before(1)
                    wait(dve, tr2, b(1, 1))
                    wait(dve, up_mm, b(NF))
                    dve.tensor_copy(h1T[:, :, :], tp[:, :, :]).then_inc(h1T_ok, 1)
                if n.among(2, ALL):
                    c = n.before(2)
                    wait(dve, lg_mm, c(1, 1))
                    dve.tensor_copy(logits[:, tiles(c), :],
                                    ro[0][:, 0, 0:GT * E].rearrange("p (t e) -> p t e", t=GT)).then_inc(lg_ok, 1)
                if n.among(1, NG + 1):
                    b = n.before(1)
                    for f in range(1, NF, 2):
                        wait(dve, up_mm, b(NF, f + 1))
                        if f == 1:
                            wait(dve, dn_mm, b(2))
                        dve.tensor_scalar(m1T[:, f, :], mm[f % 4][:], 0.0, None, ALU.max).then_inc(m1v_ok, 1)
                if n.among(0, NG):
                    wait(dve, xx_ok, n(1))
                    for j in range(2):
                        wait(dve, out_mm, n(2, j + 1))
                        dve.tensor_tensor(x1[:, 2 * j:2 * j + 2, :], ro[j][:, :, :],
                                          x_in[par][:, 2 * j:2 * j + 2, :], ALU.add).then_inc(x1_ok, 1)
                    wait(dve, x1_ok, n(2, 2))
                    scaled(n, x1, rn2, rn2_ok, h1, tr2, h1_ok)
                if n.among(1, NG + 1):
                    b = n.before(1)
                    wait(dve, xx_ok, b(1, 1))
                    wait(dve, xa_ok, b(1))
                    for j in range(2):
                        wait(dve, dn_mm, b(2, j + 1))
                        dve.tensor_tensor(x2[:, 2 * j:2 * j + 2, :], ro[j][:, :, :], xx[:, 2 * j:2 * j + 2, :],
                                          ALU.add).then_inc(x2_ok, 1)
                    for t in range(GT):
                        wait(dve, x2_ok, b(2, t // 2 + 1))
                        dve.bn_stats(bn[:, t, :], x2[:, t, :]).then_inc(bn_ok, 1)
                    wait(dve, bn_ok, b(GT, GT))
                    dve.sem_inc(passed_dve, 1)
                    for t in range(GT):
                        dve.bn_aggr(mv[:, t, :], bn[:, t, :]).then_inc(mv_ok, 1)
                    wait(dve, mv_ok, b(GT, GT))
                    wait(dve, rs_ok, b(1, 1))
                    wait(dve, row_st, b(16))
                    wait(dve, xs_ok, b(1))
                    wait(dve, tr3, b(1))
                    for t in range(GT):
                        last = dve.tensor_scalar(xa[:, t, :], x2[:, t, :], mv[:, t, 0:1], rs[:, t:t + 1],
                                                 ALU.subtract, ALU.mult)
                    last.then_inc(xa_ok, 1)

        @block.tensor
        def _(pe):
            def transposes(src, done):
                for f in range(KD):
                    for t in range(GT):
                        last = pe.transpose(tp[:, f, t * P:(t + 1) * P], src[:, t, f * P:(f + 1) * P], ident[:])
                last.then_inc(done, 1)

            def chunk(c, w, rhsT, done):
                for k in range(KD):
                    last = pe.matmul(mm[c % 4][:], w[:, k, c * P:(c + 1) * P], rhsT[:, k, :],
                                     start=(k == 0), stop=(k == KD - 1))
                last.then_inc(done, 1)

            def rows(lhsT, w, chunks, done):
                for t in range(GT):
                    for k in range(chunks):
                        last = pe.matmul(ro[t // 2][:, t % 2, :], lhsT[:, k, t * P:(t + 1) * P], w[:, k, :],
                                         start=(k == 0), stop=(k == chunks - 1))
                    if t % 2:
                        last.then_inc(done, 1)

            pe.wait_ge(consts, N_CONST * 16)
            for n, par in steps(pe, 2, ALL):
                a, b, c3 = n, n.before(1), n.before(2)
                has_a, has_b, has_c = n.among(0, NG), n.among(1, NG + 1), n.among(2, ALL)
                if has_a:
                    wait(pe, h_ok, a(1, 1))
                    wait(pe, h1T_ok, a(1, -1))
                    transposes(h, tr1)
                    wait(pe, hT_ok, a(1, 1))
                    for c in range(2 * NCI):
                        if c < 4:
                            wait(pe, sz_ok, a(NCI, c - NCI + 1))
                            if c == 0:
                                wait(pe, m1a_ok, a(NF // 2, -NF // 2))
                                wait(pe, m1v_ok, a(NF // 2, -NF // 2))
                        else:
                            wait(pe, xp_ok, a(NCI, c - 4 + 1))
                        chunk(c, w_in, hT, in_mm)
                if has_c:
                    wait(pe, xa_ok, c3(1, 1))
                    wait(pe, hT_ok, a(1, 1)) if has_a else wait(pe, h1T_ok, c3(1, 1))
                    transposes(xa, tr3)
                if has_b:
                    wait(pe, h1_ok, b(1, 1))
                    if has_a:
                        wait(pe, hT_ok, a(1, 1))
                    if has_c:
                        wait(pe, xaT_ok, c3(1, 1))
                    transposes(h1, tr2)
                if has_c:
                    wait(pe, xaT_ok, c3(1, 1))
                    wait(pe, x2_ok, c3(2, 2))
                    for t in range(GT):
                        for k in range(KD):
                            last = pe.matmul(ro[0][:, 0, t * E:(t + 1) * E], xaT[:, k, t * P:(t + 1) * P],
                                             w_gate[:, k, :], start=(k == 0), stop=(k == KD - 1))
                    last.then_inc(lg_mm, 1)
                if has_b:
                    wait(pe, h1T_ok, b(1, 1))
                    for c in range(NF):
                        if c < 4:
                            if has_a:
                                wait(pe, sz_ok, a(NCI, c + 1))
                            elif c == 0:
                                wait(pe, m1a_ok, b(NF // 2))
                                wait(pe, m1v_ok, b(NF // 2))
                        else:
                            wait(pe, (m1a_ok, m1v_ok)[c % 2], b(NF // 2, (c - 4) // 2 + 1))
                        chunk(c, w_up, h1T, up_mm)
                if has_a:
                    wait(pe, y_ok, a(NCI, NCI))
                    wait(pe, x2_ok, a(2, -2))
                    if has_c:
                        wait(pe, lg_ok, c3(1, 1))
                    rows(yT, w_out, NCI, out_mm)
                if has_b:
                    wait(pe, m1a_ok, b(NF // 2, NF // 2))
                    wait(pe, m1v_ok, b(NF // 2, NF // 2))
                    if has_a:
                        wait(pe, x1_ok, a(2, 2))
                    if has_c:
                        wait(pe, lg_ok, c3(1, 1))
                    rows(m1T, w_dn, NF, dn_mm)



CAP = 48
TOPK = 6
TOPG = 3
EG = 8
IX = 88
NIX = 2
NSX = 4
CG = 4
CJ = CAP // CG
RING = 8
SCALE_MOE = 16.0
LOW = -3.0e38
TAKEN = 3.0e38


def experts_phase(nc, io, keep):
    with ExitStack() as ctx:
        kit = Kit(nc, ctx)
        sb, ps = kit.sb, kit.ps
        x_sb, ident, logits = keep["x_sb"], keep["ident"], keep["logits"]
        inner = ctx.enter_context(ExitStack())

        ws_gu = sb("ws_gu", [P, KD, 2 * NSX * IX])
        ws_dn = sb("ws_dn", [IX, NSX, D])
        we_gu = sb("we_gu", [P, RING, KD, 2 * NIX * IX])
        we_dn = sb("we_dn", [IX, RING, NIX, D])
        upper = sb("upper", [P, P], BF16)
        ones = sb("ones", [P, P], BF16)
        ones_f = sb("ones_f", [P, 1])
        place = sb("place", [P, CJ])
        mine = sb("mine", [P, E])
        lane = sb("lane", [P, P])
        sg = sb("sg", [IX, NSX, GTOK])
        su = sb("su", [IX, NSX, GTOK])
        so = sb("so", [P, GT, D])
        sel = sb("sel", [P, NT, E])
        selr = sb("selr", [P, NT, CG, E], BF16)
        pre = [sb(f"pre{i}", [P, NT // 2 + NT, E], BF16) for i in range(2)]
        prer = sb("prer", [P, NT, CG, E], BF16)
        cum = sb("cum", [P, TOK], BF16)
        eg = sb("eg", [IX, 2, NIX, CAP])
        ea = sb("ea", [IX, 2, NIX, CAP])
        cnt = sb("cnt", [P, CJ])
        idx = sb("idx", [P, CJ], U32)
        w_slot = sb("w_slot", [P, CJ])
        wtmp = sb("wtmp", [P, CJ, E])
        rel = sb("rel", [P, NT, CJ])
        base = sb("base", [P, NT])
        busy_f = sb("busy_f", [P, NT])
        busy = sb("busy", [1, NT], I32)
        rden = sb("rden", [P, NT])
        rsum = sb("rsum", [P, NT])
        arena = sb("arena", [P, 7168])
        at = [0]

        def view(*shape):
            n = int(np.prod(shape))
            v = arena[:, at[0]:at[0] + n]
            at[0] += n
            names = "abc"[:len(shape)]
            return v.rearrange(f"p ({' '.join(names)}) -> p {' '.join(names)}", **dict(zip(names, shape)))

        gm, gr = view(NT, 2 * EG), view(NT, 2 * EG)
        kept = view(NT, EG)
        sc, sr = view(NT, E + 8), view(NT, E + 8)
        ex, wt = view(NT, E), view(NT, E)
        t8, t8b = sb("t8", [P, NT, 8]), sb("t8b", [P, NT, 8])
        at[0] = 0
        xg = view(CJ, ROW)
        y = view(CJ, D)
        dump = arena[:, 0:TOK // 2].bitcast(BF16)
        xgT = keep["xT"][:, 0, 0:KD * E * CAP].rearrange("p (k e c) -> p k e c", k=KD, e=E)
        yT = keep["xT"][:, 1, 0:KD * E * CAP].rearrange("p (k c e) -> p k c e", k=KD, e=E)
        xT = keep["xT"]

        mm = [ps(f"em{i}", [P, GTOK]) for i in range(4)]
        ro = [ps(f"er{i}", [P, 2, D]) for i in range(2)]
        tp = [ps(f"et{i}", [P, GTOK]) for i in range(2)]

        (consts, gu_mm, sg_ok, su_ok, sa_ok, dn_mm, so_ok, r_ok, rt, mset, sub_ok, exp_ok, pre_ok, cum_mm,
         cum_ok, cnt_ok, idx_ok, w_st, gath, busy_mm, busy_ok, tr_ok, xg_ok, egu_mm, eg_ok, ea_ok, edn_mm, ey_ok,
         ty_ok, y_ok, ws_ok, oh_ok, cb_mm, cb_ok, rel_ok) = kit.sems(
            "consts2 shared_gu_done shared_gate_ready shared_up_ready shared_act_ready shared_down_done "
            "shared_out_ready shared_added route_step softmax_step centered exp_ready prefix_ready cum_done cum_ready "
            "count_done slot_token_ready weights_stored gathered busy_done busy_ready slots_transposed "
            "slot_features_ready expert_gu_done expert_gate_ready expert_act_ready expert_down_done "
            "expert_out_ready out_transposed slot_out_ready slot_weight_ready onehot_ready combine_done "
            "combined relative_ready")
        ring = kit.sems(" ".join(f"expert_weights_{i}" for i in range(RING)))
        N2 = 10
        HALF = 5

        def shared(eng, lo, hi):
            with eng.Fori(0, hi - lo) as r:
                yield Step(r, 1, lo)

        block = inner.enter_context(nc.Block())

        @block.sync
        def _(sp):
            for src, dst in (("ws_gu", ws_gu), ("ws_dn", ws_dn), ("upper", upper), ("ones", ones), ("ones_f", ones_f),
                             ("place", place), ("mine", mine), ("lane", lane), ("base", base)):
                sp.dma_start(dst[:], io[src]).then_inc(consts, 16)
            sp.dma_start(io["rows"][TOK:TOK + P, :], io["zeros"]).then_inc(consts, 16)

            def weights(i, e):
                sp.dma_start(we_gu[:, i, :, :], io["we_gu"][:, bass.ds(e, 1), :, :].rearrange("p e k n -> p (e k) n")).then_inc(ring[i], 16)
                sp.dma_start(we_dn[:, i, :, :], io["we_dn"][:, bass.ds(e, 1), :, :].rearrange("p e k n -> p (e k) n")).then_inc(ring[i], 16)

            for i in range(RING):
                weights(i, i)
            sp.wait_ge(rt, 12)
            sp.dma_start(io["rows_t"][:, :, D:ROW], wt).then_inc(w_st, 16)
            with sp.Fori(0, E // RING - 1) as r:
                for i in range(RING):
                    sp.wait_ge(edn_mm, r * RING + (i + 1))
                    weights(i, r * RING + (RING + i))

        @block.gpsimd
        def _(pool):
            def act(n):
                for i in range(NSX):
                    wait(pool, sg_ok, n(NSX, i + 1))
                    wait(pool, su_ok, n(NSX, i + 1))
                    pool.tensor_tensor(su[:, i, :], sg[:, i, :], su[:, i, :], ALU.mult).then_inc(sa_ok, 1)

            def add(b):
                wait(pool, so_ok, b(2, 2))
                pool.tensor_tensor(x_sb[:, tiles(b), :], x_sb[:, tiles(b), :], so[:, :, :], ALU.add).then_inc(r_ok, 1)

            act(Step(None, 0, 0))
            for n in shared(pool, 1, NG):
                act(n)
                add(n.before(1))
            pool.wait_ge(idx_ok, 1)
            pool.wait_ge(w_st, 16)
            pool.wait_ge(consts, 16 * N2)
            for j in range(CJ):
                pool.indirect_dma_start(out=xg[:, j, :], out_offset=None, in_=io["rows"][:, :],
                                        in_offset=bass.IndirectOffsetOnAxis(ap=idx[:, j:j + 1], axis=0)).then_inc(gath, 16)
            add(Step(None, 0, NG - 1))

        @block.scalar
        def _(act):
            def gate_up(n):
                for i in range(NSX):
                    wait(act, gu_mm, n(2 * NSX, 2 * i + 1))
                    if i == 0:
                        wait(act, sa_ok, n(NSX))
                        wait(act, dn_mm, n(2))
                    act.activation(sg[:, i, :], mm[(2 * i) % 4][0:IX, :], ACT.Silu).then_inc(sg_ok, 1)
                    wait(act, gu_mm, n(2 * NSX, 2 * i + 2))
                    act.activation(su[:, i, :], mm[(2 * i + 1) % 4][0:IX, :], ACT.Copy).then_inc(su_ok, 1)

            def down(b):
                wait(act, r_ok, b(1))
                for j in range(2):
                    wait(act, dn_mm, b(2, j + 1))
                    act.activation(so[:, 2 * j:2 * j + 2, :], ro[j][:, :, :], ACT.Copy).then_inc(so_ok, 1)

            gate_up(Step(None, 0, 0))
            for lo, hi in ((1, HALF), (HALF, NG)):
                for n in shared(act, lo, hi):
                    down(n.before(1))
                    gate_up(n)
                if lo == 1:
                    act.wait_ge(sub_ok, 1)
                    act.activation(ex, ex, ACT.Exp).then_inc(exp_ok, 1)
            down(Step(None, 0, NG - 1))
            with act.Fori(0, E // RING) as r:
                for i in range(RING):
                    act.wait_ge(egu_mm, r * RING + (i + 1))
                    if i >= 2:
                        act.wait_ge(ea_ok, r * RING + (i - 1))
                    else:
                        act.wait_ge(ea_ok, r * RING)
                    act.activation(eg[:, i % 2, :, :],
                                   mm[i % 4][0:IX, 0:NIX * CAP].rearrange("p (a c) -> p a c", a=NIX), ACT.Silu).then_inc(eg_ok, 1)
                    act.wait_ge(edn_mm, r * RING + (i + 1))
                    act.activation(yT[:, :, :, bass.ds(r * RING + i, 1)].rearrange("p k c e -> p k (c e)"),
                                   ro[i % 2][:, 0, 0:KD * CAP].rearrange("p (k c) -> p k c", k=KD), ACT.Copy).then_inc(ey_ok, 1)

        @block.vector
        def _(dve):
            step = [0]

            def then(ins):
                step[0] += 1
                ins.then_inc(rt, 1)
                dve.wait_ge(rt, step[0])

            dve.memset(gm[:, :, EG:], LOW)
            dve.memset(sc[:, :, E:], LOW)
            dve.memset(pre[0][:, 0:NT // 2, :], 0.0)
            dve.memset(pre[1][:, 0:NT // 2, :], 0.0)
            then(dve.tensor_reduce(gm[:, :, 0:EG], logits[:, :, :].rearrange("p t (g m) -> p t g m", g=EG), AX.X, ALU.max))
            for t in range(NT):
                last = dve.max(t8[:, t, :], gm[:, t, 0:EG])
            then(last)
            then(dve.memset(t8[:, :, TOPG:], LOW))
            for t in range(NT):
                last = dve.match_replace(gr[:, t, :], t8[:, t, :], gm[:, t, :], TAKEN)
            then(last)
            then(dve.tensor_scalar(kept, gr[:, :, 0:EG], TAKEN, None, ALU.is_equal))
            then(dve.tensor_tensor(wt.rearrange("p t (g m) -> p (t g) m", g=EG),
                                   logits[:, :, :].rearrange("p t (g m) -> p (t g) m", g=EG),
                                   kept.rearrange("p t g -> p (t g)").unsqueeze(2).to_broadcast([P, NT * EG, E // EG]), ALU.mult))
            then(dve.tensor_scalar(sc[:, :, 0:E], wt, 0.0, None, ALU.add))
            for t in range(NT):
                last = dve.max(t8b[:, t, :], sc[:, t, 0:E])
            then(last)
            dve.tensor_tensor(ex, sc[:, :, 0:E], t8b[:, :, 0:1].to_broadcast([P, NT, E]), ALU.subtract).then_inc(sub_ok, 1)
            then(dve.memset(t8b[:, :, TOPK:], LOW))
            for t in range(NT):
                last = dve.match_replace(sr[:, t, :], t8b[:, t, :], sc[:, t, :], TAKEN)
            then(last)
            then(dve.tensor_scalar(sel[:, :, :], sr[:, :, 0:E], TAKEN, None, ALU.is_equal))
            dve.tensor_copy(selr[:, :, :, :], sel[:, :, :].unsqueeze(2).to_broadcast([P, NT, CG, E])).then_inc(pre_ok, 1)
            dve.tensor_copy(pre[0][:, NT // 2:, :], sel[:, :, :]).then_inc(pre_ok, 1)
            for d in range(5):
                dve.wait_ge(pre_ok, 2 + d)
                a, b = pre[d % 2], pre[(d + 1) % 2]
                dve.tensor_tensor(b[:, NT // 2:, :], a[:, NT // 2:, :],
                                  a[:, NT // 2 - (1 << d):NT // 2 + NT - (1 << d), :], ALU.add).then_inc(pre_ok, 1)
            dve.wait_ge(pre_ok, 7)
            dve.tensor_copy(prer[:, :, :, :],
                            pre[1][:, NT // 2 - 1:NT // 2 - 1 + NT, :].unsqueeze(2).to_broadcast([P, NT, CG, E])).then_inc(pre_ok, 1)
            dve.wait_ge(exp_ok, 1)
            dve.tensor_reduce(rsum[:], ex, AX.X, ALU.add).then_inc(mset, 1)
            dve.wait_ge(mset, 1)
            dve.reciprocal(rden[:], rsum[:]).then_inc(mset, 1)
            dve.wait_ge(mset, 2)
            dve.tensor_tensor(wt, ex, rden[:, :].unsqueeze(2).to_broadcast([P, NT, E]), ALU.mult).then_inc(mset, 1)
            dve.wait_ge(mset, 3)
            then(dve.scalar_tensor_tensor(wt, wt, SCALE_MOE, sel[:, :, :], ALU.mult, ALU.mult))
            assert step[0] == 12
            for g in range(NG):
                dve.wait_ge(cum_mm, g + 1)
                dve.tensor_copy(cum[:, g * GTOK:(g + 1) * GTOK], tp[g % 2][:, :]).then_inc(cum_ok, 1)
            dve.wait_ge(cum_ok, NG)
            dve.wait_ge(consts, 16 * N2)
            dve.memset(busy_f[:, 0:1], 1.0)
            dve.tensor_scalar(busy_f[:, 1:], cum[:, 0:TOK].rearrange("p (t c) -> p t c", c=P)[:, 0:NT - 1, P - 1],
                              float(CAP), None, ALU.is_lt).then_inc(cnt_ok, 1)
            for j in range(CJ):
                dve.wait_ge(cnt_ok, j + 1)
                dve.tensor_scalar(dump, cum[:, :], place[:, j:j + 1], 0.0, ALU.is_le, ALU.add,
                                  accum_out=cnt[:, j:j + 1]).then_inc(cnt_ok, 1)
            dve.wait_ge(cnt_ok, CJ + 1)
            dve.tensor_copy(idx[:, :], cnt[:, :]).then_inc(idx_ok, 1)
            dve.wait_ge(busy_mm, 1)
            dve.tensor_copy(busy[:, :], tp[0][0:1, 0:NT]).then_inc(busy_ok, 1)
            dve.wait_ge(gath, 16 * CJ)
            dve.tensor_tensor(wtmp[:, :, :], xg[:, :, D:ROW], mine[:, :].unsqueeze(1).to_broadcast([P, CJ, E]), ALU.mult).then_inc(ws_ok, 1)
            dve.wait_ge(ws_ok, 1)
            dve.tensor_reduce(w_slot[:, :], wtmp[:, :, :], AX.X, ALU.add).then_inc(ws_ok, 1)
            for j in range(CJ):
                for k in range(KD):
                    m = j * KD + k
                    dve.wait_ge(tr_ok, m + 1)
                    dve.tensor_copy(xgT[:, k, :, j * CG:(j + 1) * CG].rearrange("p e c -> p c e"),
                                    tp[m % 2][:, 0:P].rearrange("p (c e) -> p c e", c=CG)).then_inc(xg_ok, 1)
            with dve.Fori(0, E // RING) as r:
                for i in range(RING):
                    dve.wait_ge(eg_ok, r * RING + (i + 1))
                    dve.wait_ge(edn_mm, r * RING + max(i - 1, 0))
                    dve.tensor_tensor(ea[:, i % 2, :, :], eg[:, i % 2, :, :],
                                      mm[i % 4][0:IX, NIX * CAP:2 * NIX * CAP].rearrange("p (a c) -> p a c", a=NIX),
                                      ALU.mult).then_inc(ea_ok, 1)
            dve.wait_ge(ws_ok, 2)
            for j in range(CJ):
                dve.wait_ge(ty_ok, j + 1)
                dve.tensor_scalar(y[:, j, :], tp[j % 2][:, 0:D], w_slot[:, j:j + 1], None, ALU.mult).then_inc(y_ok, 1)

        @block.tensor
        def _(pe):
            def gate_up(n):
                for c in range(2 * NSX):
                    if c == 0:
                        wait(pe, su_ok, n(NSX))
                    if c >= 4:
                        wait(pe, sg_ok if c % 2 == 0 else su_ok, n(NSX, (c - 4) // 2 + 1))
                    col = (c // 2 + (c % 2) * NSX) * IX
                    for k in range(KD):
                        last = pe.matmul(mm[c % 4][0:IX, :], ws_gu[:, k, col:col + IX],
                                         xT[:, k, bass.ds(n(GTOK), GTOK)], start=(k == 0), stop=(k == KD - 1))
                    last.then_inc(gu_mm, 1)

            def down(b):
                wait(pe, sa_ok, b(NSX, NSX))
                wait(pe, so_ok, b(2))
                for t in range(GT):
                    for k in range(NSX):
                        last = pe.matmul(ro[t // 2][:, t % 2, :], su[:, k, t * P:(t + 1) * P], ws_dn[:, k, :],
                                         start=(k == 0), stop=(k == NSX - 1))
                    if t % 2:
                        last.then_inc(dn_mm, 1)

            pe.wait_ge(consts, 16 * N2)
            gate_up(Step(None, 0, 0))
            for lo, hi in ((1, HALF), (HALF, NG)):
                for n in shared(pe, lo, hi):
                    down(n.before(1))
                    gate_up(n)
                if lo == 1:
                    pe.wait_ge(pre_ok, 8)
                    for t in range(NT):
                        g = t // GT
                        if t % GT == 0 and g >= 2:
                            pe.wait_ge(cum_ok, g - 1)
                        o = tp[g % 2][:, (t % GT) * P:(t % GT + 1) * P]
                        pe.matmul(o, selr[:, t, :, :].rearrange("p c e -> p (c e)"), upper[:], start=True, stop=False)
                        last = pe.matmul(o, prer[:, t, :, :].rearrange("p c e -> p (c e)"), ones[:], start=False, stop=True)
                        if t % GT == GT - 1:
                            last.then_inc(cum_mm, 1)
            down(Step(None, 0, NG - 1))
            pe.wait_ge(cnt_ok, 1)
            pe.wait_ge(cum_ok, NG)
            pe.matmul(tp[0][0:1, 0:NT], ones_f[:, 0:1], busy_f[:, :], start=True, stop=True).then_inc(busy_mm, 1)
            pe.wait_ge(busy_ok, 1)
            pe.wait_ge(gath, 16 * CJ)
            for j in range(CJ):
                for k in range(KD):
                    m = j * KD + k
                    if m >= 2:
                        pe.wait_ge(xg_ok, m - 1)
                    pe.transpose(tp[m % 2][:, 0:P], xg[:, j, k * P:(k + 1) * P], ident[:]).then_inc(tr_ok, 1)
            pe.wait_ge(xg_ok, CJ * KD)
            pe.wait_ge(so_ok, 2 * NG)

            def expert_gu(e, i):
                pe.wait_ge(ring[i], e[1])
                pe.wait_ge(ea_ok, e[2])
                for c in range(2 * NIX):
                    for k in range(KD):
                        last = pe.matmul(mm[i % 4][0:IX, c * CAP:(c + 1) * CAP], we_gu[:, i, k, c * IX:(c + 1) * IX],
                                         xgT[:, k, bass.ds(e[0], 1), :].rearrange("p e c -> p (e c)"),
                                         start=(k == 0), stop=(k == KD - 1))
                last.then_inc(egu_mm, 1)

            def expert_down(count, i):
                pe.wait_ge(ea_ok, count(1))
                pe.wait_ge(ey_ok, count(-1))
                for f in range(KD):
                    for k in range(NIX):
                        last = pe.matmul(ro[i % 2][:, 0, f * CAP:(f + 1) * CAP], we_dn[:, i, k, f * P:(f + 1) * P],
                                         ea[:, i % 2, k, :], start=(k == 0), stop=(k == NIX - 1))
                last.then_inc(edn_mm, 1)

            with pe.Fori(0, E // RING) as r:
                for i in range(RING):
                    expert_gu((r * RING + i, r * 32 + 32, r * RING + max(i - 3, 0)), i)
                    if i >= 1:
                        expert_down(lambda d: r * RING + (i - 1 + d) if i - 1 + d > 0 else r * RING, i - 1)
                expert_down(lambda d: r * RING + (RING - 1 + d), RING - 1)
            pe.wait_ge(ey_ok, E)
            for j in range(CJ):
                if j >= 2:
                    pe.wait_ge(y_ok, j - 1)
                for k in range(KD):
                    last = pe.transpose(tp[j % 2][:, k * P:(k + 1) * P],
                                        yT[:, k, j * CG:(j + 1) * CG, :].rearrange("p c e -> p (c e)"), ident[:])
                last.then_inc(ty_ok, 1)

        inner.close()

        hot = [xT[:, 0, i * CJ * P:(i + 1) * CJ * P].rearrange("p (j c) -> p j c", j=CJ) for i in range(2)]
        block = ctx.enter_context(nc.Block())

        @block.vector
        def _(dve):
            dve.tensor_tensor(rel[:, :, :], cnt[:, :].unsqueeze(1).to_broadcast([P, NT, CJ]),
                              base[:, :].unsqueeze(2).to_broadcast([P, NT, CJ]), ALU.subtract).then_inc(rel_ok, 1)
            dve.wait_ge(rel_ok, 1)
            with dve.Fori(0, NT // 2) as r:
                for i in range(2):
                    t = Step(r, 2, i)
                    some = dve.value_load(busy[0:1, bass.ds(t(1), 1)], min_val=0, max_val=P)
                    with dve.If(some > 0):
                        dve.wait_ge(cb_mm, r * 2)
                        dve.tensor_tensor(hot[i], rel[:, bass.ds(t(1), 1), :].rearrange("p a j -> p (a j)")
                                          .unsqueeze(2).to_broadcast([P, CJ, P]),
                                          lane[:, :].unsqueeze(1).to_broadcast([P, CJ, P]), ALU.is_equal).then_inc(oh_ok, 1)
                        dve.wait_ge(cb_mm, t(1, 1))
                        xt = x_sb[:, bass.ds(t(1), 1), :].rearrange("p a b -> p (a b)")
                        dve.tensor_tensor(xt, ro[i][:, 0, :], xt, ALU.add).then_inc(cb_ok, 1)

        @block.tensor
        def _(pe):
            with pe.Fori(0, NT // 2) as r:
                for i in range(2):
                    t = Step(r, 2, i)
                    some = pe.value_load(busy[0:1, bass.ds(t(1), 1)], min_val=0, max_val=P)
                    with pe.If(some > 0):
                        pe.wait_ge(oh_ok, t(1, 1))
                        pe.wait_ge(cb_ok, r * 2)
                        for j in range(CJ):
                            last = pe.matmul(ro[i][:, 0, :], hot[i][:, j, :], y[:, j, :],
                                             start=(j == 0), stop=(j == CJ - 1))
                        last.then_inc(cb_mm, 1)


NB = 4
ST = NT // NB
SEQ = ST * P
HEADS = 16
HD = D // HEADS
HG = 4
NHG = HEADS // HG
HALF_D = HD // 2
BLK = 64
MASKED = -1.0e30
NLN = 6
LEAD = 2

Q_PARTS = (0, 1, 0, 1, 0, 2)
K_PARTS = (0, 1, 1, 0, 2, 0)
FM = len(Q_PARTS) * HD
FW = FM + 3

BLOCKS = [(j, i) for j in range(ST) for i in range(j, ST)]
UB = 4
NU = len(BLOCKS) // UB


def runs(u):
    out = []
    for n, (j, i) in enumerate(BLOCKS[UB * u:UB * u + UB]):
        if i > j and out and out[-1][1] == j and not out[-1][4]:
            out[-1][3] += 1
        else:
            out.append([n, j, i, 1, i == j])
    return out


class Chain:

    def __init__(self, eng, sem, n, per):
        self.eng, self.sem, self.n, self.per, self.k = eng, sem, n, per, 0

    def then(self, ins):
        self.k += 1
        ins.then_inc(self.sem, 1)
        wait(self.eng, self.sem, self.n(self.per, self.k))

    def end(self):
        assert self.k == self.per, (self.k, self.per)


def head_steps(eng, b, run):
    for k in (-2, -1):
        run(Step(b, HEADS, k), 0, k, 2)
    with eng.Fori(0, NHG - 1) as g:
        for k in range(HG):
            run(Step(b * HEADS + g * HG, 1, k), g, k, 2)
    for k in range(HG):
        run(Step(b, HEADS, (NHG - 1) * HG + k), NHG - 1, k, min(2, HG - 1 - k))


def attention_ffn_phase(nc, io, keep):
    with ExitStack() as ctx:
        kit = Kit(nc, ctx)
        sb, ps = kit.sb, kit.ps
        x_sb, ident = keep["x_sb"], keep["ident"]

        w_qkv = sb("w_qkv", [P, KD, NHG, 3 * HG * HD])
        w_o = sb("w_o", [P, KD, D])
        w_fg = sb("w_fg", [P, KD, DF])
        w_fu = sb("w_fu", [P, KD, DF])
        w_fd = sb("w_fd", [P, NF, D])
        cos = sb("cos", [P, ST, HALF_D])
        sin = sb("sin", [P, ST, HALF_D])
        mask = sb("mask", [P, 2])
        ident_b = sb("ident_b", [P, P], BF16)
        power = sb("power3", [P, GT])
        eps = sb("eps3", [P, GT])
        xb = sb("xb", [P, ST, D])
        xbT = sb("xbT", [P, KD, SEQ])
        v = sb("v", [P, ST, HEADS, HD + 1])
        qks = sb("qks", [P, ST, NHG * 2 * HG, FW], BF16)
        nm = sb("nm", [P, ST])
        o = sb("o", [P, ST, HD + 1])
        rc = sb("rc", [P, ST])
        ctok = sb("ctok", [P, ST, D])
        sgl = sb("sgl", [P, 2, 512])
        nb = sb("nb", [P, 4, 512], BF16)
        ot = sb("ot", [P, GT, D])
        bn = sb("bn3", [P, GT, 6])
        mv = sb("mv3", [P, GT, 2])
        ve = sb("ve3", [P, GT])
        rs = sb("rs3", [P, GT])

        room = sb("room", [P, 10240])
        used = [0]

        def carve(words, dt=F32):
            a = room[:, used[0]:used[0] + words]
            used[0] += words
            assert used[0] <= 10240
            return a if dt == F32 else a.bitcast(dt)

        qk = carve(ST * 2 * HG * HD).rearrange("p (t h d) -> p t h d", t=ST, h=2 * HG)
        ro = carve(ST * 2 * HG * HD).rearrange("p (t h d) -> p t h d", t=ST, h=2 * HG)
        rest = carve(ST * 2 * HG * HD).rearrange("p (t h d) -> p t h d", t=ST, h=2 * HG)
        r1 = [carve(ST * 2 * HG * HALF_D).rearrange("p (t h d) -> p t h d", t=ST, h=2 * HG) for i in range(4)]
        q1T = carve(SEQ // 2, BF16)
        q2T = [carve(SEQ // 2, BF16) for i in range(2)]
        kT = [carve(SEQ // 2, BF16) for i in range(4)]
        pb = [carve(512) for i in range(3)]
        used[0] = 0
        hs = carve(NF * 512).rearrange("p (k c) -> p k c", k=NF)
        hj = carve(4 * 512).rearrange("p (k c) -> p k c", k=4)
        aj = carve(4 * 512).rearrange("p (k c) -> p k c", k=4)
        ge = carve(6 * 256, BF16).rearrange("p (k c) -> p k c", k=6)

        S = [ps(f"s{i}", [P, 2, 512]) for i in range(3)]
        C = ps("c", [P, 512])
        M = ps("m", [P, 512])
        X = S[0:2]
        W = [S[2][:, i, :] for i in range(2)]
        T = C[:, :].bitcast(BF16)
        O = M[:, 0:ST * 32].rearrange("p (t c) -> p t c", t=ST)[:, :, 0:HD + 1]

        (consts, setup, ready, passed, passed_pe, bn_ok, mv_ok, ve_ok, rs_ok, ln_ok, tx, xTv_ok, xTa_ok, qkv_mm, qkv_ok, rope_v,
         rope_p, rv_ok, rp_ok, a_ok, r_ok, b_ok, rest_ok, copies_ok, tk_mm, k_ok, tq_mm, q1_ok, tm_mm, q2_ok, max_mm,
         mx_ok, nm1_ok, nm_ok, sc_mm, exp_ok, pv_mm, o_ok, rc_ok, cn_ok,
         tc, cTv_ok, cTa_ok, wo_mm, xr_ok, ff_mm, sl_ok, hm_ok, ab_ok, sp, hs_ok, fd_mm, f2_ok, out_st) = kit.sems(
            "consts3 setup3 rows_set_up3 passed3 passed3_pe bn3_ready mv3_ready ve3_ready rs3_ready layernorm_done x_transposed "
            "xT_low_ready xT_high_ready qkv_done qkv_ready rope_step_v rope_step_p rope_low_ready rope_high_ready "
            "part1_ready rest_ready part2_ready part3_ready part_copies_ready k_transposed kT_ready q_transposed "
            "qT_ready q_max_transposed qT_max_ready max_scores_done maxima_ready max_part1_ready max_parts_ready "
            "scores_done weights_ready weighted_done sums_copied rowsum_inverted context_ready ctx_transposed "
            "cT_low_ready cT_high_ready wo_done attn_residual_ready ffn_in_done silu_ready hidden_ready abs_ready "
            "sparse_step sparse_ready ffn_down_done ffn_residual_ready out_stored")

        block = ctx.enter_context(nc.Block())

        def x_tile(n, t):
            return x_sb[:, bass.ds(n(ST, t), 1), :].rearrange("p a b -> p (a b)")

        def part(g, s, f):
            heads = bass.ds(g * (2 * HG) + (s or 0) * HG, HG if s is not None else 2 * HG)
            return qks[:, :, heads, f * HD:(f + 1) * HD]

        def rows_of(g, k, s, t):
            at = (g + k // HG) * (2 * HG) + s * HG + k % HG
            return qks[:, t, bass.ds(at, 1), :].rearrange("p a f -> p (a f)")

        @block.sync
        def _(sync):
            for src, dst in (("w_qkv", w_qkv), ("cos", cos), ("sin", sin), ("mask", mask),
                             ("w_o", w_o), ("w_fg", w_fg), ("w_fu", w_fu), ("w_fd", w_fd)):
                sync.dma_start(dst[:], io[src]).then_inc(consts, 16)
            with sync.Fori(0, NB) as b:
                n = Step(b, 1, 0)
                for g in range(2):
                    wait(sync, ln_ok, n(NLN, 5 + g))
                    sync.dma_start(io["out"][:, bass.ds(n(ST, g * GT), GT), :], ot[:, :, :]).then_inc(out_st, 16)
            sync.wait_ge(out_st, 16 * 2 * NB)

        @block.gpsimd
        def _(pool):
            pool.memset(power[:], -0.5)
            pool.memset(eps[:], 1e-5).then_inc(setup, 1)
            pool.memset(v[:, :, :, HD:HD + 1], 1.0).then_inc(setup, 1)
            pool.memset(qks[:, :, :, FM:FM + 2], 1.0).then_inc(setup, 1)
            pool.wait_ge(setup, 3)
            pool.wait_ge(consts, 16 * 8)

            def inverse_deviation(n, k):
                wait(pool, mv_ok, n(NLN, k + 1))
                wait(pool, rs_ok, n(NLN, k))
                pool.tensor_tensor(ve[:], mv[:, :, 1], eps[:], ALU.add).then_inc(ve_ok, 1)
                wait(pool, ve_ok, n(NLN, k + 1))
                wait(pool, ln_ok, n(NLN, k))
                pool.tensor_tensor(rs[:], ve[:], power[:], ALU.pow).then_inc(rs_ok, 1)

            with pool.Fori(0, NB) as b:
                n = Step(b, 1, 0)
                inverse_deviation(n, 0)
                inverse_deviation(n, 1)
                for g in range(NHG):
                    pool.memset(qks[:, :, g * 2 * HG:g * 2 * HG + HG, FM:FM + 2], 0.0)
                with pool.Fori(0, NHG) as g:
                    q = Step(b * NHG + g, 1, 0)
                    x1, x2 = qk[:, :, :, 0:HALF_D], qk[:, :, :, HALF_D:]
                    wait(pool, qkv_ok, q(2, 2))
                    wait(pool, rp_ok, q(1))
                    pool.tensor_tensor(r1[2], x2, cos[:, :, :].unsqueeze(2).to_broadcast([P, ST, 2 * HG, HALF_D]),
                                       ALU.mult).then_inc(rope_p, 1)
                    pool.tensor_tensor(r1[3], x1, sin[:, :, :].unsqueeze(2).to_broadcast([P, ST, 2 * HG, HALF_D]),
                                       ALU.mult).then_inc(rope_p, 1)
                    wait(pool, rope_p, q(2, 2))
                    wait(pool, a_ok, q(1))
                    wait(pool, r_ok, q(1))
                    pool.tensor_tensor(ro[:, :, :, HALF_D:HD], r1[2], r1[3], ALU.add).then_inc(rp_ok, 1)
                    wait(pool, a_ok, q(1, 1))
                    for s, first in ((0, 2), (1, 3)):
                        pool.tensor_copy(part(g, s, first), part(g, s, 0))
                        pool.tensor_copy(part(g, s, first + 2), part(g, s, 0))
                    wait(pool, b_ok, q(1, 1))
                    pool.tensor_copy(part(g, 0, 3), part(g, 0, 1))
                    pool.tensor_copy(part(g, 1, 2), part(g, 1, 1)).then_inc(copies_ok, 1)
                for k in range(2, NLN):
                    inverse_deviation(n, k)

        @block.scalar
        def _(act):
            act.sem_inc(exp_ok, LEAD)
            act.wait_ge(setup, 3)
            act.wait_ge(ready, 1)
            with act.Fori(0, NB) as b:
                n = Step(b, 1, 0)
                wait(act, tx, n(4, 2))
                act.activation(xbT[:, 1, :].rearrange("p (a c) -> p a c", a=2), S[1][:, :, :], ACT.Copy).then_inc(xTa_ok, 1)
                with act.Fori(0, NHG) as g:
                    q = Step(b * NHG + g, 1, 0)
                    for s in range(2):
                        wait(act, qkv_mm, q(2, s + 1))
                        wait(act, rv_ok, q(1))
                        wait(act, rp_ok, q(1))
                        wait(act, fd_mm, n(4))
                        src = S[s][:, :, :].rearrange("p a (t c) -> p (a t) c", t=2)
                        act.activation(qk[:, s * GT:(s + 1) * GT, :, :].rearrange("p t h d -> p t (h d)"),
                                       src[:, :, 0:2 * HG * HD], ACT.Copy)
                        act.activation(v[:, s * GT:(s + 1) * GT, bass.ds(g * HG, HG), 0:HD],
                                       src[:, :, 2 * HG * HD:3 * HG * HD].rearrange("p t (h d) -> p t h d", h=HG),
                                       ACT.Copy).then_inc(qkv_ok, 1)
                    wait(act, rv_ok, q(1, 1))
                    wait(act, rp_ok, q(1, 1))
                    act.activation(part(g, None, 0), ro, ACT.Copy).then_inc(a_ok, 1)
                    wait(act, r_ok, q(1, 1))
                    act.activation(part(g, None, 1), rest, ACT.Copy).then_inc(b_ok, 1)

                def run(h, g, k, ahead):
                    def key_rows():
                        wait(act, tk_mm, h(1, 3))
                        act.activation(kT[(k + 2) % 4][0:FW, :], T[0:FW, :], ACT.Copy).then_inc(k_ok, 1)

                    if k == -2:
                        return key_rows()
                    for u in range(NU):
                        if k >= 0:
                            wait(act, sc_mm, h(NU, u + 1))
                            wait(act, pv_mm, h(NU, LEAD + u - 2))
                            act.activation(pb[u % 3][:, :], W[(k * NU + u) % 2], ACT.Exp,
                                           scale=HD ** -0.5).then_inc(exp_ok, 1)
                        if u == 4 and ahead >= 2:
                            key_rows()
                        if u == 6 and ahead >= 1:
                            wait(act, tm_mm, h(1, 2))
                            act.activation(q2T[(k + 1) % 2][0:FW, :], T[0:FW, :], ACT.Copy).then_inc(q2_ok, 1)

                head_steps(act, b, run)
                wait(act, tc, n(2, 2))
                wait(act, qkv_mm, n(2 * NHG, 2 * NHG))
                act.activation(xbT[:, 1, :].rearrange("p (a c) -> p a c", a=2), S[1][:, :, :], ACT.Copy).then_inc(cTa_ok, 1)
                wait(act, tx, n(4, 4))
                act.activation(xbT[:, 1, :].rearrange("p (a c) -> p a c", a=2), S[1][:, :, :], ACT.Copy).then_inc(xTa_ok, 1)
                for w in range(17):
                    if w < 16:
                        wait(act, ff_mm, n(16, w + 1))
                        wait(act, hm_ok, n(16, max(w - 1, 0)))
                        act.activation(sgl[:, w % 2, :], S[w % 3][:, 0, :], ACT.Silu).then_inc(sl_ok, 1)
                    if w >= 1:
                        wait(act, hm_ok, n(16, w))
                        wait(act, hs_ok, n(4, (w - 1) // 4))
                        act.activation(aj[:, (w - 1) % 4, :], hj[:, (w - 1) % 4, :], ACT.Abs).then_inc(ab_ok, 1)

        @block.vector
        def _(dve):
            dve.sem_inc(mx_ok, LEAD)
            dve.sem_inc(cn_ok, LEAD)
            dve.wait_ge(consts, 16 * 8)
            dve.wait_ge(setup, 3)
            dve.tensor_copy(ident_b[:, :], ident[:, :])
            by_group = qks[:, :, :, FW - 1].rearrange("p t (g s h) -> p t g s h", g=NHG, s=2)
            for g in range(NHG):
                for s in range(2):
                    last = dve.tensor_copy(by_group[:, :, g, s, :],
                                           mask[:, s:s + 1].unsqueeze(2).to_broadcast([P, ST, HG]))
            last.then_inc(ready, 1)
            dve.wait_ge(ready, 1)

            def layernorm(n, k, src, dst):
                wait(dve, mv_ok, n(NLN, k))
                for t in range(GT):
                    last = dve.bn_stats(bn[:, t, :], src(t))
                last.then_inc(bn_ok, 1)
                wait(dve, bn_ok, n(NLN, k + 1))
                wait(dve, ln_ok, n(NLN, k))
                dve.sem_inc(passed, 1)
                for t in range(GT):
                    last = dve.bn_aggr(mv[:, t, :], bn[:, t, :])
                last.then_inc(mv_ok, 1)
                wait(dve, mv_ok, n(NLN, k + 1))
                wait(dve, rs_ok, n(NLN, k + 1))
                for t in range(GT):
                    last = dve.tensor_scalar(dst(t), src(t), mv[:, t, 0:1], rs[:, t:t + 1], ALU.subtract, ALU.mult)
                last.then_inc(ln_ok, 1)

            with dve.Fori(0, NB) as b:
                n = Step(b, 1, 0)
                wait(dve, f2_ok, n(4))
                for g in range(2):
                    layernorm(n, g, lambda t: x_tile(n, g * GT + t), lambda t: xb[:, g * GT + t, :])
                wait(dve, tx, n(4, 1))
                dve.tensor_copy(xbT[:, 0, :].rearrange("p (a c) -> p a c", a=2), S[0][:, :, :]).then_inc(xTv_ok, 1)
                with dve.Fori(0, NHG) as g:
                    q = Step(b * NHG + g, 1, 0)
                    x1, x2 = qk[:, :, :, 0:HALF_D], qk[:, :, :, HALF_D:]
                    wait(dve, qkv_ok, q(2, 2))
                    wait(dve, rv_ok, q(1))
                    dve.tensor_tensor(r1[0], x1, cos[:, :, :].unsqueeze(2).to_broadcast([P, ST, 2 * HG, HALF_D]),
                                      ALU.mult).then_inc(rope_v, 1)
                    dve.tensor_tensor(r1[1], x2, sin[:, :, :].unsqueeze(2).to_broadcast([P, ST, 2 * HG, HALF_D]),
                                      ALU.mult).then_inc(rope_v, 1)
                    wait(dve, rope_v, q(2, 2))
                    wait(dve, a_ok, q(1))
                    wait(dve, r_ok, q(1))
                    dve.tensor_tensor(ro[:, :, :, 0:HALF_D], r1[0], r1[1], ALU.subtract).then_inc(rv_ok, 1)
                    wait(dve, a_ok, q(1, 1))
                    wait(dve, rp_ok, q(1, 1))
                    wait(dve, rest_ok, q(1))
                    dve.tensor_tensor(rest, ro, part(g, None, 0), ALU.subtract).then_inc(r_ok, 1)
                    wait(dve, b_ok, q(1, 1))
                    wait(dve, r_ok, q(1, 1))
                    dve.tensor_tensor(part(g, 0, 5), rest[:, :, 0:HG, :], part(g, 0, 1), ALU.subtract)
                    dve.tensor_tensor(part(g, 1, 4), rest[:, :, HG:, :], part(g, 1, 1), ALU.subtract).then_inc(rest_ok, 1)

                def step(h, g, k, ahead):
                    def maximum(of, i):
                        wait(dve, max_mm, h(ST, ST * of + i + 1))
                        if i == 0:
                            wait(dve, nm_ok, h(1, of))
                        x = X[i % 2][:, :, :].rearrange("p a c -> p (a c)")
                        dve.tensor_reduce(nm[:, i:i + 1], x[:, 0:(i + 1) * P], AX.X, ALU.max,
                                          negate=True).then_inc(mx_ok, 1)

                    if k >= -1 and ahead >= 1:
                        for i in range(4, ST):
                            maximum(1, i)
                        own = bass.ds((g + (k + 1) // HG) * (2 * HG) + (k + 1) % HG, 1)
                        wait(dve, mx_ok, h(ST, LEAD + 2 * ST))
                        wait(dve, tq_mm, h(1, 2))
                        parts = [qks[:, :, own, FM + c] for c in range(2)]
                        nm2 = nm[:, :].unsqueeze(2)
                        dve.tensor_copy(parts[0], nm2).then_inc(nm1_ok, 1)
                        wait(dve, nm1_ok, h(1, 2))
                        dve.tensor_tensor(parts[1], nm2, parts[0], ALU.subtract).then_inc(nm_ok, 1)
                    if ahead >= 2:
                        wait(dve, tq_mm, h(1, 3))
                        if k >= -1:
                            wait(dve, max_mm, h(ST, 2 * ST))
                        dve.tensor_copy(q1T[0:FW, :], T[0:FW, :]).then_inc(q1_ok, 1)
                        for i in range(4):
                            maximum(2, i)
                    if k >= 0:
                        wait(dve, pv_mm, h(NU, LEAD + NU))
                        wait(dve, cn_ok, h(1, LEAD))
                        dve.tensor_copy(o[:, :, :], O).then_inc(o_ok, 1)
                        wait(dve, o_ok, h(1, 1))
                        dve.reciprocal(rc[:, :], o[:, :, HD]).then_inc(rc_ok, 1)
                        wait(dve, rc_ok, h(1, 1))
                        wait(dve, tc, n(2))
                        dve.tensor_tensor(ctok[:, :, bass.ds(g * (HG * HD) + k * HD, HD)], o[:, :, 0:HD],
                                          rc[:, :].unsqueeze(2).to_broadcast([P, ST, HD]), ALU.mult).then_inc(cn_ok, 1)

                head_steps(dve, b, step)
                wait(dve, tc, n(2, 1))
                wait(dve, qkv_mm, n(2 * NHG, 2 * NHG))
                dve.tensor_copy(xbT[:, 0, :].rearrange("p (a c) -> p a c", a=2), S[0][:, :, :]).then_inc(cTv_ok, 1)
                for s, bank in enumerate((S[2], S[0])):
                    wait(dve, wo_mm, n(2, s + 1))
                    rows = slice(s * GT, (s + 1) * GT)
                    dve.tensor_tensor(xb[:, rows, :], bank[:, :, :].rearrange("p a (t c) -> p (a t) c", t=2),
                                      xb[:, rows, :], ALU.add).then_inc(xr_ok, 1)
                wait(dve, xr_ok, n(2, 2))
                for g in range(2):
                    layernorm(n, 2 + g, lambda t: xb[:, g * GT + t, :], lambda t: xb[:, g * GT + t, :])
                wait(dve, tx, n(4, 3))
                dve.tensor_copy(xbT[:, 0, :].rearrange("p (a c) -> p a c", a=2), S[0][:, :, :]).then_inc(xTv_ok, 1)

                def hidden(w):
                    wait(dve, sl_ok, n(16, w + 1))
                    if w % 4 == 0:
                        wait(dve, hs_ok, n(4, w // 4))
                        wait(dve, ab_ok, n(16, w))
                    dve.tensor_tensor(hj[:, w % 4, :], S[w % 3][:, 1, :], sgl[:, w % 2, :], ALU.mult).then_inc(hm_ok, 1)

                def sparsify(k):
                    g, half = divmod(k, 2)
                    s = Step(n(4, k), 1, 0)
                    wait(dve, ab_ok, n(16, 4 * (k + 1)))
                    if k == 0:
                        wait(dve, fd_mm, n(4))
                    if k == 2:
                        wait(dve, fd_mm, n(4, 2))
                    wait(dve, hs_ok, s(1))
                    chain = Chain(dve, sp, s, 3)

                    def row(i, m):
                        return aj[:, i:i + 1, :].to_broadcast([P, m, 512])
                    dve.tensor_tensor(ge[:, 0:3, :], row(0, 3), aj[:, 1:4, :], ALU.is_ge)
                    dve.tensor_tensor(ge[:, 3:5, :], row(1, 2), aj[:, 2:4, :], ALU.is_ge)
                    chain.then(dve.tensor_tensor(ge[:, 5, :], aj[:, 2, :], aj[:, 3, :], ALU.is_ge))
                    dve.tensor_tensor(nb[:, 0, :], ge[:, 0, :], ge[:, 1, :], ALU.add)
                    dve.tensor_tensor(nb[:, 1, :], ge[:, 3, :], ge[:, 4, :], ALU.add)
                    dve.tensor_tensor(nb[:, 2, :], ge[:, 1, :], ge[:, 3, :], ALU.add)
                    chain.then(dve.tensor_tensor(nb[:, 3, :], ge[:, 2, :], ge[:, 4, :], ALU.add))
                    dve.tensor_tensor(nb[:, 0, :], nb[:, 0, :], ge[:, 2, :], ALU.add)
                    dve.tensor_tensor(nb[:, 1, :], nb[:, 1, :], ge[:, 0, :], ALU.subtract)
                    dve.tensor_tensor(nb[:, 2, :], nb[:, 2, :], ge[:, 5, :], ALU.subtract)
                    chain.then(dve.tensor_tensor(nb[:, 3, :], nb[:, 3, :], ge[:, 5, :], ALU.add))
                    for i, (op, bound) in enumerate(((ALU.is_ge, 2.0), (ALU.is_ge, 1.0), (ALU.is_le, 0.0), (ALU.is_le, 1.0))):
                        last = dve.scalar_tensor_tensor(hs[:, half * 4 + i, :], nb[:, i, :], bound, hj[:, i, :], op, ALU.mult)
                    last.then_inc(hs_ok, 1)
                    chain.end()

                def finish(g):
                    for s, bank in enumerate((C, M)):
                        wait(dve, fd_mm, n(4, 2 * g + s + 1))
                        rows = slice(g * GT + 2 * s, g * GT + 2 * s + 2)
                        dve.tensor_tensor(xb[:, rows, :], bank[:, :].rearrange("p (t c) -> p t c", t=2),
                                          xb[:, rows, :], ALU.add).then_inc(f2_ok, 1)
                    wait(dve, f2_ok, n(4, 2 * g + 2))
                    wait(dve, out_st, n(32, 16 * g))
                    layernorm(n, 4 + g, lambda t: xb[:, g * GT + t, :], lambda t: ot[:, t, :])

                for k in range(4):
                    for w in range(4 * k, 4 * k + 4):
                        hidden(w)
                    sparsify(k)
                    if k == 2:
                        finish(0)
                finish(1)

        @block.tensor
        def _(pe):
            pe.sem_inc(pv_mm, LEAD)
            pe.wait_ge(consts, 16 * 8)
            pe.wait_ge(setup, 3)
            pe.wait_ge(ready, 1)

            def transposes(dst, src, done):
                for t in range(ST):
                    last = pe.transpose(dst[:, t // 4, (t % 4) * P:(t % 4 + 1) * P], src(t), ident[:])
                last.then_inc(done, 1)

            with pe.Fori(0, NB) as b:
                n = Step(b, 1, 0)
                wait(pe, ln_ok, n(NLN, 2))
                wait(pe, hm_ok, n(16))
                for f in range(KD):
                    transposes(S[f], lambda t: xb[:, t, f * P:(f + 1) * P], tx)
                with pe.Fori(0, NHG) as g:
                    q = Step(b * NHG + g, 1, 0)
                    wait(pe, xTv_ok, n(2, 1))
                    wait(pe, xTa_ok, n(2, 1))
                    wait(pe, qkv_ok, q(2))
                    for t in range(ST):
                        for k in range(KD):
                            last = pe.matmul(S[t // 4][:, t % 4 // 2, (t % 2) * 256:(t % 2) * 256 + 3 * HG * HD],
                                             xbT[:, k, t * P:(t + 1) * P],
                                             w_qkv[:, k, bass.ds(g, 1), :].rearrange("p a b -> p (a b)"),
                                             start=(k == 0), stop=(k == KD - 1))
                        if t % 4 == 3:
                            last.then_inc(qkv_mm, 1)
                wait(pe, copies_ok, n(NHG, NHG))
                wait(pe, rest_ok, n(NHG, NHG))
                wait(pe, qkv_ok, n(2 * NHG, 2 * NHG))
                wait(pe, f2_ok, n(4))

                def step(h, g, k, ahead):
                    def rows_transposed(of, s, done):
                        pe.sem_inc(passed_pe, 1)
                        for t in range(ST):
                            last = pe.transpose(T[0:FW, t * P:(t + 1) * P], rows_of(g, k + of, s, t), ident_b[:, :])
                        last.then_inc(done, 1)

                    def for_maximum(of, i):
                        if i == 0:
                            wait(pe, k_ok, h(1, of + 1))
                            wait(pe, q1_ok, h(1, of + 1))
                        wait(pe, mx_ok, h(ST, LEAD + ST * of + i - 1))
                        query = q1T[0:FW, i * P:(i + 1) * P]
                        key = kT[(k + of) % 4]
                        bank = X[i % 2]
                        for c in range(2):
                            wide = min(4, i - 4 * c) * P
                            if wide > 0:
                                last = pe.matmul(bank[:, c, 0:wide], query[0:FW - 1, :],
                                                 key[0:FW - 1, 512 * c:512 * c + wide], start=True, stop=True)
                        last = pe.matmul(bank[:, i // 4, (i % 4) * P:(i % 4 + 1) * P], query,
                                         key[0:FW, i * P:(i + 1) * P], start=True, stop=True)
                        last.then_inc(max_mm, 1)

                    def scores(of, u):
                        if u == 0:
                            wait(pe, q2_ok, h(1, of + 1))
                        wait(pe, exp_ok, h(NU, LEAD + NU * of + u - 1))
                        bank = W[((k + of) * NU + u) % 2]
                        for at, j, i, count, diagonal in runs(u):
                            rows = FW if diagonal else FW - 1
                            last = pe.matmul(bank[:, at * P:(at + count) * P], kT[(k + of) % 4][0:rows, j * P:(j + 1) * P],
                                             q2T[(k + of) % 2][0:rows, i * P:(i + count) * P], start=True, stop=True)
                        last.then_inc(sc_mm, 1)

                    def weighted(u):
                        wait(pe, exp_ok, h(NU, LEAD + u + 1))
                        if u == 0:
                            wait(pe, o_ok, h(1))
                        for at, (j, i) in enumerate(BLOCKS[UB * u:UB * u + UB]):
                            last = pe.matmul(O[:, i, :], pb[u % 3][:, at * P:(at + 1) * P],
                                             v[:, j, bass.ds(g * HG + k, 1), :].rearrange("p a d -> p (a d)"),
                                             start=(j == 0 and i == 0), stop=(j == ST - 1))
                        last.then_inc(pv_mm, 1)

                    for s in range(NU):
                        if k >= 0 and s + 1 < NU:
                            scores(0, s + 1)
                        if s == NU - 1 and k >= -1 and ahead >= 1:
                            scores(1, 0)
                        if s <= 3 and k >= -1 and ahead >= 1:
                            for_maximum(1, 4 + s)
                        if s == 3 and ahead >= 2:
                            if k >= -1:
                                wait(pe, q2_ok, h(1, 1))
                            rows_transposed(2, 1, tk_mm)
                        if s == 4 and ahead >= 2:
                            wait(pe, k_ok, h(1, 3))
                            rows_transposed(2, 0, tq_mm)
                        if s == 5 and k >= -1 and ahead >= 1:
                            if ahead >= 2:
                                wait(pe, q1_ok, h(1, 3))
                            else:
                                wait(pe, q2_ok, h(1, 1))
                            wait(pe, nm_ok, h(1, 2))
                            rows_transposed(1, 0, tm_mm)
                        if s >= 6 and ahead >= 2:
                            for i in ((0,), (1, 2), (3,))[s - 6]:
                                for_maximum(2, i)
                        if k >= 0:
                            weighted(s)

                head_steps(pe, b, step)
                wait(pe, cn_ok, n(HEADS, LEAD + HEADS))
                for f in range(KD):
                    transposes(S[f], lambda t: ctok[:, t, f * P:(f + 1) * P], tc)
                wait(pe, cTv_ok, n(1, 1))
                wait(pe, cTa_ok, n(1, 1))
                for t in range(ST):
                    bank = (S[2], S[0])[t // 4]
                    for k in range(KD):
                        last = pe.matmul(bank[:, t % 4 // 2, (t % 2) * D:(t % 2 + 1) * D], xbT[:, k, t * P:(t + 1) * P],
                                         w_o[:, k, :], start=(k == 0), stop=(k == KD - 1))
                    if t % 4 == 3:
                        last.then_inc(wo_mm, 1)
                wait(pe, ln_ok, n(NLN, 4))
                for f in range(KD):
                    transposes(S[f], lambda t: xb[:, t, f * P:(f + 1) * P], tx)
                wait(pe, xTv_ok, n(2, 2))
                wait(pe, xTa_ok, n(2, 2))

                def hidden(w):
                    g, c = divmod(w, NF)
                    if w >= 3:
                        wait(pe, hm_ok, n(16, w - 2))
                    for e, wt in enumerate((w_fg, w_fu)):
                        for k in range(KD):
                            last = pe.matmul(S[w % 3][:, e, :], wt[:, k, c * P:(c + 1) * P],
                                             xbT[:, k, g * 512:(g + 1) * 512], start=(k == 0), stop=(k == KD - 1))
                    last.then_inc(ff_mm, 1)

                def down(g):
                    wait(pe, hs_ok, n(4, 2 * g + 2))
                    wait(pe, f2_ok, n(4, 2 * g))
                    for t in range(GT):
                        for k in range(NF):
                            last = pe.matmul((C, M)[t // 2][:, (t % 2) * D:(t % 2 + 1) * D], hs[:, k, t * P:(t + 1) * P],
                                             w_fd[:, k, :], start=(k == 0), stop=(k == NF - 1))
                        if t % 2:
                            last.then_inc(fd_mm, 1)

                for w in range(16):
                    if w == 11:
                        down(0)
                    hidden(w)
                down(1)


def build(nc, io):
    io["rows"] = nc.dram_tensor("rows", (TOK + P, ROW), F32, kind="Internal").ap()
    io["rows_t"] = io["rows"][0:TOK, :].rearrange("(t p) c -> p t c", p=P)
    with ExitStack() as ctx:
        kit = Kit(nc, ctx)
        keep = {"x_sb": kit.sb("x_sb", [P, NT, D]), "ident": kit.sb("ident", [P, P])}
        with ExitStack() as first:
            kit = Kit(nc, first)
            keep["xT"] = kit.sb("xT", [P, KD, TOK])
            keep["logits"] = kit.sb("logits", [P, NT, E])
            conv_mlp_phase(nc, io, keep)
            experts_phase(nc, io, keep)
        attention_ffn_phase(nc, io, keep)


def kernel(**inputs):
    import ml_dtypes
    from concourse import bacc
    from concourse.bass_utils import run_bass_kernel_spmd

    BF = ml_dtypes.bfloat16

    def chunks(a):
        return np.ascontiguousarray(a.reshape(-1, P, a.shape[-1]).transpose(1, 0, 2))

    def quads(a):
        return np.ascontiguousarray(a.reshape(2, P, 4, -1).transpose(0, 2, 1, 3).reshape(DF, -1))

    frequency = np.float32(1.0) / np.float32(10000.0) ** (np.arange(0, HD, 2, dtype=np.float32) / np.float32(HD))
    position = (np.arange(P)[:, None] + P * np.arange(ST)[None, :]).astype(np.float32)
    angle = position[:, :, None] * frequency[None, None, :]

    g = {k: np.asarray(v) for k, v in inputs.items()}
    arrays = {
        "x": np.pad(chunks(g["L0_attn_x"].reshape(TOK, D)), ((0, 0), (0, GT), (0, 0))),
        "ident": np.eye(P, dtype=np.float32),
        "w_in": chunks(g["L0_attn_W_in"].T),
        "conv_w": chunks(g["L0_attn_conv_w"].reshape(DI, TAPS)),
        "conv_b": np.ascontiguousarray(g["L0_attn_conv_b"].reshape(NCI, P).T),
        "w_out": chunks(g["L0_attn_W_out"].T),
        "w_up": chunks(g["L0_attn_W_mlp1"].T),
        "w_dn": chunks(g["L0_attn_W_mlp2"].T),
        "gate_w": chunks(g["L0_ffn_gate_w"].T),
        "we_gu": np.ascontiguousarray(g["L0_ffn_w_gate_up"].reshape(E, KD, P, -1).transpose(2, 0, 1, 3)),
        "we_dn": np.ascontiguousarray(g["L0_ffn_w_down"].reshape(E, NIX, IX, D).transpose(2, 0, 1, 3)),
        "ws_gu": chunks(g["L0_ffn_ws_gate_up"]),
        "ws_dn": np.ascontiguousarray(g["L0_ffn_ws_down"].reshape(NSX, IX, D).transpose(1, 0, 2)),
        "upper": np.triu(np.ones((P, P))).astype(BF),
        "ones": np.ones((P, P), BF),
        "ones_f": np.ones((P, 1), np.float32),
        "place": (np.arange(P)[:, None] // E + CG * np.arange(CJ)[None, :]).astype(np.float32),
        "mine": (np.arange(P)[:, None] % E == np.arange(E)[None, :]).astype(np.float32),
        "lane": np.tile(np.arange(P, dtype=np.float32), (P, 1)),
        "base": np.tile(P * np.arange(NT, dtype=np.float32), (P, 1)),
        "zeros": np.zeros((P, ROW), np.float32),
        "w_qkv": chunks(np.concatenate([g[f"L1_attn_w_{c}"].T.reshape(D, NHG, HG * HD) for c in "qkv"],
                                       axis=2).reshape(D, -1)).reshape(P, KD, NHG, -1),
        "w_o": chunks(g["L1_attn_w_o"].T),
        "w_fg": chunks(quads(g["L1_ffn_w_gate"].T).T),
        "w_fu": chunks(quads(g["L1_ffn_w_up"].T).T),
        "w_fd": chunks(quads(g["L1_ffn_w_down"])),
        "cos": np.ascontiguousarray(np.cos(angle).astype(np.float32)),
        "sin": np.ascontiguousarray(np.sin(angle).astype(np.float32)),
        "mask": np.stack([np.arange(P) < BLK, (np.arange(P) >= BLK) * np.float32(MASKED)], axis=1).astype(np.float32),
    }
    nc = bacc.Bacc("TRN2", target_bir_lowering=False, num_devices=1)
    io = {n: nc.dram_tensor(n, a.shape, mybir.dt.from_np(a.dtype), kind="ExternalInput").ap()
          for n, a in arrays.items()}
    io["out"] = nc.dram_tensor("out", (P, NT, D), F32, kind="ExternalOutput").ap()
    build(nc, io)
    r = run_bass_kernel_spmd(nc, [arrays], core_ids=[0])
    out = np.asarray(r.results[0]["out"])
    return out.transpose(1, 0, 2).reshape(4, 1024, D)
```

```python
from contextlib import ExitStack

import numpy as np

import concourse.bass as bass
from concourse import mybir

F32 = mybir.dt.float32
BF16 = mybir.dt.bfloat16
F16 = mybir.dt.float16
I32 = mybir.dt.int32
U32 = mybir.dt.uint32
ALU = mybir.AluOpType
ACT = mybir.ActivationFunctionType
AX = mybir.AxisListType

P = 128
D = 256
KD = D // P
NT = 32
TOK = NT * P
GT = 4
GTOK = GT * P
NG = NT // GT
DI = 512
NCI = DI // P
TAPS = 4
N_CONST = 8
DF = 1024
NF = DF // P
E = 32
ROW = D + E


class Step:

    def __init__(self, reg, mul, off):
        self.reg, self.mul, self.off = reg, mul, off

    def __call__(self, per, plus=0):
        fixed = self.off * per + plus
        return fixed if self.reg is None else self.reg * (self.mul * per) + fixed

    def before(self, k):
        return Step(self.reg, self.mul, self.off - k)

    def among(self, low, high):
        return self.reg is not None or low <= self.off < high


def wait(eng, sem, value):
    if not isinstance(value, int) or value > 0:
        eng.wait_ge(sem, value)


def steps(eng, first, last):
    pairs = (NG - first) // 2
    for n in range(first):
        yield Step(None, 0, n), n % 2
    with eng.Fori(0, pairs) as m:
        for k in range(2):
            yield Step(m, 2, first + k), (first + k) % 2
    for n in range(first + 2 * pairs, last):
        yield Step(None, 0, n), n % 2


def tiles(n, count=GT):
    return bass.ds(n(GT), count)


class Kit:

    def __init__(self, nc, ctx):
        self.nc, self.ctx = nc, ctx

    def sb(self, name, shape, dt=F32):
        return self.ctx.enter_context(self.nc.sbuf_tensor(name + "_sb", list(shape), dt))

    def ps(self, name, shape, dt=F32):
        return self.ctx.enter_context(self.nc.psum_tensor(name + "_ps", list(shape), dt))

    def sems(self, names):
        return [self.ctx.enter_context(self.nc.semaphore(n)) for n in names.split()]


def conv_mlp_phase(nc, io, keep):
    with ExitStack() as ctx:
        kit = Kit(nc, ctx)
        sb, ps = kit.sb, kit.ps
        x_sb, xT, ident, logits = keep["x_sb"], keep["xT"], keep["ident"], keep["logits"]

        w_in = sb("w_in", [P, KD, 2 * DI])
        w_out = sb("w_out", [P, NCI, D])
        w_up = sb("w_up", [P, KD, DF])
        w_dn = sb("w_dn", [P, NF, D])
        w_gate = sb("w_gate", [P, KD, E])
        conv_w = sb("conv_w", [P, NCI, TAPS])
        conv_b = sb("conv_b", [P, NCI])
        power = sb("power", [P, GT])
        eps = sb("eps", [P, GT])
        h = sb("h", [P, GT, D])
        hT = sb("hT", [P, KD, GTOK])
        xp = [sb(f"xp{i}", [P, NCI, TAPS - 1 + GTOK]) for i in range(2)]
        xc = sb("xc", [P, NCI, GTOK])
        sz = sb("sz", [P, NCI, GTOK])
        yT = sb("yT", [P, NCI, GTOK])
        x1 = sb("x1", [P, GT, D])
        h1 = sb("h1", [P, GT, D])
        h1T = sb("h1T", [P, KD, GTOK])
        m1T = sb("m1T", [P, NF, GTOK])
        sq = sb("sq", [P, GT, D], BF16)
        ss1 = sb("ss1", [P, GT])
        ss2 = sb("ss2", [P, GT])
        g1 = sb("g1", [P, GT])
        g2 = sb("g2", [P, GT])
        rn1 = sb("rn1", [P, GT])
        rn2 = sb("rn2", [P, GT])
        bn = sb("bn", [P, GT, 6])
        mv = sb("mv", [P, GT, 2])
        x_in = [sb(f"x_in{i}", [P, GT, D]) for i in range(2)]
        xx = sb("xx", [P, GT, D])
        x2 = sb("x2", [P, GT, D])
        xa = sb("xa", [P, GT, D])
        xaT = sb("xaT", [P, KD, GTOK])
        ve = sb("ve", [P, GT])
        rs = sb("rs", [P, GT])

        tp = ps("tp", [P, KD, GTOK])
        mm = [ps(f"mm{i}", [P, GTOK]) for i in range(4)]
        ro = [ps(f"ro{i}", [P, 2, D]) for i in range(2)]

        (consts, xl0, xl1, ss1_ok, g1_ok, rn1_ok, h_ok, tr1, hT_ok, in_mm, xp_ok, sz_ok, tap, conv_ok,
         xc_ok, y_ok, out_mm, x1_ok, ss2_ok, g2_ok, rn2_ok, h1_ok, xx_ok, tr2, h1T_ok, up_mm, m1a_ok,
         m1v_ok, dn_mm, x2_ok, bn_ok, mv_ok, ve_ok, rs_ok, xa_ok, tr3, xaT_ok, xT_ok, xs_ok, lg_mm, lg_ok, row_st,
         setup, passed_pool, passed_dve) = kit.sems(
            "consts x_loaded_even x_loaded_odd ss1_ready g1_ready rn1_ready h_ready tr1_done hT_ready in_done "
            "xp_ready sz_ready tap_done conv_ready xc_ready y_ready out_done x1_ready ss2_ready g2_ready "
            "rn2_ready h1_ready xx_ready tr2_done h1T_ready up_done m1_even_ready m1_odd_ready down_done "
            "x2_ready bn_ready mv_ready ve_ready rs_ready xa_ready tr3_done xaT_ready xT_kept x_kept logit_done logit_ready "
            "row_stored setup_done "
            "passed_pool passed_dve")
        x_loaded = [xl0, xl1]
        ALL = NG + 2
        block = ctx.enter_context(nc.Block())

        @block.sync
        def _(sp):
            def load(n, par):
                sp.dma_start(x_in[par][:, :, :], io["x"][:, tiles(n), :]).then_inc(x_loaded[par], 16)

            load(Step(None, 0, 0), 0)
            sp.dma_start(keep["ident"][:], io["ident"]).then_inc(consts, 16)
            for src, dst in (("w_in", w_in), ("conv_w", conv_w), ("conv_b", conv_b), ("w_out", w_out),
                             ("w_up", w_up), ("w_dn", w_dn), ("gate_w", w_gate)):
                sp.dma_start(dst[:], io[src]).then_inc(consts, 16)
            for n, par in steps(sp, 2, ALL):
                if n.among(0, NG):
                    wait(sp, xx_ok, n(1))
                    load(n.before(-1), 1 - par)
                if n.among(1, NG + 1):
                    b = n.before(1)
                    wait(sp, xa_ok, b(1, 1))
                    sp.dma_start(io["rows_t"][:, tiles(b), 0:D], xa[:, :, :]).then_inc(row_st, 16)
            sp.wait_ge(row_st, 16 * NG)

        @block.gpsimd
        def _(pool):
            pool.memset(power[:], -0.5).then_inc(setup, 1)
            pool.memset(eps[:], 1e-5).then_inc(setup, 1)
            pool.memset(xp[0][:, :, 0:TAPS - 1], 0.0).then_inc(setup, 1)
            pool.wait_ge(setup, 3)

            def rms(n, ss_ok, ss, g, g_ok, rn, rn_ok, used):
                wait(pool, ss_ok, n(GT, GT))
                wait(pool, rn_ok, n(1))
                pool.sem_inc(passed_pool, 1)
                pool.tensor_scalar(g[:], ss[:], 1e-24, None, ALU.max).then_inc(g_ok, 1)
                wait(pool, g_ok, n(1, 1))
                wait(pool, used, n(1))
                pool.tensor_tensor(rn[:], g[:], power[:], ALU.pow).then_inc(rn_ok, 1)

            rms(Step(None, 0, 0), ss1_ok, ss1, g1, g1_ok, rn1, rn1_ok, h_ok)
            for n, par in steps(pool, 2, ALL):
                if n.among(0, NG):
                    rms(n.before(-1), ss1_ok, ss1, g1, g1_ok, rn1, rn1_ok, h_ok)
                if n.among(0, NG):
                    for c in range(NCI):
                        if c == 0:
                            wait(pool, out_mm, n(2))
                        wait(pool, sz_ok, n(NCI, c + 1))
                        wait(pool, xc_ok, n(NCI, c + 1))
                        pool.tensor_tensor(yT[:, c, :], xc[:, c, :], sz[:, c, :], ALU.mult).then_inc(y_ok, 1)
                if n.among(2, ALL):
                    c = n.before(2)
                    wait(pool, xaT_ok, c(1, 1))
                    pool.tensor_copy(xT[:, :, bass.ds(c(GTOK), GTOK)], xaT[:, :, :]).then_inc(xT_ok, 1)
                if n.among(0, NG):
                    rms(n, ss2_ok, ss2, g2, g2_ok, rn2, rn2_ok, h1_ok)
                if n.among(1, NG + 1):
                    b = n.before(1)
                    wait(pool, mv_ok, b(GT, GT))
                    wait(pool, rs_ok, b(1))
                    pool.tensor_tensor(ve[:], mv[:, :, 1], eps[:], ALU.add).then_inc(ve_ok, 1)
                    wait(pool, ve_ok, b(1, 1))
                    wait(pool, xa_ok, b(1))
                    pool.tensor_tensor(rs[:], ve[:], power[:], ALU.pow).then_inc(rs_ok, 1)
                if n.among(0, NG):
                    wait(pool, x1_ok, n(2, 2))
                    wait(pool, x2_ok, n(2))
                    pool.tensor_tensor(xx[:, :, :], x_in[par][:, :, :], x1[:, :, :], ALU.add).then_inc(xx_ok, 1)
                if n.among(1, NG + 1):
                    b = n.before(1)
                    wait(pool, xa_ok, b(1, 1))
                    pool.tensor_copy(x_sb[:, tiles(b), :], xa[:, :, :]).then_inc(xs_ok, 1)
            pool.wait_ge(xs_ok, NG)
            pool.wait_ge(xT_ok, NG)

        @block.scalar
        def _(act):
            def squares(src, ss, ss_ok):
                for t in range(GT):
                    act.activation(sq[:, t, :], src[:, t, :], ACT.Square, accum_out=ss[:, t:t + 1]).then_inc(ss_ok, 1)

            act.wait_ge(x_loaded[0], 16)
            squares(x_in[0], ss1, ss1_ok)
            for n, par in steps(act, 2, ALL):
                if n.among(0, NG):
                    loads = n.before(-1)
                    if n.reg is None:
                        act.wait_ge(x_loaded[1 - par], 16 * (loads.off // 2 + 1))
                    else:
                        act.wait_ge(x_loaded[1 - par], n.reg * 16 + 16 * (loads.off // 2 + 1))
                    wait(act, g1_ok, n(1, 1))
                    squares(x_in[1 - par], ss1, ss1_ok)
                if n.among(0, NG):
                    for c in range(NCI):
                        wait(act, in_mm, n(2 * NCI, c + 1))
                        wait(act, conv_ok, n(NCI, c - NCI + 1))
                        last = act.activation(xp[par][:, c, TAPS - 1:], mm[c][:], ACT.Copy)
                        if par == 0:
                            last = act.activation(xp[1][:, c, 0:TAPS - 1], mm[c][:, GTOK - TAPS + 1:], ACT.Copy)
                        last.then_inc(xp_ok, 1)
                    for c in range(NCI):
                        wait(act, in_mm, n(2 * NCI, NCI + c + 1))
                        wait(act, y_ok, n(NCI, c - NCI + 1))
                        act.activation(sz[:, c, :], mm[c][:], ACT.Silu).then_inc(sz_ok, 1)
                if n.among(2, ALL):
                    c = n.before(2)
                    wait(act, tr3, c(1, 1))
                    wait(act, xT_ok, c(1))
                    wait(act, lg_mm, c(1))
                    act.activation(xaT[:, :, :], tp[:, :, :], ACT.Copy).then_inc(xaT_ok, 1)
                if n.among(0, NG):
                    for c in range(NCI):
                        wait(act, conv_ok, n(NCI, c + 1))
                        act.activation(xc[:, c, :], xc[:, c, :], ACT.Silu).then_inc(xc_ok, 1)
                if n.among(1, NG + 1):
                    b = n.before(1)
                    for f in range(0, NF, 2):
                        wait(act, up_mm, b(NF, f + 1))
                        if f == 0:
                            wait(act, dn_mm, b(2))
                        act.activation(m1T[:, f, :], mm[f % 4][:], ACT.Relu).then_inc(m1a_ok, 1)
                if n.among(0, NG):
                    wait(act, x1_ok, n(2, 2))
                    wait(act, g2_ok, n(1))
                    squares(x1, ss2, ss2_ok)

        @block.vector
        def _(dve):
            def scaled(n, src, rn, rn_ok, dst, used, ok):
                wait(dve, rn_ok, n(1, 1))
                wait(dve, used, n(1))
                for t in range(GT):
                    last = dve.tensor_scalar(dst[:, t, :], src[:, t, :], rn[:, t:t + 1], D ** 0.5, ALU.mult, ALU.mult)
                last.then_inc(ok, 1)

            dve.wait_ge(x_loaded[0], 16)
            scaled(Step(None, 0, 0), x_in[0], rn1, rn1_ok, h, tr1, h_ok)
            dve.wait_ge(consts, N_CONST * 16)
            dve.wait_ge(setup, 3)
            for n, par in steps(dve, 2, ALL):
                if n.among(0, NG):
                    wait(dve, tr1, n(1, 1))
                    wait(dve, in_mm, n(2 * NCI))
                    dve.tensor_copy(hT[:, :, :], tp[:, :, :]).then_inc(hT_ok, 1)
                    for c in range(NCI):
                        wait(dve, xp_ok, n(NCI, c + 1))
                        wait(dve, y_ok, n(NCI, c - NCI + 1))
                        dve.tensor_scalar(xc[:, c, :], xp[par][:, c, TAPS - 1:], conv_w[:, c, TAPS - 1:],
                                          conv_b[:, c:c + 1], ALU.mult, ALU.add).then_inc(tap, 1)
                        for k in range(TAPS - 1):
                            wait(dve, tap, n(NCI * (TAPS - 1), c * (TAPS - 1) + k + 1))
                            dve.scalar_tensor_tensor(xc[:, c, :], xp[par][:, c, k:k + GTOK], conv_w[:, c, k:k + 1],
                                                     xc[:, c, :], ALU.mult, ALU.add)\
                               .then_inc(conv_ok if k == TAPS - 2 else tap, 1)
                if n.among(0, NG):
                    if n.reg is None:
                        dve.wait_ge(x_loaded[1 - par], 16 * ((n.off + 1) // 2 + 1))
                    else:
                        dve.wait_ge(x_loaded[1 - par], n.reg * 16 + 16 * ((n.off + 1) // 2 + 1))
                    scaled(n.before(-1), x_in[1 - par], rn1, rn1_ok, h, tr1, h_ok)
                if n.among(1, NG + 1):
                    b = n.before(1)
                    wait(dve, tr2, b(1, 1))
                    wait(dve, up_mm, b(NF))
                    dve.tensor_copy(h1T[:, :, :], tp[:, :, :]).then_inc(h1T_ok, 1)
                if n.among(2, ALL):
                    c = n.before(2)
                    wait(dve, lg_mm, c(1, 1))
                    dve.tensor_copy(logits[:, tiles(c), :],
                                    ro[0][:, 0, 0:GT * E].rearrange("p (t e) -> p t e", t=GT)).then_inc(lg_ok, 1)
                if n.among(1, NG + 1):
                    b = n.before(1)
                    for f in range(1, NF, 2):
                        wait(dve, up_mm, b(NF, f + 1))
                        if f == 1:
                            wait(dve, dn_mm, b(2))
                        dve.tensor_scalar(m1T[:, f, :], mm[f % 4][:], 0.0, None, ALU.max).then_inc(m1v_ok, 1)
                if n.among(0, NG):
                    wait(dve, xx_ok, n(1))
                    for j in range(2):
                        wait(dve, out_mm, n(2, j + 1))
                        dve.tensor_tensor(x1[:, 2 * j:2 * j + 2, :], ro[j][:, :, :],
                                          x_in[par][:, 2 * j:2 * j + 2, :], ALU.add).then_inc(x1_ok, 1)
                    wait(dve, x1_ok, n(2, 2))
                    scaled(n, x1, rn2, rn2_ok, h1, tr2, h1_ok)
                if n.among(1, NG + 1):
                    b = n.before(1)
                    wait(dve, xx_ok, b(1, 1))
                    wait(dve, xa_ok, b(1))
                    for j in range(2):
                        wait(dve, dn_mm, b(2, j + 1))
                        dve.tensor_tensor(x2[:, 2 * j:2 * j + 2, :], ro[j][:, :, :], xx[:, 2 * j:2 * j + 2, :],
                                          ALU.add).then_inc(x2_ok, 1)
                    for t in range(GT):
                        wait(dve, x2_ok, b(2, t // 2 + 1))
                        dve.bn_stats(bn[:, t, :], x2[:, t, :]).then_inc(bn_ok, 1)
                    wait(dve, bn_ok, b(GT, GT))
                    dve.sem_inc(passed_dve, 1)
                    for t in range(GT):
                        dve.bn_aggr(mv[:, t, :], bn[:, t, :]).then_inc(mv_ok, 1)
                    wait(dve, mv_ok, b(GT, GT))
                    wait(dve, rs_ok, b(1, 1))
                    wait(dve, row_st, b(16))
                    wait(dve, xs_ok, b(1))
                    wait(dve, tr3, b(1))
                    for t in range(GT):
                        last = dve.tensor_scalar(xa[:, t, :], x2[:, t, :], mv[:, t, 0:1], rs[:, t:t + 1],
                                                 ALU.subtract, ALU.mult)
                    last.then_inc(xa_ok, 1)

        @block.tensor
        def _(pe):
            def transposes(src, done):
                for f in range(KD):
                    for t in range(GT):
                        last = pe.transpose(tp[:, f, t * P:(t + 1) * P], src[:, t, f * P:(f + 1) * P], ident[:])
                last.then_inc(done, 1)

            def chunk(c, w, rhsT, done):
                for k in range(KD):
                    last = pe.matmul(mm[c % 4][:], w[:, k, c * P:(c + 1) * P], rhsT[:, k, :],
                                     start=(k == 0), stop=(k == KD - 1))
                last.then_inc(done, 1)

            def rows(lhsT, w, chunks, done):
                for t in range(GT):
                    for k in range(chunks):
                        last = pe.matmul(ro[t // 2][:, t % 2, :], lhsT[:, k, t * P:(t + 1) * P], w[:, k, :],
                                         start=(k == 0), stop=(k == chunks - 1))
                    if t % 2:
                        last.then_inc(done, 1)

            pe.wait_ge(consts, N_CONST * 16)
            for n, par in steps(pe, 2, ALL):
                a, b, c3 = n, n.before(1), n.before(2)
                has_a, has_b, has_c = n.among(0, NG), n.among(1, NG + 1), n.among(2, ALL)
                if has_a:
                    wait(pe, h_ok, a(1, 1))
                    wait(pe, h1T_ok, a(1, -1))
                    transposes(h, tr1)
                    wait(pe, hT_ok, a(1, 1))
                    for c in range(2 * NCI):
                        if c < 4:
                            wait(pe, sz_ok, a(NCI, c - NCI + 1))
                            if c == 0:
                                wait(pe, m1a_ok, a(NF // 2, -NF // 2))
                                wait(pe, m1v_ok, a(NF // 2, -NF // 2))
                        else:
                            wait(pe, xp_ok, a(NCI, c - 4 + 1))
                        chunk(c, w_in, hT, in_mm)
                if has_c:
                    wait(pe, xa_ok, c3(1, 1))
                    wait(pe, hT_ok, a(1, 1)) if has_a else wait(pe, h1T_ok, c3(1, 1))
                    transposes(xa, tr3)
                if has_b:
                    wait(pe, h1_ok, b(1, 1))
                    if has_a:
                        wait(pe, hT_ok, a(1, 1))
                    if has_c:
                        wait(pe, xaT_ok, c3(1, 1))
                    transposes(h1, tr2)
                if has_c:
                    wait(pe, xaT_ok, c3(1, 1))
                    wait(pe, x2_ok, c3(2, 2))
                    for t in range(GT):
                        for k in range(KD):
                            last = pe.matmul(ro[0][:, 0, t * E:(t + 1) * E], xaT[:, k, t * P:(t + 1) * P],
                                             w_gate[:, k, :], start=(k == 0), stop=(k == KD - 1))
                    last.then_inc(lg_mm, 1)
                if has_b:
                    wait(pe, h1T_ok, b(1, 1))
                    for c in range(NF):
                        if c < 4:
                            if has_a:
                                wait(pe, sz_ok, a(NCI, c + 1))
                            elif c == 0:
                                wait(pe, m1a_ok, b(NF // 2))
                                wait(pe, m1v_ok, b(NF // 2))
                        else:
                            wait(pe, (m1a_ok, m1v_ok)[c % 2], b(NF // 2, (c - 4) // 2 + 1))
                        chunk(c, w_up, h1T, up_mm)
                if has_a:
                    wait(pe, y_ok, a(NCI, NCI))
                    wait(pe, x2_ok, a(2, -2))
                    if has_c:
                        wait(pe, lg_ok, c3(1, 1))
                    rows(yT, w_out, NCI, out_mm)
                if has_b:
                    wait(pe, m1a_ok, b(NF // 2, NF // 2))
                    wait(pe, m1v_ok, b(NF // 2, NF // 2))
                    if has_a:
                        wait(pe, x1_ok, a(2, 2))
                    if has_c:
                        wait(pe, lg_ok, c3(1, 1))
                    rows(m1T, w_dn, NF, dn_mm)



CAP = 48
TOPK = 6
TOPG = 3
EG = 8
IX = 88
NIX = 2
NSX = 3
SHARED = 352
CG = 4
CJ = CAP // CG
RING = 8
SCALE_MOE = 16.0
LOW = -3.0e38
TAKEN = 3.0e38


def experts_phase(nc, io, keep):
    with ExitStack() as ctx:
        kit = Kit(nc, ctx)
        sb, ps = kit.sb, kit.ps
        x_sb, ident, logits = keep["x_sb"], keep["ident"], keep["logits"]
        inner = ctx.enter_context(ExitStack())

        ws_gu = sb("ws_gu", [P, KD, 2 * NSX * P])
        ws_dn = sb("ws_dn", [P, NSX, D])
        we_gu = sb("we_gu", [P, RING, KD, 2 * NIX * IX])
        we_dn = sb("we_dn", [IX, RING, NIX, D])
        upper = sb("upper", [P, P], BF16)
        ones = sb("ones", [P, P], BF16)
        ones_f = sb("ones_f", [P, 1])
        place = sb("place", [P, CJ])
        mine = sb("mine", [P, E])
        lane = sb("lane", [P, P])
        sg = sb("sg", [P, NSX, GTOK])
        su = sb("su", [P, NSX, GTOK])
        so = sb("so", [P, GT, D])
        sel = sb("sel", [P, NT, E])
        selr = sb("selr", [P, NT, CG, E], BF16)
        pre = [sb(f"pre{i}", [P, NT // 2 + NT, E], BF16) for i in range(2)]
        prer = sb("prer", [P, NT, CG, E], BF16)
        cum = sb("cum", [P, TOK], BF16)
        eg = sb("eg", [IX, 2, NIX, CAP])
        ea = sb("ea", [IX, 2, NIX, CAP])
        cnt = sb("cnt", [P, CJ])
        idx = sb("idx", [P, CJ], U32)
        w_slot = sb("w_slot", [P, CJ])
        wtmp = sb("wtmp", [P, CJ, E])
        rel = sb("rel", [P, NT, CJ])
        base = sb("base", [P, NT])
        busy_f = sb("busy_f", [P, NT])
        busy = sb("busy", [1, NT], I32)
        rden = sb("rden", [P, NT])
        rsum = sb("rsum", [P, NT])
        arena = sb("arena", [P, 7168])
        at = [0]

        def view(*shape):
            n = int(np.prod(shape))
            v = arena[:, at[0]:at[0] + n]
            at[0] += n
            names = "abc"[:len(shape)]
            return v.rearrange(f"p ({' '.join(names)}) -> p {' '.join(names)}", **dict(zip(names, shape)))

        gm, gr = view(NT, 2 * EG), view(NT, 2 * EG)
        kept = view(NT, EG)
        sc, sr = view(NT, E + 8), view(NT, E + 8)
        ex, wt = view(NT, E), view(NT, E)
        t8, t8b = sb("t8", [P, NT, 8]), sb("t8b", [P, NT, 8])
        at[0] = 0
        xg = view(CJ, ROW)
        y = view(CJ, D)
        dump = arena[:, 0:TOK // 2].bitcast(BF16)
        xgT = keep["xT"][:, 0, 0:KD * E * CAP].rearrange("p (k e c) -> p k e c", k=KD, e=E)
        yT = keep["xT"][:, 1, 0:KD * E * CAP].rearrange("p (k c e) -> p k c e", k=KD, e=E)
        xT = keep["xT"]

        mm = [ps(f"em{i}", [P, GTOK]) for i in range(4)]
        ro = [ps(f"er{i}", [P, 2, D]) for i in range(2)]
        tp = [ps(f"et{i}", [P, GTOK]) for i in range(2)]

        (consts, gu_mm, sg_ok, su_ok, sa_ok, dn_mm, so_ok, r_ok, rt, mset, sub_ok, exp_ok, pre_ok, cum_mm,
         cum_ok, cnt_ok, idx_ok, w_st, gath, busy_mm, busy_ok, tr_ok, xg_ok, egu_mm, eg_ok, ea_ok, edn_mm, ey_ok,
         ty_ok, y_ok, ws_ok, oh_ok, cb_mm, cb_ok, rel_ok) = kit.sems(
            "consts2 shared_gu_done shared_gate_ready shared_up_ready shared_act_ready shared_down_done "
            "shared_out_ready shared_added route_step softmax_step centered exp_ready prefix_ready cum_done cum_ready "
            "count_done slot_token_ready weights_stored gathered busy_done busy_ready slots_transposed "
            "slot_features_ready expert_gu_done expert_gate_ready expert_act_ready expert_down_done "
            "expert_out_ready out_transposed slot_out_ready slot_weight_ready onehot_ready combine_done "
            "combined relative_ready")
        ring = kit.sems(" ".join(f"expert_weights_{i}" for i in range(RING)))
        N2 = 10
        HALF = 5

        def shared(eng, lo, hi):
            with eng.Fori(0, hi - lo) as r:
                yield Step(r, 1, lo)

        block = inner.enter_context(nc.Block())

        @block.sync
        def _(sp):
            for src, dst in (("ws_gu", ws_gu), ("ws_dn", ws_dn), ("upper", upper), ("ones", ones), ("ones_f", ones_f),
                             ("place", place), ("mine", mine), ("lane", lane), ("base", base)):
                sp.dma_start(dst[:], io[src]).then_inc(consts, 16)
            sp.dma_start(io["rows"][TOK:TOK + P, :], io["zeros"]).then_inc(consts, 16)

            def weights(i, e):
                sp.dma_start(we_gu[:, i, :, :], io["we_gu"][:, bass.ds(e, 1), :, :].rearrange("p e k n -> p (e k) n")).then_inc(ring[i], 16)
                sp.dma_start(we_dn[:, i, :, :], io["we_dn"][:, bass.ds(e, 1), :, :].rearrange("p e k n -> p (e k) n")).then_inc(ring[i], 16)

            for i in range(RING):
                weights(i, i)
            sp.wait_ge(rt, 12)
            sp.dma_start(io["rows_t"][:, :, D:ROW], wt).then_inc(w_st, 16)
            with sp.Fori(0, E // RING - 1) as r:
                for i in range(RING):
                    sp.wait_ge(edn_mm, r * RING + (i + 1))
                    weights(i, r * RING + (RING + i))

        @block.gpsimd
        def _(pool):
            def act(n):
                for i in range(NSX):
                    wait(pool, sg_ok, n(NSX, i + 1))
                    wait(pool, su_ok, n(NSX, i + 1))
                    pool.tensor_tensor(su[:, i, :], sg[:, i, :], su[:, i, :], ALU.mult).then_inc(sa_ok, 1)

            def add(b):
                wait(pool, so_ok, b(2, 2))
                pool.tensor_tensor(x_sb[:, tiles(b), :], x_sb[:, tiles(b), :], so[:, :, :], ALU.add).then_inc(r_ok, 1)

            act(Step(None, 0, 0))
            for n in shared(pool, 1, NG):
                act(n)
                add(n.before(1))
            pool.wait_ge(idx_ok, 1)
            pool.wait_ge(w_st, 16)
            pool.wait_ge(consts, 16 * N2)
            for j in range(CJ):
                pool.indirect_dma_start(out=xg[:, j, :], out_offset=None, in_=io["rows"][:, :],
                                        in_offset=bass.IndirectOffsetOnAxis(ap=idx[:, j:j + 1], axis=0)).then_inc(gath, 16)
            add(Step(None, 0, NG - 1))

        @block.scalar
        def _(act):
            def gate_up(n):
                for i in range(NSX):
                    wait(act, gu_mm, n(2 * NSX, 2 * i + 1))
                    if i == 0:
                        wait(act, sa_ok, n(NSX))
                        wait(act, dn_mm, n(2))
                    act.activation(sg[:, i, :], mm[(2 * i) % 4][:, :], ACT.Silu).then_inc(sg_ok, 1)
                    wait(act, gu_mm, n(2 * NSX, 2 * i + 2))
                    act.activation(su[:, i, :], mm[(2 * i + 1) % 4][:, :], ACT.Copy).then_inc(su_ok, 1)

            def down(b):
                wait(act, r_ok, b(1))
                for j in range(2):
                    wait(act, dn_mm, b(2, j + 1))
                    act.activation(so[:, 2 * j:2 * j + 2, :], ro[j][:, :, :], ACT.Copy).then_inc(so_ok, 1)

            gate_up(Step(None, 0, 0))
            for lo, hi in ((1, HALF), (HALF, NG)):
                for n in shared(act, lo, hi):
                    down(n.before(1))
                    gate_up(n)
                if lo == 1:
                    act.wait_ge(sub_ok, 1)
                    act.activation(ex, ex, ACT.Exp).then_inc(exp_ok, 1)
            down(Step(None, 0, NG - 1))
            with act.Fori(0, E // RING) as r:
                for i in range(RING):
                    act.wait_ge(egu_mm, r * RING + (i + 1))
                    if i >= 2:
                        act.wait_ge(ea_ok, r * RING + (i - 1))
                    else:
                        act.wait_ge(ea_ok, r * RING)
                    act.activation(eg[:, i % 2, :, :],
                                   mm[i % 4][0:IX, 0:NIX * CAP].rearrange("p (a c) -> p a c", a=NIX), ACT.Silu).then_inc(eg_ok, 1)
                    act.wait_ge(edn_mm, r * RING + (i + 1))
                    act.activation(yT[:, :, :, bass.ds(r * RING + i, 1)].rearrange("p k c e -> p k (c e)"),
                                   ro[i % 2][:, 0, 0:KD * CAP].rearrange("p (k c) -> p k c", k=KD), ACT.Copy).then_inc(ey_ok, 1)

        @block.vector
        def _(dve):
            step = [0]

            def then(ins):
                step[0] += 1
                ins.then_inc(rt, 1)
                dve.wait_ge(rt, step[0])

            dve.memset(gm[:, :, EG:], LOW)
            dve.memset(sc[:, :, E:], LOW)
            dve.memset(pre[0][:, 0:NT // 2, :], 0.0)
            dve.memset(pre[1][:, 0:NT // 2, :], 0.0)
            then(dve.tensor_reduce(gm[:, :, 0:EG], logits[:, :, :].rearrange("p t (g m) -> p t g m", g=EG), AX.X, ALU.max))
            for t in range(NT):
                last = dve.max(t8[:, t, :], gm[:, t, 0:EG])
            then(last)
            then(dve.memset(t8[:, :, TOPG:], LOW))
            for t in range(NT):
                last = dve.match_replace(gr[:, t, :], t8[:, t, :], gm[:, t, :], TAKEN)
            then(last)
            then(dve.tensor_scalar(kept, gr[:, :, 0:EG], TAKEN, None, ALU.is_equal))
            then(dve.tensor_tensor(wt.rearrange("p t (g m) -> p (t g) m", g=EG),
                                   logits[:, :, :].rearrange("p t (g m) -> p (t g) m", g=EG),
                                   kept.rearrange("p t g -> p (t g)").unsqueeze(2).to_broadcast([P, NT * EG, E // EG]), ALU.mult))
            then(dve.tensor_scalar(sc[:, :, 0:E], wt, 0.0, None, ALU.add))
            for t in range(NT):
                last = dve.max(t8b[:, t, :], sc[:, t, 0:E])
            then(last)
            dve.tensor_tensor(ex, sc[:, :, 0:E], t8b[:, :, 0:1].to_broadcast([P, NT, E]), ALU.subtract).then_inc(sub_ok, 1)
            then(dve.memset(t8b[:, :, TOPK:], LOW))
            for t in range(NT):
                last = dve.match_replace(sr[:, t, :], t8b[:, t, :], sc[:, t, :], TAKEN)
            then(last)
            then(dve.tensor_scalar(sel[:, :, :], sr[:, :, 0:E], TAKEN, None, ALU.is_equal))
            dve.tensor_copy(selr[:, :, :, :], sel[:, :, :].unsqueeze(2).to_broadcast([P, NT, CG, E])).then_inc(pre_ok, 1)
            dve.tensor_copy(pre[0][:, NT // 2:, :], sel[:, :, :]).then_inc(pre_ok, 1)
            for d in range(5):
                dve.wait_ge(pre_ok, 2 + d)
                a, b = pre[d % 2], pre[(d + 1) % 2]
                dve.tensor_tensor(b[:, NT // 2:, :], a[:, NT // 2:, :],
                                  a[:, NT // 2 - (1 << d):NT // 2 + NT - (1 << d), :], ALU.add).then_inc(pre_ok, 1)
            dve.wait_ge(pre_ok, 7)
            dve.tensor_copy(prer[:, :, :, :],
                            pre[1][:, NT // 2 - 1:NT // 2 - 1 + NT, :].unsqueeze(2).to_broadcast([P, NT, CG, E])).then_inc(pre_ok, 1)
            dve.wait_ge(exp_ok, 1)
            dve.tensor_reduce(rsum[:], ex, AX.X, ALU.add).then_inc(mset, 1)
            dve.wait_ge(mset, 1)
            dve.reciprocal(rden[:], rsum[:]).then_inc(mset, 1)
            dve.wait_ge(mset, 2)
            dve.tensor_tensor(wt, ex, rden[:, :].unsqueeze(2).to_broadcast([P, NT, E]), ALU.mult).then_inc(mset, 1)
            dve.wait_ge(mset, 3)
            then(dve.scalar_tensor_tensor(wt, wt, SCALE_MOE, sel[:, :, :], ALU.mult, ALU.mult))
            assert step[0] == 12
            for g in range(NG):
                dve.wait_ge(cum_mm, g + 1)
                dve.tensor_copy(cum[:, g * GTOK:(g + 1) * GTOK], tp[g % 2][:, :]).then_inc(cum_ok, 1)
            dve.wait_ge(cum_ok, NG)
            dve.wait_ge(consts, 16 * N2)
            dve.memset(busy_f[:, 0:1], 1.0)
            dve.tensor_scalar(busy_f[:, 1:], cum[:, 0:TOK].rearrange("p (t c) -> p t c", c=P)[:, 0:NT - 1, P - 1],
                              float(CAP), None, ALU.is_lt).then_inc(cnt_ok, 1)
            for j in range(CJ):
                dve.wait_ge(cnt_ok, j + 1)
                dve.tensor_scalar(dump, cum[:, :], place[:, j:j + 1], 0.0, ALU.is_le, ALU.add,
                                  accum_out=cnt[:, j:j + 1]).then_inc(cnt_ok, 1)
            dve.wait_ge(cnt_ok, CJ + 1)
            dve.tensor_copy(idx[:, :], cnt[:, :]).then_inc(idx_ok, 1)
            dve.wait_ge(busy_mm, 1)
            dve.tensor_copy(busy[:, :], tp[0][0:1, 0:NT]).then_inc(busy_ok, 1)
            dve.wait_ge(gath, 16 * CJ)
            dve.tensor_tensor(wtmp[:, :, :], xg[:, :, D:ROW], mine[:, :].unsqueeze(1).to_broadcast([P, CJ, E]), ALU.mult).then_inc(ws_ok, 1)
            dve.wait_ge(ws_ok, 1)
            dve.tensor_reduce(w_slot[:, :], wtmp[:, :, :], AX.X, ALU.add).then_inc(ws_ok, 1)
            for j in range(CJ):
                for k in range(KD):
                    m = j * KD + k
                    dve.wait_ge(tr_ok, m + 1)
                    dve.tensor_copy(xgT[:, k, :, j * CG:(j + 1) * CG].rearrange("p e c -> p c e"),
                                    tp[m % 2][:, 0:P].rearrange("p (c e) -> p c e", c=CG)).then_inc(xg_ok, 1)
            with dve.Fori(0, E // RING) as r:
                for i in range(RING):
                    dve.wait_ge(eg_ok, r * RING + (i + 1))
                    dve.wait_ge(edn_mm, r * RING + max(i - 1, 0))
                    dve.tensor_tensor(ea[:, i % 2, :, :], eg[:, i % 2, :, :],
                                      mm[i % 4][0:IX, NIX * CAP:2 * NIX * CAP].rearrange("p (a c) -> p a c", a=NIX),
                                      ALU.mult).then_inc(ea_ok, 1)
            dve.wait_ge(ws_ok, 2)
            for j in range(CJ):
                dve.wait_ge(ty_ok, j + 1)
                dve.tensor_scalar(y[:, j, :], tp[j % 2][:, 0:D], w_slot[:, j:j + 1], None, ALU.mult).then_inc(y_ok, 1)

        @block.tensor
        def _(pe):
            def gate_up(n):
                for c in range(2 * NSX):
                    if c == 0:
                        wait(pe, su_ok, n(NSX))
                    if c >= 4:
                        wait(pe, sg_ok if c % 2 == 0 else su_ok, n(NSX, (c - 4) // 2 + 1))
                    col = (c // 2 + (c % 2) * NSX) * P
                    for k in range(KD):
                        last = pe.matmul(mm[c % 4][:, :], ws_gu[:, k, col:col + P],
                                         xT[:, k, bass.ds(n(GTOK), GTOK)], start=(k == 0), stop=(k == KD - 1))
                    last.then_inc(gu_mm, 1)

            def down(b):
                wait(pe, sa_ok, b(NSX, NSX))
                wait(pe, so_ok, b(2))
                for t in range(GT):
                    for k in range(NSX):
                        last = pe.matmul(ro[t // 2][:, t % 2, :], su[:, k, t * P:(t + 1) * P], ws_dn[:, k, :],
                                         start=(k == 0), stop=(k == NSX - 1))
                    if t % 2:
                        last.then_inc(dn_mm, 1)

            pe.wait_ge(consts, 16 * N2)
            gate_up(Step(None, 0, 0))
            for lo, hi in ((1, HALF), (HALF, NG)):
                for n in shared(pe, lo, hi):
                    down(n.before(1))
                    gate_up(n)
                if lo == 1:
                    pe.wait_ge(pre_ok, 8)
                    for t in range(NT):
                        g = t // GT
                        if t % GT == 0 and g >= 2:
                            pe.wait_ge(cum_ok, g - 1)
                        o = tp[g % 2][:, (t % GT) * P:(t % GT + 1) * P]
                        pe.matmul(o, selr[:, t, :, :].rearrange("p c e -> p (c e)"), upper[:], start=True, stop=False)
                        last = pe.matmul(o, prer[:, t, :, :].rearrange("p c e -> p (c e)"), ones[:], start=False, stop=True)
                        if t % GT == GT - 1:
                            last.then_inc(cum_mm, 1)
            down(Step(None, 0, NG - 1))
            pe.wait_ge(cnt_ok, 1)
            pe.wait_ge(cum_ok, NG)
            pe.matmul(tp[0][0:1, 0:NT], ones_f[:, 0:1], busy_f[:, :], start=True, stop=True).then_inc(busy_mm, 1)
            pe.wait_ge(busy_ok, 1)
            pe.wait_ge(gath, 16 * CJ)
            for j in range(CJ):
                for k in range(KD):
                    m = j * KD + k
                    if m >= 2:
                        pe.wait_ge(xg_ok, m - 1)
                    pe.transpose(tp[m % 2][:, 0:P], xg[:, j, k * P:(k + 1) * P], ident[:]).then_inc(tr_ok, 1)
            pe.wait_ge(xg_ok, CJ * KD)
            pe.wait_ge(so_ok, 2 * NG)

            def expert_gu(e, i):
                pe.wait_ge(ring[i], e[1])
                pe.wait_ge(ea_ok, e[2])
                for c in range(2 * NIX):
                    for k in range(KD):
                        last = pe.matmul(mm[i % 4][0:IX, c * CAP:(c + 1) * CAP], we_gu[:, i, k, c * IX:(c + 1) * IX],
                                         xgT[:, k, bass.ds(e[0], 1), :].rearrange("p e c -> p (e c)"),
                                         start=(k == 0), stop=(k == KD - 1))
                last.then_inc(egu_mm, 1)

            def expert_down(count, i):
                pe.wait_ge(ea_ok, count(1))
                pe.wait_ge(ey_ok, count(-1))
                for f in range(KD):
                    for k in range(NIX):
                        last = pe.matmul(ro[i % 2][:, 0, f * CAP:(f + 1) * CAP], we_dn[:, i, k, f * P:(f + 1) * P],
                                         ea[:, i % 2, k, :], start=(k == 0), stop=(k == NIX - 1))
                last.then_inc(edn_mm, 1)

            with pe.Fori(0, E // RING) as r:
                for i in range(RING):
                    expert_gu((r * RING + i, r * 32 + 32, r * RING + max(i - 3, 0)), i)
                    if i >= 1:
                        expert_down(lambda d: r * RING + (i - 1 + d) if i - 1 + d > 0 else r * RING, i - 1)
                expert_down(lambda d: r * RING + (RING - 1 + d), RING - 1)
            pe.wait_ge(ey_ok, E)
            for j in range(CJ):
                if j >= 2:
                    pe.wait_ge(y_ok, j - 1)
                for k in range(KD):
                    last = pe.transpose(tp[j % 2][:, k * P:(k + 1) * P],
                                        yT[:, k, j * CG:(j + 1) * CG, :].rearrange("p c e -> p (c e)"), ident[:])
                last.then_inc(ty_ok, 1)

        inner.close()

        hot = [xT[:, 0, i * CJ * P:(i + 1) * CJ * P].rearrange("p (j c) -> p j c", j=CJ) for i in range(2)]

        def busy_tiles(eng):
            with eng.Fori(0, NT // 8) as o:
                with eng.If(eng.value_load(busy[0:1, bass.ds(o * 8, 1)], min_val=0, max_val=P) > 0):
                    with eng.Fori(0, 4) as m:
                        r = o * 4 + m
                        for i in range(2):
                            t = Step(r, 2, i)
                            with eng.If(eng.value_load(busy[0:1, bass.ds(t(1), 1)], min_val=0, max_val=P) > 0):
                                yield r, i, t

        block = ctx.enter_context(nc.Block())

        @block.vector
        def _(dve):
            dve.tensor_tensor(rel[:, :, :], cnt[:, :].unsqueeze(1).to_broadcast([P, NT, CJ]),
                              base[:, :].unsqueeze(2).to_broadcast([P, NT, CJ]), ALU.subtract).then_inc(rel_ok, 1)
            dve.wait_ge(rel_ok, 1)
            for r, i, t in busy_tiles(dve):
                dve.wait_ge(cb_mm, r * 2)
                dve.tensor_tensor(hot[i], rel[:, bass.ds(t(1), 1), :].rearrange("p a j -> p (a j)")
                                  .unsqueeze(2).to_broadcast([P, CJ, P]),
                                  lane[:, :].unsqueeze(1).to_broadcast([P, CJ, P]), ALU.is_equal).then_inc(oh_ok, 1)
                dve.wait_ge(cb_mm, t(1, 1))
                xt = x_sb[:, bass.ds(t(1), 1), :].rearrange("p a b -> p (a b)")
                dve.tensor_tensor(xt, ro[i][:, 0, :], xt, ALU.add).then_inc(cb_ok, 1)

        @block.tensor
        def _(pe):
            for r, i, t in busy_tiles(pe):
                pe.wait_ge(oh_ok, t(1, 1))
                pe.wait_ge(cb_ok, r * 2)
                for j in range(CJ):
                    last = pe.matmul(ro[i][:, 0, :], hot[i][:, j, :], y[:, j, :],
                                     start=(j == 0), stop=(j == CJ - 1))
                last.then_inc(cb_mm, 1)


NB = 4
ST = NT // NB
SEQ = ST * P
HEADS = 16
HD = D // HEADS
HG = 4
NHG = HEADS // HG
HALF_D = HD // 2
BLK = 64
HALF_AT = 3
DOWN_AT = 13
MASKED = -1.0e30
NLN = 6
ROOM = 11776
LEAD = 4

Q_PARTS = (0, 1, 0, 1, 0, 2)
K_PARTS = (0, 1, 1, 0, 2, 0)
assert len(Q_PARTS) == len(K_PARTS)
FM = len(Q_PARTS) * HD
FW = FM + 3

BLOCKS = [(j, i) for j in range(ST) for i in range(j, ST)]
UB = 4
NU = len(BLOCKS) // UB
POOL_UNITS = (0, 1, 2, 3, 5, 7)
NPU = len(POOL_UNITS)
NVU = NU - NPU
RING = 4


def runs(u):
    out = []
    for n, (j, i) in enumerate(BLOCKS[UB * u:UB * u + UB]):
        if i > j and out and out[-1][1] == j and not out[-1][4]:
            out[-1][3] += 1
        else:
            out.append([n, j, i, 1, i == j])
    return out


class Chain:

    def __init__(self, eng, sem, n, per):
        self.eng, self.sem, self.n, self.per, self.k = eng, sem, n, per, 0

    def then(self, ins):
        self.k += 1
        ins.then_inc(self.sem, 1)
        wait(self.eng, self.sem, self.n(self.per, self.k))

    def end(self):
        assert self.k == self.per, (self.k, self.per)


def head_steps(eng, b, run):
    for k in (-2, -1):
        run(Step(b, HEADS, k), 0, k, 2)
    with eng.Fori(0, NHG - 1) as g:
        for k in range(HG):
            run(Step(b * HEADS + g * HG, 1, k), g, k, 2)
    for k in range(HG):
        run(Step(b, HEADS, (NHG - 1) * HG + k), NHG - 1, k, min(2, HG - 1 - k))


def attention_ffn_phase(nc, io, keep):
    with ExitStack() as ctx:
        kit = Kit(nc, ctx)
        sb, ps = kit.sb, kit.ps
        x_sb, ident = keep["x_sb"], keep["ident"]

        w_qkv = sb("w_qkv", [P, KD, NHG, 3 * HG * HD])
        w_o = sb("w_o", [P, KD, D])
        w_fg = sb("w_fg", [P, KD, DF])
        w_fu = sb("w_fu", [P, KD, DF])
        w_fd = sb("w_fd", [P, NF, D])
        cos = sb("cos", [P, ST, HALF_D])
        sin = sb("sin", [P, ST, HALF_D])
        mask = sb("mask", [P, 2])
        ident_b = sb("ident_b", [P, P], BF16)
        power = sb("power3", [P, GT])
        eps = sb("eps3", [P, GT])
        xb = sb("xb", [P, ST, D])
        xbT = sb("xbT", [P, KD, SEQ])
        v = sb("v", [P, ST, HEADS, 2 * HD + 1], F16)
        qks = sb("qks", [P, ST, NHG * 2 * HG, FW], BF16)
        nm = sb("nm", [P, ST])
        o1 = sb("o1", [P, ST, HD])
        o = sb("o", [P, ST, HD])
        rc = sb("rc", [P, ST])
        ctok = sb("ctok", [P, ST, D])
        sgl = sb("sgl", [P, 2, 512])
        nb = sb("nb", [P, 4, 512], BF16)
        ot = sb("ot", [P, GT, D])
        bn = sb("bn3", [P, GT, 6])
        mv = sb("mv3", [P, GT, 2])
        ve = sb("ve3", [P, GT])
        rs = sb("rs3", [P, GT])

        room = sb("room", [P, ROOM])
        used = [0]

        def carve(words, dt=F32):
            a = room[:, used[0]:used[0] + words]
            used[0] += words
            assert used[0] <= ROOM
            return a if dt == F32 else a.bitcast(dt)

        qk = carve(ST * 2 * HG * HD).rearrange("p (t h d) -> p t h d", t=ST, h=2 * HG)
        ro = carve(ST * 2 * HG * HD).rearrange("p (t h d) -> p t h d", t=ST, h=2 * HG)
        rest = carve(ST * 2 * HG * HD).rearrange("p (t h d) -> p t h d", t=ST, h=2 * HG)
        r1 = [carve(ST * 2 * HG * HALF_D).rearrange("p (t h d) -> p t h d", t=ST, h=2 * HG) for i in range(4)]
        q1T = carve(SEQ // 2, BF16)
        q2T = [carve(SEQ // 2, BF16) for i in range(2)]
        kT = [carve(SEQ // 2, BF16) for i in range(4)]
        used[0] = 0
        pf = [carve(512) for i in range(3)]
        p1 = [carve(256, F16) for i in range(RING)]
        p2 = [carve(256, F16) for i in range(RING)]
        used[0] = 0
        hs = carve(3 * 4 * 512).rearrange("p (k c) -> p k c", k=12)
        hj = carve(4 * 512).rearrange("p (k c) -> p k c", k=4)
        aj = carve(4 * 512).rearrange("p (k c) -> p k c", k=4)
        ge = carve(6 * 256, BF16).rearrange("p (k c) -> p k c", k=6)

        S = [ps(f"s{i}", [P, 2, 512]) for i in range(3)]
        C = ps("c", [P, 512])
        M = ps("m", [P, 512])
        half_banks = ((S[2][:, 0, :], S[2][:, 1, :]), (C[:, :], M[:, :]))
        X = S[0:2]
        W = [S[2][:, i, :] for i in range(2)]
        T = C[:, :].bitcast(BF16)
        O = M[:, :].rearrange("p (t c) -> p t c", t=ST)[:, :, 0:2 * HD + 1]

        (consts, late, setup, ready, passed, passed_pe, bn_ok, mv_ok, ve_ok, rs_ok, ln_ok, xb_ok, tx, xTv_ok, xTa_ok, qkv_mm, qkv_ok, v2_ok, rope_v,
         rope_p, rv_ok, rp_ok, a_ok, r_ok, b_ok, rest_ok, ca_ok, tk_mm, k_ok, tq_mm, q1_ok, tm_mm, q2_ok, max_mm,
         mx_ok, nm1_ok, nm_ok, sc_mm, exp_ok, p2v_ok, p2p_ok, pv_mm, o_ok, rc_ok, cn_ok,
         tc, cTv_ok, cTa_ok, wo_mm, xr_ok, ff_mm, sl_ok, hm_ok, ab_ok, sp, hs_ok, fd_mm, f2_ok, out_st) = kit.sems(
            "consts3 ffn_weights3 setup3 rows_set_up3 passed3 passed3_pe bn3_ready mv3_ready ve3_ready rs3_ready layernorm_done x_copied x_transposed "
            "xT_low_ready xT_high_ready qkv_done qkv_ready v_part2_ready rope_step_v rope_step_p rope_low_ready rope_high_ready "
            "part1_ready rest_ready part2_ready part3_ready part_copies_ready k_transposed kT_ready q_transposed "
            "qT_ready q_max_transposed qT_max_ready max_scores_done maxima_ready max_part1_ready max_parts_ready "
            "scores_done weights_ready part2_by_vector part2_by_gpsimd weighted_done sums_joined sums_copied context_ready ctx_transposed "
            "cT_low_ready cT_high_ready wo_done attn_residual_ready ffn_in_done silu_ready hidden_ready abs_ready "
            "sparse_step sparse_ready ffn_down_done ffn_residual_ready out_stored")

        block = ctx.enter_context(nc.Block())

        def x_tile(n, t):
            return x_sb[:, bass.ds(n(ST, t), 1), :].rearrange("p a b -> p (a b)")

        def part(g, s, f):
            heads = bass.ds(g * (2 * HG) + (s or 0) * HG, HG if s is not None else 2 * HG)
            return qks[:, :, heads, f * HD:(f + 1) * HD]

        def rows_of(g, k, s, t):
            at = (g + k // HG) * (2 * HG) + s * HG + k % HG
            return qks[:, t, bass.ds(at, 1), :].rearrange("p a f -> p (a f)")

        def second_part(eng, h, k, u, done, per, i):
            wait(eng, exp_ok, h(NU, LEAD + u + 1))
            wait(eng, pv_mm, h(NU, LEAD + u + 1 - RING))
            at = (k * NU + u) % RING
            eng.tensor_tensor(p2[at], pf[u % 3], p1[at], ALU.subtract).then_inc(done, 1)

        @block.sync
        def _(sync):
            for src, dst in (("mask", mask), ("cos", cos), ("sin", sin), ("w_qkv", w_qkv),
                             ("w_o", w_o), ("w_fg", w_fg), ("w_fu", w_fu), ("w_fd", w_fd)):
                sync.dma_start(dst[:], io[src]).then_inc(late if dst in (w_o, w_fg, w_fu, w_fd) else consts, 16)
            with sync.Fori(0, NB) as b:
                n = Step(b, 1, 0)
                for g in range(2):
                    wait(sync, ln_ok, n(NLN, 2 + (3, 6)[g]))
                    sync.dma_start(io["out"][:, bass.ds(n(ST, g * GT), GT), :], ot[:, :, :]).then_inc(out_st, 16)
            sync.wait_ge(out_st, 16 * 2 * NB)

        @block.gpsimd
        def _(pool):
            def inverse_deviation(n, k):
                wait(pool, mv_ok, n(NLN, k + 1))
                wait(pool, rs_ok, n(NLN, k))
                pool.tensor_tensor(ve[:], mv[:, :, 1], eps[:], ALU.add).then_inc(ve_ok, 1)
                wait(pool, ve_ok, n(NLN, k + 1))
                wait(pool, ln_ok, n(NLN, k))
                pool.tensor_tensor(rs[:], ve[:], power[:], ALU.pow).then_inc(rs_ok, 1)

            pool.sem_inc(p2p_ok, LEAD)
            pool.memset(power[:], -0.5)
            pool.memset(eps[:], 1e-5).then_inc(setup, 1)
            pool.wait_ge(setup, 1)
            for k in range(2):
                inverse_deviation(Step(None, 0, 0), k)
            pool.memset(v[:, :, :, HD:HD + 1], 1.0).then_inc(setup, 1)
            pool.memset(qks[:, :, :, FM:FM + 2], 1.0).then_inc(setup, 1)
            pool.wait_ge(setup, 3)
            pool.wait_ge(consts, 16 * 4)

            with pool.Fori(0, NB) as b:
                n = Step(b, 1, 0)
                for g in range(NHG):
                    pool.memset(qks[:, :, g * 2 * HG:g * 2 * HG + HG, FM:FM + 2], 0.0)
                with pool.Fori(0, NHG) as g:
                    q = Step(b * NHG + g, 1, 0)
                    x1, x2 = qk[:, :, :, 0:HALF_D], qk[:, :, :, HALF_D:]
                    wait(pool, qkv_ok, q(2, 2))
                    wait(pool, rp_ok, q(1))
                    pool.tensor_tensor(r1[2], x2, cos[:, :, :].unsqueeze(2).to_broadcast([P, ST, 2 * HG, HALF_D]),
                                       ALU.mult).then_inc(rope_p, 1)
                    pool.tensor_tensor(r1[3], x1, sin[:, :, :].unsqueeze(2).to_broadcast([P, ST, 2 * HG, HALF_D]),
                                       ALU.mult).then_inc(rope_p, 1)
                    wait(pool, rope_p, q(2, 2))
                    wait(pool, a_ok, q(1))
                    wait(pool, r_ok, q(1))
                    pool.tensor_tensor(ro[:, :, :, HALF_D:HD], r1[2], r1[3], ALU.add).then_inc(rp_ok, 1)

                def run(h, g, k, ahead):
                    if k >= 0:
                        for i, u in enumerate(POOL_UNITS):
                            second_part(pool, h, k, u, p2p_ok, NPU, i)

                head_steps(pool, b, run)
                for k in range(2, 2 + NLN):
                    inverse_deviation(n, k)

        @block.scalar
        def _(act):
            act.sem_inc(exp_ok, LEAD)
            act.wait_ge(setup, 3)
            act.wait_ge(ready, 1)
            with act.Fori(0, NB) as b:
                n = Step(b, 1, 0)
                for g in range(2):
                    wait(act, ln_ok, n(NLN, 1 + g))
                    act.activation(xb[:, g * GT:(g + 1) * GT, :], x_sb[:, bass.ds(n(ST, g * GT), GT), :],
                                   ACT.Copy).then_inc(xb_ok, 1)
                for s in range(2):
                    wait(act, tx, n(8, 2 * s + 2))
                    act.activation(xbT[:, 1, s * 512:(s + 1) * 512], half_banks[s][1], ACT.Copy).then_inc(xTa_ok, 1)
                def copies(q, g):
                    for s in range(2):
                        wait(act, qkv_mm, q(2, s + 1))
                        wait(act, rv_ok, q(1))
                        wait(act, rp_ok, q(1))
                        wait(act, fd_mm, n(4))
                        src = S[s][:, :, :].rearrange("p a (t c) -> p (a t) c", t=2)
                        act.activation(qk[:, s * GT:(s + 1) * GT, :, :].rearrange("p t h d -> p t (h d)"),
                                       src[:, :, 0:2 * HG * HD], ACT.Copy)
                        act.activation(v[:, s * GT:(s + 1) * GT, g * HG:(g + 1) * HG, 0:HD],
                                       src[:, :, 2 * HG * HD:3 * HG * HD].rearrange("p t (h d) -> p t h d", h=HG),
                                       ACT.Copy).then_inc(qkv_ok, 1)

                def first_parts(q, g):
                    wait(act, rv_ok, q(1, 1))
                    wait(act, rp_ok, q(1, 1))
                    act.activation(part(g, None, 0), ro, ACT.Copy).then_inc(a_ok, 1)

                def second_parts(q, g):
                    wait(act, r_ok, q(1, 1))
                    act.activation(part(g, None, 1), rest, ACT.Copy).then_inc(b_ok, 1)
                    wait(act, a_ok, q(1, 1))
                    for f in (3, 5):
                        act.activation(part(g, 1, f), part(g, 1, 0), ACT.Copy)
                    wait(act, b_ok, q(1, 1))
                    act.activation(part(g, 1, 2), part(g, 1, 1), ACT.Copy).then_inc(ca_ok, 1)

                copies(Step(b, NHG, 0), 0)
                for g in range(NHG):
                    first_parts(Step(b, NHG, g), g)
                    if g + 1 < NHG:
                        copies(Step(b, NHG, g + 1), g + 1)
                    second_parts(Step(b, NHG, g), g)

                def run(h, g, k, ahead):
                    for u in range(NU):
                        if k >= 0:
                            wait(act, sc_mm, h(NU, u + 1))
                            by_pool = sum(w <= u - 3 for w in POOL_UNITS) - sum(w > NU + u - 3 for w in POOL_UNITS)
                            wait(act, p2p_ok, h(NPU, LEAD + by_pool))
                            wait(act, p2v_ok, h(NVU, LEAD + u - 2 - by_pool))
                            wait(act, pv_mm, h(NU, LEAD + u + 1 - RING))
                            at = (k * NU + u) % RING
                            act.activation(pf[u % 3], W[(k * NU + u) % 2], ACT.Exp, scale=HD ** -0.5)
                            act.activation(p1[at], W[(k * NU + u) % 2], ACT.Exp, scale=HD ** -0.5).then_inc(exp_ok, 1)
                        if u == 6 and k >= -1 and ahead >= 1:
                            wait(act, tm_mm, h(1, 2))
                            act.activation(q2T[(k + 1) % 2][0:FW, :], T[0:FW, :], ACT.Copy).then_inc(q2_ok, 1)

                head_steps(act, b, run)
                wait(act, tc, n(2, 2))
                wait(act, qkv_mm, n(2 * NHG, 2 * NHG))
                act.activation(xbT[:, 1, :].rearrange("p (a c) -> p a c", a=2), S[1][:, :, :], ACT.Copy).then_inc(cTa_ok, 1)

                def second_chunk(s):
                    wait(act, tx, n(8, 4 + 2 * s + 2))
                    act.activation(xbT[:, 1, s * 512:(s + 1) * 512], half_banks[s][1], ACT.Copy).then_inc(xTa_ok, 1)

                wait(act, wo_mm, n(2, 1))
                second_chunk(0)
                for w in range(17):
                    if w == HALF_AT:
                        second_chunk(1)
                    if w < 16:
                        wait(act, ff_mm, n(16, w + 1))
                        wait(act, hm_ok, n(16, max(w - 1, 0)))
                        act.activation(sgl[:, w % 2, :], S[w % 3][:, 0, :], ACT.Silu).then_inc(sl_ok, 1)
                    if w >= 1:
                        wait(act, hm_ok, n(16, w))
                        wait(act, hs_ok, n(4, (w - 1) // 4))
                        act.activation(aj[:, (w - 1) % 4, :], hj[:, (w - 1) % 4, :], ACT.Abs).then_inc(ab_ok, 1)

        @block.vector
        def _(dve):
            dve.sem_inc(mx_ok, LEAD)
            dve.sem_inc(cn_ok, LEAD)
            dve.sem_inc(p2v_ok, LEAD)
            def layernorm(n, k, src, dst):
                wait(dve, mv_ok, n(NLN, k))
                for t in range(GT):
                    last = dve.bn_stats(bn[:, t, :], src(t))
                last.then_inc(bn_ok, 1)
                wait(dve, bn_ok, n(NLN, k + 1))
                wait(dve, ln_ok, n(NLN, k))
                dve.sem_inc(passed, 1)
                for t in range(GT):
                    last = dve.bn_aggr(mv[:, t, :], bn[:, t, :])
                last.then_inc(mv_ok, 1)
                wait(dve, mv_ok, n(NLN, k + 1))
                wait(dve, rs_ok, n(NLN, k + 1))
                for t in range(GT):
                    last = dve.tensor_scalar(dst(t), src(t), mv[:, t, 0:1], rs[:, t:t + 1], ALU.subtract, ALU.mult)
                last.then_inc(ln_ok, 1)

            for g in range(2):
                layernorm(Step(None, 0, 0), g, lambda t: x_sb[:, g * GT + t, :], lambda t: x_sb[:, g * GT + t, :])
            dve.wait_ge(consts, 16 * 4)
            dve.wait_ge(setup, 3)
            dve.tensor_copy(ident_b[:, :], ident[:, :])
            by_group = qks[:, :, :, FW - 1].rearrange("p t (g s h) -> p t g s h", g=NHG, s=2)
            for g in range(NHG):
                for s in range(2):
                    last = dve.tensor_copy(by_group[:, :, g, s, :],
                                           mask[:, s:s + 1].unsqueeze(2).to_broadcast([P, ST, HG]))
            last.then_inc(ready, 1)
            dve.wait_ge(ready, 1)
            with dve.Fori(0, NB) as b:
                n = Step(b, 1, 0)
                for s in range(2):
                    wait(dve, tx, n(8, 2 * s + 1))
                    dve.tensor_copy(xbT[:, 0, s * 512:(s + 1) * 512], half_banks[s][0]).then_inc(xTv_ok, 1)
                def rotate_steps(q, g):
                    x1, x2 = qk[:, :, :, 0:HALF_D], qk[:, :, :, HALF_D:]
                    wait(dve, qkv_ok, q(2, 2))
                    for s in range(2):
                        own = v[:, s * GT:(s + 1) * GT, g * HG:(g + 1) * HG, :]
                        exact = S[s][:, :, :].rearrange("p a (t c) -> p (a t) c", t=2)[:, :, 2 * HG * HD:3 * HG * HD]
                        last = dve.tensor_tensor(own[:, :, :, HD + 1:], exact.rearrange("p t (h d) -> p t h d", h=HG),
                                                 own[:, :, :, 0:HD], ALU.subtract)
                    last.then_inc(v2_ok, 1)
                    wait(dve, rv_ok, q(1))
                    dve.tensor_tensor(r1[0], x1, cos[:, :, :].unsqueeze(2).to_broadcast([P, ST, 2 * HG, HALF_D]),
                                      ALU.mult).then_inc(rope_v, 1)
                    dve.tensor_tensor(r1[1], x2, sin[:, :, :].unsqueeze(2).to_broadcast([P, ST, 2 * HG, HALF_D]),
                                      ALU.mult).then_inc(rope_v, 1)

                def rotate(q, g):
                    wait(dve, rope_v, q(2, 2))
                    wait(dve, a_ok, q(1))
                    wait(dve, r_ok, q(1))
                    dve.tensor_tensor(ro[:, :, :, 0:HALF_D], r1[0], r1[1], ALU.subtract).then_inc(rv_ok, 1)

                def without_first(q, g):
                    wait(dve, a_ok, q(1, 1))
                    wait(dve, rp_ok, q(1, 1))
                    wait(dve, rest_ok, q(1))
                    dve.tensor_tensor(rest, ro, part(g, None, 0), ALU.subtract).then_inc(r_ok, 1)

                def third_parts(q, g):
                    wait(dve, b_ok, q(1, 1))
                    wait(dve, r_ok, q(1, 1))
                    dve.tensor_tensor(part(g, 0, 5), rest[:, :, 0:HG, :], part(g, 0, 1), ALU.subtract)
                    dve.tensor_tensor(part(g, 1, 4), rest[:, :, HG:, :], part(g, 1, 1), ALU.subtract)
                    for f, first in ((2, 0), (4, 0), (3, 1)):
                        last = dve.tensor_copy(part(g, 0, f), part(g, 0, first))
                    last.then_inc(rest_ok, 1)

                rotate_steps(Step(b, NHG, 0), 0)
                rotate(Step(b, NHG, 0), 0)
                for g in range(NHG):
                    without_first(Step(b, NHG, g), g)
                    if g + 1 < NHG:
                        rotate_steps(Step(b, NHG, g + 1), g + 1)
                        rotate(Step(b, NHG, g + 1), g + 1)
                    third_parts(Step(b, NHG, g), g)

                def step(h, g, k, ahead):
                    def maximum(of, i):
                        wait(dve, max_mm, h(ST, ST * of + i + 1))
                        if i == 0:
                            wait(dve, nm_ok, h(1, of))
                        x = X[i % 2][:, :, :].rearrange("p a c -> p (a c)")
                        dve.tensor_reduce(nm[:, i:i + 1], x[:, 0:(i + 1) * P], AX.X, ALU.max,
                                          negate=True).then_inc(mx_ok, 1)

                    def max_parts():
                        own = bass.ds((g + (k + 1) // HG) * (2 * HG) + (k + 1) % HG, 1)
                        wait(dve, mx_ok, h(ST, LEAD + 2 * ST))
                        wait(dve, tq_mm, h(1, 2))
                        parts = [qks[:, :, own, FM + c] for c in range(2)]
                        nm2 = nm[:, :].unsqueeze(2)
                        dve.tensor_copy(parts[0], nm2).then_inc(nm1_ok, 1)
                        wait(dve, nm1_ok, h(1, 2))
                        dve.tensor_tensor(parts[1], nm2, parts[0], ALU.subtract).then_inc(nm_ok, 1)

                    by_vector = [u for u in range(NU) if u not in POOL_UNITS]
                    for s in range(NU):
                        if s <= 3 and k >= -1 and ahead >= 1:
                            maximum(1, 4 + s)
                        if s == 1 and ahead >= 2:
                            wait(dve, tk_mm, h(1, 3))
                            dve.tensor_copy(kT[(k + 2) % 4][0:FW, :], T[0:FW, :]).then_inc(k_ok, 1)
                        if s == 3 and ahead >= 2:
                            wait(dve, tq_mm, h(1, 3))
                            dve.tensor_copy(q1T[0:FW, :], T[0:FW, :]).then_inc(q1_ok, 1)
                        if s == 4 and k >= -1 and ahead >= 1:
                            max_parts()
                        if k >= 0 and s in by_vector:
                            second_part(dve, h, k, s, p2v_ok, NVU, by_vector.index(s))
                        if s >= 6 and ahead >= 2:
                            for i in ((0, 1), (2,), (3,))[s - 6]:
                                maximum(2, i)
                    if k >= 0:
                        wait(dve, pv_mm, h(NU, LEAD + NU))
                        wait(dve, cn_ok, h(1, LEAD))
                        dve.tensor_copy(o1[:, :, :], O[:, :, 0:HD]).then_inc(rc_ok, 1)
                        wait(dve, rc_ok, h(1, 1))
                        dve.tensor_tensor(o[:, :, :], O[:, :, HD + 1:], o1[:, :, :], ALU.add)
                        dve.reciprocal(rc[:, :], O[:, :, HD]).then_inc(o_ok, 1)
                        wait(dve, o_ok, h(1, 1))
                        wait(dve, tc, n(2))
                        dve.tensor_tensor(ctok[:, :, bass.ds(g * (HG * HD) + k * HD, HD)], o[:, :, 0:HD],
                                          rc[:, :].unsqueeze(2).to_broadcast([P, ST, HD]), ALU.mult).then_inc(cn_ok, 1)

                head_steps(dve, b, step)
                wait(dve, tc, n(2, 1))
                wait(dve, qkv_mm, n(2 * NHG, 2 * NHG))
                dve.tensor_copy(xbT[:, 0, :].rearrange("p (a c) -> p a c", a=2), S[0][:, :, :]).then_inc(cTv_ok, 1)
                for s, bank in enumerate((S[2], S[0])):
                    wait(dve, wo_mm, n(2, s + 1))
                    rows = slice(s * GT, (s + 1) * GT)
                    dve.tensor_tensor(xb[:, rows, :], bank[:, :, :].rearrange("p a (t c) -> p (a t) c", t=2),
                                      xb[:, rows, :], ALU.add).then_inc(xr_ok, 1)
                    if s == 0:
                        wait(dve, xr_ok, n(2, 1))
                        layernorm(n, 2, lambda t: xb[:, t, :], lambda t: xb[:, t, :])

                def first_chunk(s):
                    wait(dve, tx, n(8, 4 + 2 * s + 1))
                    dve.tensor_copy(xbT[:, 0, s * 512:(s + 1) * 512], half_banks[s][0]).then_inc(xTv_ok, 1)

                first_chunk(0)
                wait(dve, xr_ok, n(2, 2))
                layernorm(n, 3, lambda t: xb[:, GT + t, :], lambda t: xb[:, GT + t, :])

                def hidden(w):
                    wait(dve, sl_ok, n(16, w + 1))
                    if w % 4 == 0:
                        wait(dve, hs_ok, n(4, w // 4))
                        wait(dve, ab_ok, n(16, w))
                    dve.tensor_tensor(hj[:, w % 4, :], S[w % 3][:, 1, :], sgl[:, w % 2, :], ALU.mult).then_inc(hm_ok, 1)

                def sparsify(k):
                    s = Step(n(4, k), 1, 0)
                    wait(dve, ab_ok, n(16, 4 * (k + 1)))
                    if k == 0:
                        wait(dve, fd_mm, n(4))
                    if k == 3:
                        wait(dve, fd_mm, n(4, 2))
                    wait(dve, hs_ok, s(1))
                    chain = Chain(dve, sp, s, 3)

                    def row(i, m):
                        return aj[:, i:i + 1, :].to_broadcast([P, m, 512])
                    dve.tensor_tensor(ge[:, 0:3, :], row(0, 3), aj[:, 1:4, :], ALU.is_ge)
                    dve.tensor_tensor(ge[:, 3:5, :], row(1, 2), aj[:, 2:4, :], ALU.is_ge)
                    chain.then(dve.tensor_tensor(ge[:, 5, :], aj[:, 2, :], aj[:, 3, :], ALU.is_ge))
                    dve.tensor_tensor(nb[:, 0, :], ge[:, 0, :], ge[:, 1, :], ALU.add)
                    dve.tensor_tensor(nb[:, 1, :], ge[:, 3, :], ge[:, 4, :], ALU.add)
                    dve.tensor_tensor(nb[:, 2, :], ge[:, 1, :], ge[:, 3, :], ALU.add)
                    chain.then(dve.tensor_tensor(nb[:, 3, :], ge[:, 2, :], ge[:, 4, :], ALU.add))
                    dve.tensor_tensor(nb[:, 0, :], nb[:, 0, :], ge[:, 2, :], ALU.add)
                    dve.tensor_tensor(nb[:, 1, :], nb[:, 1, :], ge[:, 0, :], ALU.subtract)
                    dve.tensor_tensor(nb[:, 2, :], nb[:, 2, :], ge[:, 5, :], ALU.subtract)
                    chain.then(dve.tensor_tensor(nb[:, 3, :], nb[:, 3, :], ge[:, 5, :], ALU.add))
                    for i, (op, bound) in enumerate(((ALU.is_ge, 2.0), (ALU.is_ge, 1.0), (ALU.is_le, 0.0), (ALU.is_le, 1.0))):
                        last = dve.scalar_tensor_tensor(hs[:, k % 3 * 4 + i, :], nb[:, i, :], bound, hj[:, i, :], op, ALU.mult)
                    last.then_inc(hs_ok, 1)
                    chain.end()

                def residual(g):
                    for s, bank in enumerate((C, M)):
                        wait(dve, fd_mm, n(4, 2 * g + s + 1))
                        rows = slice(g * GT + 2 * s, g * GT + 2 * s + 2)
                        dve.tensor_tensor(xb[:, rows, :], bank[:, :].rearrange("p (t c) -> p t c", t=2),
                                          xb[:, rows, :], ALU.add).then_inc(f2_ok, 1)

                def finish(g, k):
                    wait(dve, f2_ok, n(4, 2 * g + 2))
                    wait(dve, out_st, n(32, 16 * g))
                    layernorm(n, k, lambda t: xb[:, g * GT + t, :], lambda t: ot[:, t, :])

                for k in range(4):
                    for w in range(4 * k, 4 * k + 4):
                        if w == HALF_AT:
                            first_chunk(1)
                        hidden(w)
                        if w == DOWN_AT:
                            residual(0)
                    sparsify(k)
                finish(0, 4)
                after = Step((b + 1) % NB, 1, 0)
                for g in range(2):
                    layernorm(n, 5 + g, lambda t: x_tile(after, g * GT + t), lambda t: x_tile(after, g * GT + t))
                residual(1)
                finish(1, 7)

        @block.tensor
        def _(pe):
            pe.sem_inc(pv_mm, LEAD)
            pe.wait_ge(consts, 16 * 4)
            pe.wait_ge(setup, 3)
            pe.wait_ge(ready, 1)

            def transposes(dst, src, done):
                for t in range(ST):
                    last = pe.transpose(dst[:, t // 4, (t % 4) * P:(t % 4 + 1) * P], src(t), ident[:])
                last.then_inc(done, 1)

            def half_transposed(s):
                for f in range(KD):
                    for t in range(GT):
                        last = pe.transpose(half_banks[s][f][:, t * P:(t + 1) * P],
                                            xb[:, s * GT + t, f * P:(f + 1) * P], ident[:])
                    last.then_inc(tx, 1)

            with pe.Fori(0, NB) as b:
                n = Step(b, 1, 0)
                wait(pe, xb_ok, n(2, 1))
                wait(pe, hm_ok, n(16))
                half_transposed(0)
                wait(pe, xb_ok, n(2, 2))
                wait(pe, f2_ok, n(4))
                half_transposed(1)
                with pe.Fori(0, NHG) as g:
                    q = Step(b * NHG + g, 1, 0)
                    wait(pe, xTv_ok, n(4, 2))
                    wait(pe, xTa_ok, n(4, 2))
                    wait(pe, qkv_ok, q(2))
                    wait(pe, v2_ok, q(1))
                    for t in range(ST):
                        for k in range(KD):
                            last = pe.matmul(S[t // 4][:, t % 4 // 2, (t % 2) * 256:(t % 2) * 256 + 3 * HG * HD],
                                             xbT[:, k, t * P:(t + 1) * P],
                                             w_qkv[:, k, bass.ds(g, 1), :].rearrange("p a b -> p (a b)"),
                                             start=(k == 0), stop=(k == KD - 1))
                        if t % 4 == 3:
                            last.then_inc(qkv_mm, 1)
                wait(pe, ca_ok, n(NHG, NHG))
                wait(pe, rest_ok, n(NHG, NHG))
                wait(pe, v2_ok, n(NHG, NHG))
                wait(pe, f2_ok, n(4))

                def step(h, g, k, ahead):
                    def rows_transposed(of, s, done):
                        pe.sem_inc(passed_pe, 1)
                        for t in range(ST):
                            last = pe.transpose(T[0:FW, t * P:(t + 1) * P], rows_of(g, k + of, s, t), ident_b[:, :])
                        last.then_inc(done, 1)

                    def for_maximum(of, i):
                        if i == 0:
                            wait(pe, k_ok, h(1, of + 1))
                            wait(pe, q1_ok, h(1, of + 1))
                        wait(pe, mx_ok, h(ST, LEAD + ST * of + i - 1))
                        query = q1T[0:FW, i * P:(i + 1) * P]
                        key = kT[(k + of) % 4]
                        bank = X[i % 2]
                        for c in range(2):
                            wide = min(4, i - 4 * c) * P
                            if wide > 0:
                                last = pe.matmul(bank[:, c, 0:wide], query[0:FW - 1, :],
                                                 key[0:FW - 1, 512 * c:512 * c + wide], start=True, stop=True)
                        last = pe.matmul(bank[:, i // 4, (i % 4) * P:(i % 4 + 1) * P], query,
                                         key[0:FW, i * P:(i + 1) * P], start=True, stop=True)
                        last.then_inc(max_mm, 1)

                    def scores(of, u):
                        if u == 0:
                            wait(pe, q2_ok, h(1, of + 1))
                        wait(pe, exp_ok, h(NU, LEAD + NU * of + u - 1))
                        bank = W[((k + of) * NU + u) % 2]
                        for at, j, i, count, diagonal in runs(u):
                            rows = FW if diagonal else FW - 1
                            last = pe.matmul(bank[:, at * P:(at + count) * P], kT[(k + of) % 4][0:rows, j * P:(j + 1) * P],
                                             q2T[(k + of) % 2][0:rows, i * P:(i + count) * P], start=True, stop=True)
                        last.then_inc(sc_mm, 1)

                    def weighted(u):
                        by_pool = sum(w <= u for w in POOL_UNITS)
                        if u in POOL_UNITS:
                            wait(pe, p2p_ok, h(NPU, LEAD + by_pool))
                        else:
                            wait(pe, p2v_ok, h(NVU, LEAD + u + 1 - by_pool))
                        if u == 0:
                            wait(pe, o_ok, h(1))
                        at = (k * NU + u) % RING
                        for place, (j, i) in enumerate(BLOCKS[UB * u:UB * u + UB]):
                            for w, columns in ((p1[at], 2 * HD + 1), (p2[at], HD + 1)):
                                last = pe.matmul(O[:, i, 0:columns], w[:, place * P:(place + 1) * P],
                                                 v[:, j, bass.ds(g * HG + k, 1), 0:columns].rearrange("p a d -> p (a d)"),
                                                 start=(i == j == 0 and columns > HD + 1),
                                                 stop=(j == ST - 1 and columns == HD + 1))
                        last.then_inc(pv_mm, 1)

                    for s in range(NU):
                        if k >= 0 and s + 1 < NU:
                            scores(0, s + 1)
                        if s == NU - 1 and k >= -1 and ahead >= 1:
                            scores(1, 0)
                        if s <= 3 and k >= -1 and ahead >= 1:
                            for_maximum(1, 4 + s)
                        if s == 1 and ahead >= 2:
                            if k >= -1:
                                wait(pe, q2_ok, h(1, 1))
                            rows_transposed(2, 1, tk_mm)
                        if s == 3 and ahead >= 2:
                            wait(pe, k_ok, h(1, 3))
                            rows_transposed(2, 0, tq_mm)
                        if s == 5 and k >= -1 and ahead >= 1:
                            if ahead >= 2:
                                wait(pe, q1_ok, h(1, 3))
                            else:
                                wait(pe, q2_ok, h(1, 1))
                            wait(pe, nm_ok, h(1, 2))
                            rows_transposed(1, 0, tm_mm)
                        if s >= 6 and ahead >= 2:
                            for i in ((0, 1), (2,), (3,))[s - 6]:
                                for_maximum(2, i)
                        if k >= 0 and s > 0:
                            weighted(s - 1)
                    if k >= 0:
                        weighted(NU - 1)

                head_steps(pe, b, step)
                wait(pe, cn_ok, n(HEADS, LEAD + HEADS))
                pe.wait_ge(late, 16 * 4)
                for f in range(KD):
                    transposes(S[f], lambda t: ctok[:, t, f * P:(f + 1) * P], tc)
                wait(pe, cTv_ok, n(1, 1))
                wait(pe, cTa_ok, n(1, 1))
                for t in range(ST):
                    bank = (S[2], S[0])[t // 4]
                    for k in range(KD):
                        last = pe.matmul(bank[:, t % 4 // 2, (t % 2) * D:(t % 2 + 1) * D], xbT[:, k, t * P:(t + 1) * P],
                                         w_o[:, k, :], start=(k == 0), stop=(k == KD - 1))
                    if t % 4 == 3:
                        last.then_inc(wo_mm, 1)
                wait(pe, ln_ok, n(NLN, 2 + 1))
                half_transposed(0)
                wait(pe, xTv_ok, n(4, 3))
                wait(pe, xTa_ok, n(4, 3))

                def hidden(w):
                    g, c = divmod(w, NF)
                    if w >= 3:
                        wait(pe, hm_ok, n(16, w - 2))
                    for e, wt in enumerate((w_fg, w_fu)):
                        for k in range(KD):
                            last = pe.matmul(S[w % 3][:, e, :], wt[:, k, c * P:(c + 1) * P],
                                             xbT[:, k, g * 512:(g + 1) * 512], start=(k == 0), stop=(k == KD - 1))
                    last.then_inc(ff_mm, 1)

                def down(g):
                    wait(pe, f2_ok, n(4, 2 * g))
                    for k in range(2 * g, 2 * g + 2):
                        wait(pe, hs_ok, n(4, k + 1))
                        for t in range(GT):
                            for i in range(4):
                                last = pe.matmul((C, M)[t // 2][:, (t % 2) * D:(t % 2 + 1) * D],
                                                 hs[:, k % 3 * 4 + i, t * P:(t + 1) * P], w_fd[:, k % 2 * 4 + i, :],
                                                 start=(k % 2 == t % 2 == i == 0), stop=(k % 2 == t % 2 == 1 and i == 3))
                            if k % 2 and t % 2:
                                last.then_inc(fd_mm, 1)

                wait(pe, xr_ok, n(2, 2))
                for w in range(16):
                    if w == HALF_AT:
                        wait(pe, ln_ok, n(NLN, 2 + 2))
                        half_transposed(1)
                    if w == NF:
                        wait(pe, xTv_ok, n(4, 4))
                        wait(pe, xTa_ok, n(4, 4))
                    if w == DOWN_AT:
                        down(0)
                    hidden(w)
                down(1)


def build(nc, io):
    io["rows"] = nc.dram_tensor("rows", (TOK + P, ROW), F32, kind="Internal").ap()
    io["rows_t"] = io["rows"][0:TOK, :].rearrange("(t p) c -> p t c", p=P)
    with ExitStack() as ctx:
        kit = Kit(nc, ctx)
        keep = {"x_sb": kit.sb("x_sb", [P, NT, D]), "ident": kit.sb("ident", [P, P])}
        with ExitStack() as first:
            kit = Kit(nc, first)
            keep["xT"] = kit.sb("xT", [P, KD, TOK])
            keep["logits"] = kit.sb("logits", [P, NT, E])
            conv_mlp_phase(nc, io, keep)
            experts_phase(nc, io, keep)
        attention_ffn_phase(nc, io, keep)


def kernel(**inputs):
    import ml_dtypes
    from concourse import bacc
    from concourse.bass_utils import run_bass_kernel_spmd

    BF = ml_dtypes.bfloat16

    def chunks(a):
        return np.ascontiguousarray(a.reshape(-1, P, a.shape[-1]).transpose(1, 0, 2))

    def quads(a):
        return np.ascontiguousarray(a.reshape(2, P, 4, -1).transpose(0, 2, 1, 3).reshape(DF, -1))

    frequency = np.float32(1.0) / np.float32(10000.0) ** (np.arange(0, HD, 2, dtype=np.float32) / np.float32(HD))
    position = (np.arange(P)[:, None] + P * np.arange(ST)[None, :]).astype(np.float32)
    angle = position[:, :, None] * frequency[None, None, :]

    g = {k: np.asarray(v) for k, v in inputs.items()}
    arrays = {
        "x": np.pad(chunks(g["L0_attn_x"].reshape(TOK, D)), ((0, 0), (0, GT), (0, 0))),
        "ident": np.eye(P, dtype=np.float32),
        "w_in": chunks(g["L0_attn_W_in"].T),
        "conv_w": chunks(g["L0_attn_conv_w"].reshape(DI, TAPS)),
        "conv_b": np.ascontiguousarray(g["L0_attn_conv_b"].reshape(NCI, P).T),
        "w_out": chunks(g["L0_attn_W_out"].T),
        "w_up": chunks(g["L0_attn_W_mlp1"].T),
        "w_dn": chunks(g["L0_attn_W_mlp2"].T),
        "gate_w": chunks(g["L0_ffn_gate_w"].T),
        "we_gu": np.ascontiguousarray(g["L0_ffn_w_gate_up"].reshape(E, KD, P, -1).transpose(2, 0, 1, 3)),
        "we_dn": np.ascontiguousarray(g["L0_ffn_w_down"].reshape(E, NIX, IX, D).transpose(2, 0, 1, 3)),
        "ws_gu": chunks(np.pad(g["L0_ffn_ws_gate_up"].reshape(D, 2, SHARED),
                               ((0, 0), (0, 0), (0, NSX * P - SHARED))).reshape(D, -1)),
        "ws_dn": chunks(np.pad(g["L0_ffn_ws_down"], ((0, NSX * P - SHARED), (0, 0)))),
        "upper": np.triu(np.ones((P, P))).astype(BF),
        "ones": np.ones((P, P), BF),
        "ones_f": np.ones((P, 1), np.float32),
        "place": (np.arange(P)[:, None] // E + CG * np.arange(CJ)[None, :]).astype(np.float32),
        "mine": (np.arange(P)[:, None] % E == np.arange(E)[None, :]).astype(np.float32),
        "lane": np.tile(np.arange(P, dtype=np.float32), (P, 1)),
        "base": np.tile(P * np.arange(NT, dtype=np.float32), (P, 1)),
        "zeros": np.zeros((P, ROW), np.float32),
        "w_qkv": chunks(np.concatenate([g[f"L1_attn_w_{c}"].T.reshape(D, NHG, HG * HD) for c in "qkv"],
                                       axis=2).reshape(D, -1)).reshape(P, KD, NHG, -1),
        "w_o": chunks(g["L1_attn_w_o"].T),
        "w_fg": chunks(quads(g["L1_ffn_w_gate"].T).T),
        "w_fu": chunks(quads(g["L1_ffn_w_up"].T).T),
        "w_fd": chunks(quads(g["L1_ffn_w_down"])),
        "cos": np.ascontiguousarray(np.cos(angle).astype(np.float32)),
        "sin": np.ascontiguousarray(np.sin(angle).astype(np.float32)),
        "mask": np.stack([np.arange(P) < BLK, (np.arange(P) >= BLK) * np.float32(MASKED)], axis=1).astype(np.float32),
    }
    nc = bacc.Bacc("TRN2", target_bir_lowering=False, num_devices=1)
    io = {n: nc.dram_tensor(n, a.shape, mybir.dt.from_np(a.dtype), kind="ExternalInput").ap()
          for n, a in arrays.items()}
    io["out"] = nc.dram_tensor("out", (P, NT, D), F32, kind="ExternalOutput").ap()
    build(nc, io)
    r = run_bass_kernel_spmd(nc, [arrays], core_ids=[0])
    out = np.asarray(r.results[0]["out"])
    return out.transpose(1, 0, 2).reshape(4, 1024, D)
```
